# Optimizing a Trainium2 kernel written in Bass

```python
import numpy as np
import jax
import jax.numpy as jnp

def _softmax(x, axis=-1):
    return jax.nn.softmax(x, axis=axis)

def _gelu(x):
    return jax.nn.gelu(x, approximate=True)

def _silu(x):
    return jax.nn.silu(x)

def _sigmoid(x):
    return jax.nn.sigmoid(x)

def _layernorm(x, axis=-1, eps=1e-05):
    m = jnp.mean(x, axis=axis, keepdims=True)
    v = jnp.var(x, axis=axis, keepdims=True)
    return (x - m) / jnp.sqrt(v + eps)

def _scatter_add(tgt, idx, src, axis=0):
    return tgt.at[idx].add(src)

def _segment_sum(src, seg, n):
    return jax.ops.segment_sum(src, seg, n)
kernel_name = 'mk_recurrent_d2_jaxref_r8_fd8f37'

def setup_inputs(seed: int=0):
    np.random.seed(seed)
    _w = jnp.asarray

    def _L0_attn_setup():
        import jax, jax.numpy as jnp
        import numpy as np
        DIM = 512
        N_HEADS = 32
        N_KV_HEADS = 8
        HEAD_DIM = DIM // N_HEADS
        N_REP = N_HEADS // N_KV_HEADS
        THETA = 10000.0
        B, S = (4, 128)

        def _rope_cos_sin(seq_len):
            freqs = 1.0 / THETA ** (jnp.arange(0, HEAD_DIM, 2, dtype=jnp.float32) / HEAD_DIM)
            t = jnp.arange(seq_len, dtype=jnp.float32)
            ang = jnp.outer(t, freqs)
            return (jnp.cos(ang), jnp.sin(ang))

        def _apply_rope(x, cos, sin):
            xr = x[..., 0::2]
            xi = x[..., 1::2]
            c = cos[None, :, None, :]
            s = sin[None, :, None, :]
            out_r = xr * c - xi * s
            out_i = xr * s + xi * c
            return jnp.stack([out_r, out_i], axis=-1).reshape(x.shape)
        key = jax.random.key(seed)
        ks = jax.random.split(key, 5)
        sc = 1.0 / np.sqrt(DIM).astype(np.float32)
        x = jax.random.normal(ks[0], (B, S, DIM), jnp.float32)
        wq = jax.random.normal(ks[1], (DIM, N_HEADS * HEAD_DIM), jnp.float32) * sc
        wk = jax.random.normal(ks[2], (DIM, N_KV_HEADS * HEAD_DIM), jnp.float32) * sc
        wv = jax.random.normal(ks[3], (DIM, N_KV_HEADS * HEAD_DIM), jnp.float32) * sc
        wo = jax.random.normal(ks[4], (N_HEADS * HEAD_DIM, DIM), jnp.float32) * sc
        return {'x': x, 'wq': wq, 'wk': wk, 'wv': wv, 'wo': wo}
    _L0_attn_in = _L0_attn_setup()

    def _L0_ffn_setup():
        import jax, jax.numpy as jnp
        import numpy as np
        TOP_K = 2
        key = jax.random.key(seed)
        k0, k1, k2 = jax.random.split(key, 3)
        B, S, D, H, E = (4, 256, 512, 512, 8)
        sc = 1.0 / np.sqrt(D).astype(np.float32)
        x = jax.random.normal(k0, (B, S, D), dtype=jnp.float32)
        W_gate = jax.random.normal(k1, (D, E), dtype=jnp.float32) * sc
        b_gate = jnp.zeros((E,), dtype=jnp.float32)
        W_e = jax.random.normal(k2, (E, D, H), dtype=jnp.float32) * sc
        b_e = jnp.zeros((E, H), dtype=jnp.float32)
        return {'x': x, 'W_gate': W_gate, 'b_gate': b_gate, 'W_e': W_e, 'b_e': b_e}
    _L0_ffn_in = _L0_ffn_setup()

    def _L1_attn_setup():
        import jax, jax.numpy as jnp
        import numpy as np
        N_STATE = 64
        SEQ_L = 512
        BATCH, HCH = (16, 64)
        DT_MIN, DT_MAX = (0.001, 0.1)

        def _make_DPLR_HiPPO(N):
            P = np.sqrt(1 + 2 * np.arange(N))
            A = P[:, None] * P[None, :]
            A = np.tril(A) - np.diag(np.arange(N))
            nhippo = -A
            p = 0.5 * np.sqrt(2 * np.arange(1, N + 1) + 1.0)
            q = 2 * p
            S = nhippo + p[:, None] * q[None, :]
            Lambda, V = np.linalg.eig(S)
            Vc = V.conj().T
            p_t = Vc @ p
            q_t = Vc @ q.conj()
            return (Lambda, p_t, q_t, Vc)

        def _ri(z):
            return np.stack([z.real, z.imag], axis=-1).astype(np.float32)

        def _cplx(x_ri):
            return x_ri[..., 0] + 1j * x_ri[..., 1]

        def _s4_kernel(Lambda, p, q, B, Ct, step, L):
            Omega = jnp.exp(-2j * jnp.pi * (jnp.arange(L) / L))
            g = 2.0 / step * ((1.0 - Omega) / (1.0 + Omega))
            c = 2.0 / (1.0 + Omega)
            denom = g[:, None] - Lambda[None, :]
            cauchy = lambda v: (v[None, :] / denom).sum(-1)
            k00 = cauchy(Ct.conj() * B)
            k01 = cauchy(Ct.conj() * p)
            k10 = cauchy(q.conj() * B)
            k11 = cauchy(q.conj() * p)
            at_roots = c * (k00 - k01 * (1.0 / (1.0 + k11)) * k10)
            return jnp.fft.ifft(at_roots, L).real
        key = jax.random.key(seed)
        k_u, k_ct, k_b, k_d, k_ls = jax.random.split(key, 5)
        Lambda, p, q, Vc = _make_DPLR_HiPPO(N_STATE)
        u = jax.random.normal(k_u, (BATCH, HCH, SEQ_L), dtype=jnp.float32)
        Ct_ri = jax.random.normal(k_ct, (1, N_STATE, 2), dtype=jnp.float32) / np.sqrt(N_STATE)
        Bp = jax.random.normal(k_b, (N_STATE, 1), dtype=jnp.float32) / np.sqrt(N_STATE)
        D = jax.random.uniform(k_d, (1,), dtype=jnp.float32)
        log_step = jax.random.uniform(k_ls, (1,), dtype=jnp.float32, minval=np.log(DT_MIN), maxval=np.log(DT_MAX))
        return {'u': u, 'Lambda_ri': jnp.asarray(_ri(Lambda)), 'p_ri': jnp.asarray(_ri(p)), 'q_ri': jnp.asarray(_ri(q)), 'Vc_ri': jnp.asarray(_ri(Vc)), 'Ct_ri': Ct_ri, 'Bp': Bp, 'D': D, 'log_step': log_step}
    _L1_attn_in = _L1_attn_setup()

    def _L1_ffn_setup():
        import jax, jax.numpy as jnp
        import numpy as np
        BLOCK = 128

        def _dequant(weight, scale_inv):
            O, I = weight.shape
            w = weight.reshape(O // BLOCK, BLOCK, I // BLOCK, BLOCK)
            w = w * scale_inv[:, None, :, None]
            return w.reshape(O, I)
        key = jax.random.key(seed)
        k_x, k_w, k_s, k_b = jax.random.split(key, 4)
        B, S, IN, OUT = (2, 256, 512, 512)
        x = jax.random.normal(k_x, (B, S, IN), dtype=jnp.float32)
        w = jax.random.normal(k_w, (OUT, IN), dtype=jnp.float32) * 0.02
        weight = w.astype(jnp.float8_e4m3fn).astype(jnp.float32)
        weight_scale_inv = jax.random.uniform(k_s, (OUT // BLOCK, IN // BLOCK), dtype=jnp.float32, minval=0.5, maxval=1.5)
        bias = jax.random.normal(k_b, (OUT,), dtype=jnp.float32) * 0.01
        return {'x': x, 'weight': weight, 'weight_scale_inv': weight_scale_inv, 'bias': bias}
    _L1_ffn_in = _L1_ffn_setup()
    _d = {'L0_attn_x': _L0_attn_in['x'], 'L0_attn_wq': _L0_attn_in['wq'], 'L0_attn_wk': _L0_attn_in['wk'], 'L0_attn_wv': _L0_attn_in['wv'], 'L0_attn_wo': _L0_attn_in['wo'], 'L0_ffn_W_gate': _L0_ffn_in['W_gate'], 'L0_ffn_b_gate': _L0_ffn_in['b_gate'], 'L0_ffn_W_e': _L0_ffn_in['W_e'], 'L0_ffn_b_e': _L0_ffn_in['b_e'], 'L1_attn_Lambda_ri': _L1_attn_in['Lambda_ri'], 'L1_attn_p_ri': _L1_attn_in['p_ri'], 'L1_attn_q_ri': _L1_attn_in['q_ri'], 'L1_attn_Vc_ri': _L1_attn_in['Vc_ri'], 'L1_attn_Ct_ri': _L1_attn_in['Ct_ri'], 'L1_attn_Bp': _L1_attn_in['Bp'], 'L1_attn_D': _L1_attn_in['D'], 'L1_attn_log_step': _L1_attn_in['log_step'], 'L1_ffn_weight': _L1_ffn_in['weight'], 'L1_ffn_weight_scale_inv': _L1_ffn_in['weight_scale_inv'], 'L1_ffn_bias': _L1_ffn_in['bias']}
    _x0 = _d['L0_attn_x']
    _d['L0_attn_x'] = jax.random.normal(jax.random.fold_in(jax.random.key(seed), 1), (4, 512, 512), dtype=_x0.dtype)
    del _x0
    return _d

def reference(L0_attn_x, L0_attn_wq, L0_attn_wk, L0_attn_wv, L0_attn_wo, L0_ffn_W_gate, L0_ffn_b_gate, L0_ffn_W_e, L0_ffn_b_e, L1_attn_Lambda_ri, L1_attn_p_ri, L1_attn_q_ri, L1_attn_Vc_ri, L1_attn_Ct_ri, L1_attn_Bp, L1_attn_D, L1_attn_log_step, L1_ffn_weight, L1_ffn_weight_scale_inv, L1_ffn_bias):

    def _L0_attn_ref(x, wq, wk, wv, wo):
        import jax, jax.numpy as jnp
        import numpy as np
        DIM = 512
        N_HEADS = 32
        N_KV_HEADS = 8
        HEAD_DIM = DIM // N_HEADS
        N_REP = N_HEADS // N_KV_HEADS
        THETA = 10000.0
        B, S = (4, 128)

        def _rope_cos_sin(seq_len):
            freqs = 1.0 / THETA ** (jnp.arange(0, HEAD_DIM, 2, dtype=jnp.float32) / HEAD_DIM)
            t = jnp.arange(seq_len, dtype=jnp.float32)
            ang = jnp.outer(t, freqs)
            return (jnp.cos(ang), jnp.sin(ang))

        def _apply_rope(x, cos, sin):
            xr = x[..., 0::2]
            xi = x[..., 1::2]
            c = cos[None, :, None, :]
            s = sin[None, :, None, :]
            out_r = xr * c - xi * s
            out_i = xr * s + xi * c
            return jnp.stack([out_r, out_i], axis=-1).reshape(x.shape)
        bsz, seq_len, _ = x.shape
        q = (x @ wq).reshape(bsz, seq_len, N_HEADS, HEAD_DIM)
        k = (x @ wk).reshape(bsz, seq_len, N_KV_HEADS, HEAD_DIM)
        v = (x @ wv).reshape(bsz, seq_len, N_KV_HEADS, HEAD_DIM)
        cos, sin = _rope_cos_sin(seq_len)
        q = _apply_rope(q, cos, sin)
        k = _apply_rope(k, cos, sin)
        k = jnp.repeat(k, N_REP, axis=2)
        v = jnp.repeat(v, N_REP, axis=2)
        scores = jnp.einsum('bqhd,bkhd->bhqk', q, k) / np.float32(np.sqrt(HEAD_DIM))
        mask = jnp.triu(jnp.full((seq_len, seq_len), -jnp.inf, dtype=scores.dtype), k=1)
        scores = scores + mask
        attn = jax.nn.softmax(scores.astype(jnp.float32), axis=-1).astype(q.dtype)
        out = jnp.einsum('bhqk,bkhd->bqhd', attn, v).reshape(bsz, seq_len, N_HEADS * HEAD_DIM)
        return out @ wo

    def _L0_ffn_ref(x, W_gate, b_gate, W_e, b_e):
        import jax, jax.numpy as jnp
        import numpy as np
        TOP_K = 2
        logits = x @ W_gate + b_gate
        _, top_idx = jax.lax.top_k(logits, TOP_K)
        y_all = jax.nn.relu(jnp.einsum('bsd,edh->bseh', x, W_e) + b_e)
        y = jnp.take_along_axis(y_all, top_idx[..., None], axis=2)
        return y.mean(axis=2)

    def _L1_attn_ref(u, Lambda_ri, p_ri, q_ri, Vc_ri, Ct_ri, Bp, D, log_step):
        import jax, jax.numpy as jnp
        import numpy as np
        N_STATE = 64
        SEQ_L = 512
        BATCH, HCH = (16, 64)
        DT_MIN, DT_MAX = (0.001, 0.1)

        def _make_DPLR_HiPPO(N):
            P = np.sqrt(1 + 2 * np.arange(N))
            A = P[:, None] * P[None, :]
            A = np.tril(A) - np.diag(np.arange(N))
            nhippo = -A
            p = 0.5 * np.sqrt(2 * np.arange(1, N + 1) + 1.0)
            q = 2 * p
            S = nhippo + p[:, None] * q[None, :]
            Lambda, V = np.linalg.eig(S)
            Vc = V.conj().T
            p_t = Vc @ p
            q_t = Vc @ q.conj()
            return (Lambda, p_t, q_t, Vc)

        def _ri(z):
            return np.stack([z.real, z.imag], axis=-1).astype(np.float32)

        def _cplx(x_ri):
            return x_ri[..., 0] + 1j * x_ri[..., 1]

        def _s4_kernel(Lambda, p, q, B, Ct, step, L):
            Omega = jnp.exp(-2j * jnp.pi * (jnp.arange(L) / L))
            g = 2.0 / step * ((1.0 - Omega) / (1.0 + Omega))
            c = 2.0 / (1.0 + Omega)
            denom = g[:, None] - Lambda[None, :]
            cauchy = lambda v: (v[None, :] / denom).sum(-1)
            k00 = cauchy(Ct.conj() * B)
            k01 = cauchy(Ct.conj() * p)
            k10 = cauchy(q.conj() * B)
            k11 = cauchy(q.conj() * p)
            at_roots = c * (k00 - k01 * (1.0 / (1.0 + k11)) * k10)
            return jnp.fft.ifft(at_roots, L).real
        L = u.shape[-1]
        Lambda = _cplx(Lambda_ri)
        p = _cplx(p_ri)
        q = _cplx(q_ri)
        Vc = _cplx(Vc_ri)
        Ct = _cplx(Ct_ri).reshape(-1)
        B = (Vc @ Bp.astype(Vc.dtype)).reshape(-1)
        step = jnp.exp(log_step)[0]
        K = _s4_kernel(Lambda, p, q, B, Ct, step, L).astype(u.dtype)
        n = 2 * L
        y = jnp.fft.irfft(jnp.fft.rfft(u, n=n) * jnp.fft.rfft(K, n=n), n=n)[..., :L]
        return y + D[0] * u

    def _L1_ffn_ref(x, weight, weight_scale_inv, bias):
        import jax, jax.numpy as jnp
        import numpy as np
        BLOCK = 128

        def _dequant(weight, scale_inv):
            O, I = weight.shape
            w = weight.reshape(O // BLOCK, BLOCK, I // BLOCK, BLOCK)
            w = w * scale_inv[:, None, :, None]
            return w.reshape(O, I)
        w_deq = _dequant(weight, weight_scale_inv)
        out = jnp.einsum('bsi,oi->bso', x, w_deq)
        return out + bias
    x = L0_attn_x
    xn = _layernorm(x, axis=-1)
    s = _L0_attn_ref(xn, L0_attn_wq, L0_attn_wk, L0_attn_wv, L0_attn_wo)
    g = _silu(_L0_ffn_ref(xn, L0_ffn_W_gate, L0_ffn_b_gate, L0_ffn_W_e, L0_ffn_b_e))
    x = x + s * g
    xn = _layernorm(x, axis=-1)
    s = _L1_attn_ref(xn, L1_attn_Lambda_ri, L1_attn_p_ri, L1_attn_q_ri, L1_attn_Vc_ri, L1_attn_Ct_ri, L1_attn_Bp, L1_attn_D, L1_attn_log_step)
    g = _silu(_L1_ffn_ref(xn, L1_ffn_weight, L1_ffn_weight_scale_inv, L1_ffn_bias))
    x = x + s * g
    return x

_drawn_inputs = setup_inputs


def setup_inputs(seed=0):
    import zlib

    import numpy as np

    out = dict(_drawn_inputs(seed))
    spreads = {'L0_ffn_b_gate': (0.0, 0.605), 'L0_ffn_b_e': (0.0, 0.8)}
    factors = {'L1_attn_Lambda_ri': 8.0,
     'L1_attn_p_ri': 8.0,
     'L1_attn_q_ri': 8.0,
     'L1_attn_Vc_ri': 8.0,
     'L1_attn_Ct_ri': 8.0,
     'L1_attn_Bp': 8.0,
     'L1_ffn_bias': 8.0}
    for name, (base, spread) in spreads.items():
        noise = np.random.default_rng([zlib.crc32(name.encode()), seed]).standard_normal(out[name].shape)
        drawn = base * np.exp(spread * noise) if base else spread * noise
        out[name] = jnp.asarray(drawn.astype(out[name].dtype))
    for name, factor in factors.items():
        out[name] = (out[name] * factor).astype(out[name].dtype)
    return out
```

```python
from contextlib import ExitStack

import numpy as np

import concourse.bass as bass
from concourse import mybir
from concourse.alu_op_type import AluOpType as ALU

ACT = mybir.ActivationFunctionType
AX = mybir.AxisListType
F32 = mybir.dt.float32
BF16 = mybir.dt.bfloat16
U32 = mybir.dt.uint32
I32 = mybir.dt.int32

P = 128
NB, S, D = 4, 512, 512
KB = D // P
TPB = S // P
NT = NB * TPB
H, HD, KV = 32, 16, 8
R = H // KV
E, TOPK = 8, 2
NS = 64
MT = NT * TOPK + E
MPB = MT // NB
EPS = 1e-5
NEG = -1.0e30
VW = 32
KVG = 2 * KV * HD + E
JW = [S - P * j for j in range(TPB)]
JO = [R * sum(JW[:j]) for j in range(TPB)]

COLS = {}
_at = 0
for _name, _n in (("ident", P), ("mask", P), ("tri", P), ("cos", TPB * 8), ("sin", TPB * 8), ("s4", 16),
                  ("lower", E * E), ("i128", NT), ("tile", MT), ("token", NT), ("half", 1), ("eps", 1), ("sel", E)):
    COLS[_name] = (_at, _at + _n)
    _at += _n
NCONST = _at


def constants():
    c = np.zeros((P, NCONST), np.float32)

    def put(name, a):
        c[:, COLS[name][0]:COLS[name][1]] = np.asarray(a, np.float32).reshape(-1, COLS[name][1] - COLS[name][0])

    p = np.arange(P)
    put("ident", np.eye(P))
    put("mask", np.where(p[None, :] > p[:, None], NEG, 0.0))
    put("tri", p[:, None] < p[None, :])
    freq = (np.float32(1.0) / np.float32(10000.0) ** (np.arange(0, HD, 2, dtype=np.float32) / np.float32(HD))).astype(np.float32)
    angle = (np.arange(S, dtype=np.float32)[:, None] * freq[None, :]).astype(np.float32).astype(np.float64)
    put("cos", np.cos(angle).reshape(TPB, P, 8).transpose(1, 0, 2).reshape(P, -1))
    put("sin", np.sin(angle).reshape(TPB, P, 8).transpose(1, 0, 2).reshape(P, -1))
    theta = 2 * np.pi * np.arange(D) / D
    s4 = np.stack([1 - np.cos(theta), np.sin(theta), (1 + np.cos(theta)) / 2, -np.sin(theta) / 2])
    put("s4", s4.reshape(4, KB, P).transpose(2, 0, 1).reshape(P, -1))
    put("lower", (np.arange(E)[None, :] < np.arange(E)[:, None]).reshape(1, -1))
    put("i128", P * np.arange(NT)[None, :])
    put("tile", np.arange(MT)[None, :])
    put("token", p[:, None] + P * np.arange(NT)[None, :])
    put("half", -0.5)
    put("eps", EPS)
    put("sel", np.arange(E)[None, :] == p[:, None] % 32)
    ang = 2 * np.pi * ((np.arange(D)[:, None] * np.arange(D)[None, :]) % D) / D
    dft = np.stack([np.cos(ang), -np.sin(ang)]) / D
    return c, dft.astype(np.float32)


def due(n):
    return not isinstance(n, int) or n > 0


def nth(b, u):
    return b * (TPB // 2) + u // 2 + 1


def alone(e):
    e.nop(nofuse=True)


class Steps:

    def __init__(self):
        self.base, self.k, self.loop, self.per, self.start = 0, 0, None, 0, 0

    def one(self):
        self.k += 1
        return 1

    def count(self):
        n = self.base + self.k
        assert n > 0
        return n if self.loop is None else (self.loop - self.start) * self.per + n

    def enter(self, loop, per, start=1):
        self.close()
        self.loop, self.per, self.start = loop, per, start

    def leave(self, start, end):
        assert self.k == self.per, (self.k, self.per)
        self.base += self.per * (end - start)
        self.loop, self.k = None, 0

    def close(self):
        self.base += self.k
        self.k = 0


def build(nc, x_d, wq_d, wk_d, wv_d, wo_d, wg_d, bg_d, we_d, be_d, lam_d, p_d, q_d, vct_d, ct_d, bp_d, dd_d,
          step_d, wft_d, sc_d, bf_d, const_d, dft_d, out_d):
    ctx = ExitStack()
    with ctx:
        def sb(name, shape, dt=F32):
            return ctx.enter_context(nc.sbuf_tensor(name, shape, dt))

        def ps(name, shape, dt=F32):
            return ctx.enter_context(nc.psum_tensor(name, shape, dt))

        def sem(name):
            return ctx.enter_context(nc.semaphore(name))

        def sems(name, n):
            return [sem(f"{name}{i}") for i in range(n)]

        xn_d = nc.dram_tensor("xn_rows", [NT * P, D], F32).ap()
        slot_d = nc.dram_tensor("token_of_slot", [MT * P, 1], U32).ap()
        y_d = nc.dram_tensor("expert_rows", [MT * P, D], F32).ap()
        kpad_d = nc.dram_tensor("s4_taps_rows", [P, P + D], F32).ap()

        x_t = x_d.rearrange("b (t p) d -> (b t) p d", p=P)
        out_t = out_d.rearrange("b (t p) d -> (b t) p d", p=P)
        xn_t = xn_d.rearrange("(n p) d -> n p d", p=P)
        y_t = y_d.rearrange("(n p) d -> n p d", p=P)

        cst = sb("cst", [P, NCONST])

        def const(name):
            return cst[:, COLS[name][0]:COLS[name][1]]

        ident = const("ident")
        ident_b = sb("ident_b", [P, P], BF16)
        mask_b = sb("mask_b", [P, P], BF16)
        tri_b = sb("tri_b", [P, P], BF16)
        ones_b = sb("ones_b", [P, P], BF16)
        w_e = sb("w_e", [P, E, KB, D])
        w_proj = sb("w_proj", [P, KB * (D + KVG)])
        wq = w_proj[:, 0:KB * D].rearrange("p (k n) -> p k n", k=KB)
        wkvg = w_proj[:, KB * D:].rearrange("p (k n) -> p k n", k=KB)
        wo = wq
        q_tok = sb("q_tok", [P, NB, TPB, D])
        s_tok = q_tok
        k_tok = sb("k_tok", [P, NB, TPB, KV * HD])
        v_tok = sb("v_tok", [P, NB, TPB, KV * HD])
        toep = sb("toep", [P, D])
        slots = sb("slots", [P, TOPK, NT], U32)
        slots_i = sb("slots_i", [P, MT], U32)
        eid_i = sb("eid_i", [1, MT], I32)
        be3 = sb("be3", [P, D], BF16)
        sel_e = sb("sel_e", [P, E, P], BF16)
        zero = sb("zero", [P, MT], U32)
        tok_i = sb("tok_i", [P, NT], U32)
        NAR = 18400
        arena = sb("arena", [P, NAR])
        used = [0]

        def take(shape, dt=F32, restart=None):
            if restart is not None:
                used[0] = restart
            n = int(np.prod(shape[1:]))
            words = n if dt in (F32, U32, I32) else (n + 1) // 2
            a = arena[:, used[0]:used[0] + words]
            used[0] += words
            assert used[0] <= NAR, used[0]
            if dt != F32:
                a = a.bitcast(dt)
            names = "abcdef"[:len(shape) - 1]
            if len(shape) > 2:
                a = a.rearrange(f"p ({' '.join(names)}) -> p {' '.join(names)}",
                                **{m: k for m, k in zip(names, shape[1:])})
            return a

        bank = [ps(f"bank{i}", [P, D]) for i in range(8)]

        a_load = sem("a_load")
        a_w = sem("a_w")
        a_x = sems("a_x", TPB)
        a_stat = sems("a_stat", 2)
        a_rstd = sems("a_rstd", 2)
        a_xn = sems("a_xn", 2)
        a_store = sems("a_store", TPB)
        a_tr = sems("a_tr", 2)
        a_xt = sems("a_xt", 2)
        a_q = sems("a_q", 2)
        a_kvg = sems("a_kvg", 2)
        a_rope = sems("a_rope", 2)
        a_add = sems("a_add", 2)
        dve_steps, pool_steps = sem("dve_steps"), sem("pool_steps")

        xin = take([P, TPB, D], restart=0)
        xn = take([P, 2, D])
        xt = take([P, 2, KB, P])
        rt = take([P, 2, 2, D + KV * HD])
        stats = take([P, TPB, 8])
        mv = take([P, TPB, 2])
        rstd = take([P, TPB, 1])
        bgb = take([P, E])
        logit = take([P, NT, E])
        be_f = take([P, D])
        e_load = sem("e_load")
        be_load = sem("be_load")
        ps_t, ps_q, ps_kvg = bank[0:2], bank[2:4], bank[4:6]

        lam_b = take([P, NS, 2])
        left_b = take([P, 2, NS, 2])
        right_b = take([P, 2, NS, 2])
        vct = take([P, NS, 2])
        bp_c = take([P, 1])
        bp_w = take([P, P])
        log_step = take([P, 1])
        inv_step = take([P, 1])
        d_c = take([P, 1])
        dft = take([P, 2, KB, D])
        num = take([P, 2, 2, 2, NS])
        num_t = take([P, 2, 2, NS])
        den_r, den_i, den_a, den_b = (take([P, KB, NS]) for _ in range(4))
        big = [take([P, KB, 4, NS]) for _ in range(3)]
        sums = take([P, 2, KB, 4])
        hx = take([P, 6, KB, 2])
        w_r, w_i, sq = (take([P, KB]) for _ in range(3))
        roots = take([P, 2, KB])
        taps = take([P, P + D])
        s4_load = sem("s4_load")
        s4_b = sem("s4_b")
        s4_bw = sem("s4_bw")
        s4_step = sem("s4_step")
        s4_roots = sem("s4_roots")
        s4_taps = sem("s4_taps")
        s4_row = sem("s4_row")
        s4_out = sem("s4_out")
        s4_toep = sem("s4_toep")
        slot_zero = sem("slot_zero")

        rank = take([P, NT, E], restart=0)
        first, second, tot, scan_a, scan_b, pos = (take([P, NT, E]) for _ in range(6))
        chosen_b = take([P, NT, E], BF16)
        tiles_of, end_a, end_b = (take([P, E]) for _ in range(3))
        slot_f = take([P, NT])
        eid_f = take([P, MT])
        r_chosen = sem("r_chosen")
        r_count = sem("r_count")
        r_slots = sem("r_slots")
        r_eid = sem("r_eid")
        r_scatter = sem("r_scatter")
        r_load = sem("r_load")

        block = ctx.enter_context(nc.Block())

        def sp_a(e):
            e.dma_start(cst[:, :], const_d).then_inc(a_load, 16)
            e.dma_start(bgb, bg_d.partition_broadcast(P)).then_inc(a_load, 16)
            e.dma_start(wq, wq_d.rearrange("(k p) n -> p k n", p=P)).then_inc(a_w, 16)
            e.dma_start(wkvg[:, :, 0:KV * HD], wk_d.rearrange("(k p) n -> p k n", p=P)).then_inc(a_w, 16)
            e.dma_start(wkvg[:, :, KV * HD:2 * KV * HD], wv_d.rearrange("(k p) n -> p k n", p=P)).then_inc(a_w, 16)
            e.dma_start(wkvg[:, :, 2 * KV * HD:], wg_d.rearrange("(k p) n -> p k n", p=P)).then_inc(a_w, 16)
            for u in range(TPB):
                e.dma_start(xin[:, u, :], x_t[u]).then_inc(a_x[u], 16)
            for part in range(3):
                e.dma_start(be_f[32 * part:32 * part + E, :], be_d).then_inc(be_load, 16)

            def store_and_load(b, more):
                for u in range(TPB):
                    e.wait_ge(a_xn[u % 2], nth(b, u))
                    e.dma_start(xn_t[b * TPB + u], xn[:, u % 2, :]).then_inc(a_store[u], 16)
                    if more:
                        e.dma_start(xin[:, u, :], x_t[(b + 1) * TPB + u]).then_inc(a_x[u], 16)

            store_and_load(0, True)
            with e.Fori(1, NB - 1) as b:
                store_and_load(b, True)
            store_and_load(NB - 1, False)

        def dve_a(e, st):
            v = nc.vector
            e.wait_ge(a_load, 32)
            v.tensor_copy(ident_b[:, :], ident).then_inc(dve_steps, st.one())
            v.tensor_copy(mask_b[:, :], const("mask")).then_inc(dve_steps, st.one())
            v.tensor_copy(tri_b[:, :], const("tri")).then_inc(dve_steps, st.one())
            v.memset(ones_b[:, :], 1.0).then_inc(dve_steps, st.one())
            v.tensor_copy(sel_e[:, :, :], const("sel").unsqueeze(2).to_broadcast([P, E, P])).then_inc(dve_steps, st.one())
            v.memset(be3[:, :], 0.0).then_inc(dve_steps, st.one())
            e.wait_ge(be_load, 48)
            e.wait_ge(dve_steps, st.count())
            for part in range(3):
                rows = slice(32 * part, 32 * part + E)
                for cut in range(part + 1):
                    v.tensor_copy(be3[rows, :], be_f[rows, :]).then_inc(dve_steps, st.one())
                    e.wait_ge(dve_steps, st.count())
                    if cut < part:
                        v.tensor_tensor(be_f[rows, :], be_f[rows, :], be3[rows, :], ALU.subtract).then_inc(dve_steps, st.one())
                        e.wait_ge(dve_steps, st.count())
            v.tensor_copy(tok_i[:, :], const("token")).then_inc(dve_steps, st.one())
            st.close()

            def stat(b, u):
                e.wait_ge(a_x[u], b * 16 + 16)
                v.bn_stats(stats[:, u, 0:6], xin[:, u, :]).then_inc(dve_steps, st.one())
                e.wait_ge(dve_steps, st.count())
                alone(e)
                v.bn_aggr(mv[:, u, :], stats[:, u, 0:6]).then_inc(a_stat[u % 2], 1)

            def normalise(b, u):
                e.wait_ge(a_stat[u % 2], nth(b, u))
                e.wait_ge(a_rstd[u % 2], nth(b, u))
                if due(at := nth(b, u) - 1):
                    e.wait_ge(a_tr[u % 2], at)
                if u >= 2:
                    e.wait_ge(a_store[u - 2], b * 16 + 16)
                else:
                    if due(at := b * 16):
                        e.wait_ge(a_store[u + 2], at)
                v.tensor_scalar(xn[:, u % 2, :], xin[:, u, :], mv[:, u, 0:1], rstd[:, u, :],
                                ALU.subtract, ALU.mult).then_inc(a_xn[u % 2], 1)

            def rope(b, u):
                if due(at := 4 * (nth(b, u) - 1)):
                    e.wait_ge(a_add[u % 2], at)
                for name, w, off, heads, src in (("q", D, 0, H, ps_q), ("k", KV * HD, D, KV, ps_kvg)):
                    e.wait_ge((a_q if name == "q" else a_kvg)[u % 2], nth(b, u))
                    x4 = src[u % 2][:, 0:w].rearrange("p (h d c) -> p h c d", h=heads, c=2)
                    for i, table in enumerate(("cos", "sin")):
                        o4 = rt[:, u % 2, i, off:off + w].rearrange("p (h c d) -> p h c d", h=heads, c=2)
                        tab = const(table)[:, u * 8:u * 8 + 8].unsqueeze(1).unsqueeze(1)
                        v.tensor_tensor(o4, x4, tab.to_broadcast([P, heads, 2, 8]), ALU.mult).then_inc(dve_steps, st.one())
                v.tensor_copy(v_tok[:, b, u, :], ps_kvg[u % 2][:, KV * HD:2 * KV * HD]).then_inc(dve_steps, st.one())
                e.wait_ge(dve_steps, st.count())
                v.tensor_tensor(logit[:, b * TPB + u, :], ps_kvg[u % 2][:, 2 * KV * HD:KVG], bgb, ALU.add)\
                    .then_inc(a_rope[u % 2], 1)

            def ahead(b, u, more, *stages):
                if u + 2 < TPB or more:
                    for stage in stages:
                        stage(b + (u + 2) // TPB, (u + 2) % TPB)

            def sequence(b, more):
                for u in range(TPB):
                    ahead(b, u, more, stat, normalise)
                    rope(b, u)

            for u in range(2):
                stat(0, u)
                normalise(0, u)
            st.close()
            sequence(0, True)
            st.close()
            with e.Fori(1, NB - 1) as b:
                st.enter(b, TPB * (1 + 4 + 1))
                sequence(b, True)
            st.leave(1, NB - 1)
            sequence(NB - 1, False)
            st.close()

        def act_s4_loads(e):
            for dst, src in ((lam_b, lam_d), (left_b[:, 0], ct_d.rearrange("o n c -> (o n) c")), (left_b[:, 1], q_d), (right_b[:, 1], p_d)):
                e.dma_start(dst, src.partition_broadcast(P)).then_inc(s4_load, 16)
            e.dma_start(vct[0:NS], vct_d).then_inc(s4_load, 16)
            e.dma_start(bp_c[0:NS], bp_d).then_inc(s4_load, 16)
            e.dma_start(log_step, step_d.partition_broadcast(P)).then_inc(s4_load, 16)
            e.dma_start(d_c, dd_d.partition_broadcast(P)).then_inc(s4_load, 16)
            e.dma_start(dft, dft_d.rearrange("c (k p) n -> p c k n", p=P)).then_inc(s4_load, 16)

        def dve_s4(e, st):
            v = nc.vector

            def tt(out, a, b, op):
                v.tensor_tensor(out, a, b, op).then_inc(dve_steps, st.one())
                e.wait_ge(dve_steps, st.count())

            e.wait_ge(a_load, 32)
            e.wait_ge(s4_load, 144)
            v.tensor_scalar(bp_w[0:NS, :], ident[0:NS, :], 0.0, bp_c[0:NS, :], ALU.mult, ALU.add).then_inc(s4_bw, 1)
            e.wait_ge(s4_b, 1)
            v.tensor_copy(right_b[:, 0], bank[6][:, 0:2 * NS].rearrange("p (n c) -> p n c", c=2)).then_inc(dve_steps, st.one())
            e.wait_ge(dve_steps, st.count())
            shape = [P, 2, 2, NS]
            lr, li = (left_b[:, :, :, c].unsqueeze(2).to_broadcast(shape) for c in (0, 1))
            rr, ri = (right_b[:, :, :, c].unsqueeze(1).to_broadcast(shape) for c in (0, 1))
            tt(num[:, 0], lr, rr, ALU.mult)
            tt(num_t, li, ri, ALU.mult)
            tt(num[:, 0], num[:, 0], num_t, ALU.add)
            tt(num[:, 1], lr, ri, ALU.mult)
            tt(num_t, li, rr, ALU.mult)
            tt(num[:, 1], num[:, 1], num_t, ALU.subtract)
            tab = const("s4").rearrange("p (c k) -> p c k", c=4)
            shape = [P, KB, NS]
            lam_r, lam_i = (lam_b[:, :, c].unsqueeze(1).to_broadcast(shape) for c in (0, 1))
            h_r, h_i = (tab[:, c].unsqueeze(2).to_broadcast(shape) for c in (2, 3))
            e.wait_ge(s4_step, 1)
            v.tensor_scalar(sq, tab[:, 0], inv_step, None, ALU.mult).then_inc(dve_steps, st.one())
            e.wait_ge(dve_steps, st.count())
            v.tensor_scalar(w_r, tab[:, 1], inv_step, None, ALU.mult).then_inc(dve_steps, st.one())
            e.wait_ge(dve_steps, st.count())
            for den, top, x, y, op in ((den_r, sq, h_r, h_i, ALU.add), (den_i, w_r, h_i, h_r, ALU.subtract)):
                tt(den, lam_r, x, ALU.mult)
                tt(den_a, lam_i, y, ALU.mult)
                tt(den, top.unsqueeze(2).to_broadcast(shape), den, ALU.subtract)
                tt(den, den, den_a, op)
            tt(den_a, den_r, den_r, ALU.mult)
            tt(den_b, den_i, den_i, ALU.mult)
            tt(den_a, den_a, den_b, ALU.add)
            v.reciprocal(den_a, den_a).then_inc(dve_steps, st.one())
            e.wait_ge(dve_steps, st.count())
            tt(den_r, den_r, den_a, ALU.mult)
            tt(den_i, den_i, den_a, ALU.mult)
            shape = [P, KB, 4, NS]
            n_r, n_i = (num[:, c].rearrange("p l r n -> p (l r) n").unsqueeze(1).to_broadcast(shape) for c in (0, 1))
            d_r, d_i = (d.unsqueeze(2).to_broadcast(shape) for d in (den_r, den_i))
            for c, x, y, op in ((0, n_r, n_i, ALU.add), (1, n_i, n_r, ALU.subtract)):
                tt(big[0], x, d_r, ALU.mult)
                tt(big[1], y, d_i, ALU.mult)
                tt(big[2], big[0], big[1], op)
                v.tensor_reduce(sums[:, c], big[2], AX.X, ALU.add).then_inc(dve_steps, st.one())
                e.wait_ge(dve_steps, st.count())
            shape = [P, KB, 2]
            h_r, h_i = (tab[:, c].unsqueeze(2).to_broadcast(shape) for c in (2, 3))
            s_r, s_i = sums[:, 0, :, 2:4], sums[:, 1, :, 2:4]
            tt(hx[:, 0], h_r, s_r, ALU.mult)
            tt(hx[:, 1], h_i, s_i, ALU.mult)
            tt(hx[:, 0], hx[:, 0], hx[:, 1], ALU.subtract)
            tt(hx[:, 1], h_r, s_i, ALU.mult)
            tt(hx[:, 2], h_i, s_r, ALU.mult)
            tt(hx[:, 1], hx[:, 1], hx[:, 2], ALU.add)
            y_r, y_i, x_r, x_i = hx[:, 0, :, 0], hx[:, 1, :, 0], hx[:, 0, :, 1], hx[:, 1, :, 1]
            v.tensor_scalar(x_r, x_r, 1.0, None, ALU.add).then_inc(dve_steps, st.one())
            e.wait_ge(dve_steps, st.count())
            tt(sq, x_r, x_r, ALU.mult)
            tt(w_r, x_i, x_i, ALU.mult)
            tt(sq, sq, w_r, ALU.add)
            v.reciprocal(sq, sq).then_inc(dve_steps, st.one())
            e.wait_ge(dve_steps, st.count())
            t0, t1 = hx[:, 3, :, 0], hx[:, 4, :, 0]
            for w, a, b, op in ((w_r, y_r, y_i, ALU.add), (w_i, y_i, y_r, ALU.subtract)):
                tt(t0, a, x_r, ALU.mult)
                tt(t1, b, x_i, ALU.mult)
                tt(w, t0, t1, op)
                tt(w, w, sq, ALU.mult)
            a_r, a_i = sums[:, 0, :, 1], sums[:, 1, :, 1]
            for c, x, y, op in ((0, w_r, w_i, ALU.subtract), (1, w_i, w_r, ALU.add)):
                tt(t0, a_r, x, ALU.mult)
                tt(t1, a_i, y, ALU.mult)
                tt(t0, t0, t1, op)
                tt(roots[:, c], sums[:, c, :, 0], t0, ALU.subtract)
            v.memset(taps[:, 0:P], 0.0).then_inc(s4_roots, 1)
            st.close()

        def dve_taps(e, st):
            v = nc.vector
            e.wait_ge(s4_taps, 1)
            v.tensor_copy(taps[:, P:P + D], bank[6][:, :]).then_inc(dve_steps, st.one())
            e.wait_ge(dve_steps, st.count())
            v.tensor_tensor(taps[:, P:P + 1], taps[:, P:P + 1], d_c, ALU.add).then_inc(s4_row, 1)
            st.close()

        def pe_s4(e):
            t = nc.tensor
            e.wait_ge(s4_bw, 1)
            t.matmul(bank[6][:, 0:2 * NS], bp_w[0:NS, :], vct[0:NS].rearrange("p n c -> p (n c)"), start=True, stop=True).then_inc(s4_b, 1)

        def pe_taps(e):
            t = nc.tensor
            e.wait_ge(s4_roots, 1)
            for c in range(2):
                for k in range(KB):
                    i = t.matmul(bank[6][:, :], roots[:, c, k:k + 1].to_broadcast([P, P]), dft[:, c, k, :], start=(c + k == 0), stop=(c + k == KB))
            i.then_inc(s4_taps, 1)

        def sp_taps(e):
            e.wait_ge(s4_row, 1)
            e.dma_start(kpad_d, taps).then_inc(s4_out, 16)
            e.wait_ge(s4_out, 16)
            e.dma_start(toep[:, :], bass.AP(kpad_d.tensor, P, [[P + D - 1, P], [1, D]])).then_inc(s4_toep, 16)

        def pool_a(e, st):
            g = nc.gpsimd
            g.memset(zero[:, :], 0).then_inc(pool_steps, st.one())
            e.wait_ge(pool_steps, st.count())
            st.close()
            e.dma_start(slot_d.rearrange("(p m) o -> p (m o)", p=P), zero[:, :]).then_inc(slot_zero, 16)
            e.wait_ge(a_load, 32)

            def inverse_root(b, u):
                e.wait_ge(a_stat[u % 2], nth(b, u))
                g.tensor_tensor(rstd[:, u, :], mv[:, u, 1:2], const("eps"), ALU.add).then_inc(pool_steps, st.one())
                e.wait_ge(pool_steps, st.count())
                g.tensor_tensor(rstd[:, u, :], rstd[:, u, :], const("half"), ALU.pow).then_inc(a_rstd[u % 2], 1)

            def add(b, u):
                e.wait_ge(a_rope[u % 2], nth(b, u))
                alone(e)
                for w, off, heads, dst in ((D, 0, H, q_tok), (KV * HD, D, KV, k_tok)):
                    xc, xs = (rt[:, u % 2, i, off:off + w].rearrange("p (h c d) -> p h c d", h=heads, c=2) for i in (0, 1))
                    o = dst[:, b, u, :].rearrange("p (h c d) -> p h c d", h=heads, c=2)
                    for c, op in ((0, ALU.subtract), (1, ALU.add)):
                        i = g.tensor_tensor(o[:, :, c, :], xc[:, :, c, :], xs[:, :, 1 - c, :], op)
                        i.then_inc(a_add[u % 2], 1)

            def sequence(b, more):
                for u in range(TPB):
                    if u + 2 < TPB or more:
                        inverse_root(b + (u + 2) // TPB, (u + 2) % TPB)
                    add(b, u)

            inverse_root(0, 0)
            inverse_root(0, 1)
            st.close()
            sequence(0, True)
            st.close()
            with e.Fori(1, NB - 1) as b:
                st.enter(b, TPB)
                sequence(b, True)
            st.leave(1, NB - 1)
            sequence(NB - 1, False)
            st.close()

        def act_a(e):
            act_s4_loads(e)
            for x in range(E):
                e.dma_start(w_e[:, x], we_d[x].rearrange("(k p) n -> p k n", p=P)).then_inc(e_load, 16)
            e.wait_ge(s4_load, 144)
            nc.scalar.activation(inv_step, log_step, ACT.Exp, scale=-1.0).then_inc(s4_step, 1)
            def sequence(b):
                for u in range(TPB):
                    e.wait_ge(a_tr[u % 2], nth(b, u))
                    if due(at := nth(b, u) - 1):
                        e.wait_ge(a_kvg[u % 2], at)
                    nc.scalar.copy(xt[:, u % 2, :, :].rearrange("p k t -> p (k t)"), ps_t[u % 2][:, :]).then_inc(a_xt[u % 2], 1)

            sequence(0)
            with e.Fori(1, NB) as b:
                sequence(b)

        def pe_a(e):
            t = nc.tensor
            e.wait_ge(a_load, 32)

            def turn(b, u):
                e.wait_ge(a_xn[u % 2], nth(b, u))
                if due(at := nth(b, u) - 1):
                    e.wait_ge(a_xt[u % 2], at)
                for k in range(KB):
                    i = t.transpose(ps_t[u % 2][:, k * P:(k + 1) * P], xn[:, u % 2, k * P:(k + 1) * P], ident)
                i.then_inc(a_tr[u % 2], 1)

            pe_s4(e)
            e.wait_ge(a_w, 64)

            def sequence(b, more):
                for u in range(TPB):
                    if u + 1 < TPB or more:
                        turn(b + (u + 1) // TPB, (u + 1) % TPB)
                    e.wait_ge(a_xt[u % 2], nth(b, u))
                    if due(at := nth(b, u) - 1):
                        e.wait_ge(a_rope[u % 2], at)
                    for w, out, n, signal in ((wq, ps_q, D, a_q), (wkvg, ps_kvg, KVG, a_kvg)):
                        for k in range(KB):
                            i = t.matmul(out[u % 2][:, 0:n], xt[:, u % 2, k, :], w[:, k, :], start=(k == 0), stop=(k == KB - 1))
                        i.then_inc(signal[u % 2], 1)

            turn(0, 0)
            sequence(0, True)
            with e.Fori(1, NB - 1) as b:
                sequence(b, True)
            sequence(NB - 1, False)

        def dve_route(e, st):
            v = nc.vector

            def tt(out, a, b, op):
                v.tensor_tensor(out, a, b, op).then_inc(dve_steps, st.one())
                e.wait_ge(dve_steps, st.count())

            for u in range(TPB):
                e.wait_ge(a_rope[u % 2], NT // 2)
            e.wait_ge(dve_steps, st.count())
            shape = [P, NT, E, E]
            other = logit.unsqueeze(2).to_broadcast(shape)
            own = logit.unsqueeze(3).to_broadcast(shape)
            above, equal = (x.rearrange("p k v n -> p (k v n)").rearrange("p (t e j) -> p t e j", t=NT, e=E) for x in big[0:2])
            tt(above, other, own, ALU.is_gt)
            tt(equal, other, own, ALU.is_equal)
            lower = const("lower").rearrange("p (e j) -> p e j", e=E).unsqueeze(1).to_broadcast(shape)
            tt(equal, equal, lower, ALU.mult)
            tt(above, above, equal, ALU.add)
            v.tensor_reduce(rank, above, AX.X, ALU.add).then_inc(dve_steps, st.one())
            e.wait_ge(dve_steps, st.count())
            v.tensor_scalar(first, rank, 0.0, None, ALU.is_equal).then_inc(dve_steps, st.one())
            e.wait_ge(dve_steps, st.count())
            v.tensor_scalar(second, rank, 1.0, None, ALU.is_equal).then_inc(dve_steps, st.one())
            e.wait_ge(dve_steps, st.count())
            v.tensor_tensor(chosen_b, first, second, ALU.add).then_inc(r_chosen, 1)
            e.wait_ge(r_count, 1)
            flat = lambda x: x.rearrange("p t e -> p (t e)")
            v.tensor_copy(flat(tot), bank[6][:, P:2 * P]).then_inc(dve_steps, st.one())
            e.wait_ge(dve_steps, st.count())
            a, o = tot, scan_a
            for step in (1, 2, 4, 8):
                v.tensor_copy(o[:, 0:step], a[:, 0:step]).then_inc(dve_steps, st.one())
                tt(o[:, step:], a[:, step:], a[:, 0:NT - step], ALU.add)
                a, o = o, (scan_b if o is scan_a else scan_a)
            incl = a
            tt(flat(pos), flat(incl), bank[6][:, 0:P], ALU.add)
            tt(pos, pos, tot, ALU.subtract)
            n_e = incl[:, NT - 1, :]
            cmp = above.rearrange("p t e j -> p (t e j)")[:, 0:E * NT].rearrange("p (e i) -> p e i", e=E)
            tt(cmp, n_e.unsqueeze(2).to_broadcast([P, E, NT]), const("i128").unsqueeze(1).to_broadcast([P, E, NT]), ALU.is_gt)
            v.tensor_reduce(tiles_of, cmp, AX.X, ALU.add).then_inc(dve_steps, st.one())
            e.wait_ge(dve_steps, st.count())
            a, o = tiles_of, end_a
            for step in (1, 2, 4):
                v.tensor_copy(o[:, 0:step], a[:, 0:step]).then_inc(dve_steps, st.one())
                tt(o[:, step:], a[:, step:], a[:, 0:E - step], ALU.add)
                a, o = o, (end_b if o is end_a else end_a)
            end = a
            tt(o, end, tiles_of, ALU.subtract)
            v.tensor_scalar(o, o, float(P), None, ALU.mult).then_inc(dve_steps, st.one())
            e.wait_ge(dve_steps, st.count())
            tt(pos, pos, o.unsqueeze(1).to_broadcast([P, NT, E]), ALU.add)
            for k, pick in enumerate((first, second)):
                tt(pick, pick, pos, ALU.mult)
                v.tensor_reduce(slot_f, pick, AX.X, ALU.add).then_inc(dve_steps, st.one())
                e.wait_ge(dve_steps, st.count())
                v.tensor_copy(slots[:, k, :], slot_f).then_inc(r_slots, 1)
                e.wait_ge(r_slots, k + 1)
            cmp = above.rearrange("p t e j -> p (t e j)")[:, 0:MT * E].rearrange("p (i e) -> p i e", e=E)
            tt(cmp, end.unsqueeze(1).to_broadcast([P, MT, E]), const("tile").unsqueeze(2).to_broadcast([P, MT, E]), ALU.is_le)
            v.tensor_reduce(eid_f, cmp, AX.X, ALU.add).then_inc(dve_steps, st.one())
            e.wait_ge(dve_steps, st.count())
            v.tensor_scalar(eid_f, eid_f, float(E - 1), None, ALU.min).then_inc(dve_steps, st.one())
            e.wait_ge(dve_steps, st.count())
            v.tensor_copy(eid_i[:, :], eid_f[0:1, :]).then_inc(r_eid, 1)
            st.close()

        def pe_route(e):
            t = nc.tensor
            e.wait_ge(r_chosen, 1)
            rhs = chosen_b.rearrange("p t e -> p (t e)")
            e.wait_ge(s4_row, 1)
            t.matmul(bank[6][:, 0:P], tri_b[:, :], rhs, start=True, stop=True)
            t.matmul(bank[6][:, P:2 * P], ones_b[:, :], rhs, start=True, stop=True).then_inc(r_count, 1)

        def pool_route(e, st):
            e.wait_ge(slot_zero, 16)
            for k in range(TOPK):
                e.wait_ge(r_slots, k + 1)
                for n in range(NT):
                    e.indirect_dma_start(slot_d, bass.IndirectOffsetOnAxis(ap=slots[:, k, n:n + 1], axis=0),
                                         tok_i[:, n:n + 1], None).then_inc(r_scatter, 16)

        def sp_route(e):
            e.wait_ge(r_scatter, 16 * TOPK * NT)
            e.dma_start(slots_i[:, :], slot_d.rearrange("(i p) o -> p (i o)", p=P), allow_slow_non_contiguous=True)\
             .then_inc(r_load, 16)

        qstk = take([P, TPB, R, P], BF16, restart=0)
        mstk = take([P, 2, TPB, R, 32], BF16)
        kstk = take([P, TPB, P], BF16)
        qt = take([P, 2, R, S], BF16)
        kt = take([P, 2, S], BF16)
        pt = take([P, JO[-1] + R * JW[-1]])
        vb = take([P, TPB, KV, VW])
        ot = take([P, KB, TPB, P])
        oe = take([P, S])
        o2 = take([P, TPB, 2 * R * HD])
        xg = take([P, 2, D])
        xgt = take([P, KB, P])
        yo = take([P, 2, D])
        rest = take([P, TPB, R, HD])
        krest = take([P, TPB, HD])
        rmax = take([P, TPB, R])
        rmax_t = take([P, TPB, R])
        rsum = take([P, TPB, R])
        tok_b = take([P, MPB], U32)

        b_init = sem("b_init")
        b_wo = sem("b_wo")
        b_v = sem("b_v")
        b_q, b_k = sem("b_q"), sem("b_k")
        b_tq, b_te = sem("b_tq"), sem("b_te")
        b_tm, b_me = sem("b_tm"), sem("b_me")
        b_s1, b_m, b_mx = sem("b_s1"), sem("b_m"), sem("b_mx")
        b_s2, b_e, b_sel, b_pv = sem("b_s2"), sem("b_e"), sem("b_sel"), sem("b_pv")
        b_o, b_ot, b_on, b_o2, b_o2e = sem("b_o"), sem("b_ot"), sem("b_on"), sem("b_o2"), sem("b_o2e")
        b_p, b_s = sem("b_p"), sem("b_s")
        m_idx, m_xt, m_xe, m_y, m_ye = sem("m_idx"), sem("m_xt"), sem("m_xe"), sem("m_y"), sem("m_ye")
        m_x, m_st = sems("m_x", 2), sems("m_st", 2)

        NG = KV
        JOBS1 = [(q, h, n) for q, n in ((3, 1), (2, 1), (1, 2), (0, 4)) for h in range(0, R, n)]
        JOBS2 = [(j, h, n) for j, n in ((0, 1), (1, 1), (2, 2), (3, 4)) for h in range(0, R, n)]
        NJ = len(JOBS1)
        LAST2 = [max(i for i, job in enumerate(JOBS2) if job[0] == j) + 1 for j in range(TPB)]
        tb = bank[5][:, :].bitcast(BF16).rearrange("p (h s) -> p h s", h=2)
        xb = bank[6][:, :].rearrange("p (k t) -> p k t", k=KB)

        def since(b, per, k):
            return b * per + k

        def phase_a_over(e):
            for u in range(TPB):
                e.wait_ge(a_add[u % 2], 4 * NT // 2)
                e.wait_ge(a_store[u], 16 * NB)
            e.wait_ge(r_eid, 1)
            e.wait_ge(s4_toep, 16)
            e.wait_ge(e_load, 16 * E)

        def pool_b(e, st):
            g = nc.gpsimd
            phase_a_over(e)
            g.memset(kstk[:, :, 112:P], 1.0).then_inc(pool_steps, st.one())
            g.memset(mstk, 0.0).then_inc(pool_steps, st.one())
            g.memset(qstk[:, :, :, 112:P], 0.0).then_inc(pool_steps, st.one())
            g.memset(vb[:, :, :, HD:HD + 1], 1.0).then_inc(pool_steps, st.one())
            g.memset(vb[:, :, :, HD + 1:], 0.0).then_inc(b_init, 1)
            e.wait_ge(pool_steps, st.count())
            e.wait_ge(b_init, 1)
            e.wait_ge(r_load, 16)
            st.close()

            def values(b):
                if due(at := since(b, 4 * NG, 0)):
                    e.wait_ge(b_pv, at)
                alone(e)
                g.tensor_copy(vb[:, :, :, 0:HD], v_tok[:, b].rearrange("p t (h d) -> p t h d", h=KV)).then_inc(b_v, 1)

            def k_parts(b, h):
                if due(at := since(b, 3 * NG, 3 * h)):
                    e.wait_ge(b_tq, at)
                e.wait_ge(pool_steps, st.count())
                alone(e)
                k = k_tok[:, b, :, HD * h:HD * h + HD]
                shape = [P, TPB, 2, HD]

                def twice(a, c):
                    return kstk[:, :, a:c].rearrange("p t (n d) -> p t n d", n=2)

                g.tensor_copy(twice(0, 32), k.unsqueeze(2).to_broadcast(shape)).then_inc(pool_steps, st.one())
                g.tensor_copy(kstk[:, :, 96:112], k).then_inc(pool_steps, st.one())
                e.wait_ge(pool_steps, st.count())
                alone(e)
                g.tensor_tensor(krest, k, kstk[:, :, 0:HD], ALU.subtract).then_inc(pool_steps, st.one())
                e.wait_ge(pool_steps, st.count())
                alone(e)
                g.tensor_copy(twice(32, 64), krest.unsqueeze(2).to_broadcast(shape)).then_inc(pool_steps, st.one())
                e.wait_ge(pool_steps, st.count())
                alone(e)
                g.tensor_tensor(twice(64, 96), krest.unsqueeze(2).to_broadcast(shape), twice(32, 64), ALU.subtract).then_inc(b_k, 1)

            def select(b, h):
                for j in range(TPB):
                    e.wait_ge(b_e, since(b, NJ * NG, NJ * h + LAST2[j]))
                    alone(e)
                    diag = pt[:, JO[j]:JO[j] + R * JW[j]].rearrange("p (h q) -> p h q", h=R)[:, :, 0:P]
                    g.affine_select(out=diag, in_=diag, compare_op=ALU.is_ge, fill=0.0, base=0,
                                    pattern=[[0, R], [1, P]], channel_multiplier=-1).then_inc(b_sel, 1)

            def gather(b, m):
                if due(at := since(b, MPB, m - 1)):
                    e.wait_ge(m_xt, at)
                alone(e)
                e.indirect_dma_start(xg[:, m % 2, :], None, xn_d, bass.IndirectOffsetOnAxis(ap=tok_b[:, m:m + 1], axis=0))\
                 .then_inc(m_x[m % 2], 16)

            def sequence(b):
                for par in range(2):
                    if due(at := since(b, 16 * MPB // 2, 0)):
                        e.wait_ge(m_x[par], at)
                alone(e)
                g.tensor_copy(tok_b, slots_i[:, bass.ts(b, MPB)]).then_inc(m_idx, 1)
                k_parts(b, 0)
                values(b)
                e.wait_ge(m_idx, b + 1)
                gather(b, 0)
                gather(b, 1)
                k_parts(b, 1)
                for h in range(NG):
                    select(b, h)
                    if h + 2 < NG:
                        k_parts(b, h + 2)
                    gather(b, h + 2)

            sequence(0)
            st.close()
            with e.Fori(1, NB) as b:
                st.enter(b, 4 * NG)
                sequence(b)
            st.leave(1, NB)

        def dve_b(e, st):
            v = nc.vector
            phase_a_over(e)
            e.wait_ge(b_init, 1)

            def q_parts(b, h):
                if due(at := since(b, 3 * NG, 3 * h)):
                    e.wait_ge(b_tq, at)
                if due(at := since(b, 2 * NG, 2 * (h - 1))):
                    e.wait_ge(b_tm, at)
                e.wait_ge(dve_steps, st.count())
                q = q_tok[:, b, :, R * HD * h:R * HD * (h + 1)].rearrange("p t (h d) -> p t h d", h=R)
                high, mid, low = (qstk[:, :, :, a:a + HD] for a in (0, 16, 96))
                v.tensor_copy(high, q).then_inc(dve_steps, st.one())
                e.wait_ge(dve_steps, st.count())
                v.tensor_tensor(rest, q, high, ALU.subtract).then_inc(dve_steps, st.one())
                e.wait_ge(dve_steps, st.count())
                v.tensor_copy(mid, rest).then_inc(dve_steps, st.one())
                e.wait_ge(dve_steps, st.count())
                v.tensor_copy(qstk[:, :, :, 32:64], qstk[:, :, :, 0:32]).then_inc(dve_steps, st.one())
                v.tensor_copy(qstk[:, :, :, 64:96], qstk[:, :, :, 0:32]).then_inc(dve_steps, st.one())
                v.tensor_tensor(low, rest, mid, ALU.subtract).then_inc(dve_steps, st.one())
                e.wait_ge(dve_steps, st.count())
                v.tensor_copy(mstk[:, h % 2, :, :, 0:HD], low).then_inc(b_q, 1)

            def maxima(b, h):
                if due(at := since(b, NG, h)):
                    e.wait_ge(b_mx, at)
                for n, (q, r, m) in enumerate(JOBS1):
                    e.wait_ge(b_s1, since(b, NJ * NG, NJ * h + n + 1))
                    w = P * (q + 1)
                    v.tensor_reduce(rmax[:, q, r:r + m], bank[(NJ * h + n) % 2][:, 0:m * w].rearrange("p (h k) -> p h k", h=m),
                                    AX.X, ALU.max).then_inc(b_m, 1)
                e.wait_ge(b_m, since(b, NJ * NG, NJ * (h + 1)))
                part = [mstk[:, h % 2, :, :, HD + i] for i in range(3)]
                v.tensor_scalar(part[0], rmax, -1.0, None, ALU.mult).then_inc(dve_steps, st.one())
                e.wait_ge(dve_steps, st.count())
                v.scalar_tensor_tensor(out=rmax_t, in0=rmax, scalar=-1.0, in1=part[0], op0=ALU.mult, op1=ALU.subtract).then_inc(dve_steps, st.one())
                e.wait_ge(dve_steps, st.count())
                v.tensor_copy(part[1], rmax_t).then_inc(dve_steps, st.one())
                e.wait_ge(dve_steps, st.count())
                v.tensor_tensor(part[2], rmax_t, part[1], ALU.subtract).then_inc(b_mx, 1)

            def maxima_rows(b, h):
                for n in range(2):
                    e.wait_ge(b_tm, since(b, 2 * NG, 2 * h + n + 1))
                    v.tensor_copy(qt[96:P, h % 2, 2 * n:2 * n + 2, :], tb[96:P]).then_inc(b_me, 1)

            def normalise(b, h):
                e.wait_ge(b_ot, since(b, NG, h + 1))
                o4 = bank[6][:, :].rearrange("p (t r c) -> p t r c", t=TPB, r=R)
                v.reciprocal(rsum, o4[:, :, :, HD]).then_inc(dve_steps, st.one())
                if h % 2 == 0:
                    if due(at := since(b, NG // 2, h // 2)):
                        e.wait_ge(b_o2, at)
                e.wait_ge(dve_steps, st.count())
                half = o2[:, :, (h % 2) * R * HD:(h % 2 + 1) * R * HD].rearrange("p t (r d) -> p t r d", r=R)
                v.tensor_tensor(half, o4[:, :, :, 0:HD], rsum.unsqueeze(3).to_broadcast([P, TPB, R, HD]), ALU.mult)\
                    .then_inc(b_on, 1)

            def sequence(b):
                q_parts(b, 0)
                q_parts(b, 1)
                maxima(b, 0)
                maxima_rows(b, 0)
                for h in range(NG):
                    if h + 2 < NG:
                        q_parts(b, h + 2)
                    if h + 1 < NG:
                        maxima(b, h + 1)
                        maxima_rows(b, h + 1)
                    normalise(b, h)

            sequence(0)
            st.close()
            with e.Fori(1, NB) as b:
                st.enter(b, NG * (6 + 3 + 1))
                sequence(b)
            st.leave(1, NB)

        def act_b(e):
            a = nc.scalar
            phase_a_over(e)

            def turned(b, h):
                for n in range(3):
                    e.wait_ge(b_tq, since(b, 3 * NG, 3 * h + n + 1))
                    if due(at := since(b, NJ * NG, NJ * (h - 1))):
                        e.wait_ge(b_s2, at)
                    if n < 2:
                        a.copy(qt[:, h % 2, 2 * n:2 * n + 2, :], tb).then_inc(b_te, 1)
                    else:
                        a.copy(kt[:, h % 2, :], tb[:, 0, :]).then_inc(b_te, 1)

            def exps(b, h, lo, hi):
                for n in range(lo, hi):
                    j, r, m = JOBS2[n]
                    e.wait_ge(b_s2, since(b, NJ * NG, NJ * h + n + 1))
                    if due(at := since(b, 4 * NG, 4 * h + j - 3)):
                        e.wait_ge(b_pv, at)
                    o = pt[:, JO[j] + r * JW[j]:JO[j] + (r + m) * JW[j]]
                    a.activation(o, bank[2 + (NJ * h + n) % 2][:, 0:m * JW[j]], ACT.Exp, scale=HD ** -0.5).then_inc(b_e, 1)

            def expert_x(b, m):
                e.wait_ge(m_xt, since(b, MPB, m + 1))
                if due(at := since(b, MPB, m)):
                    e.wait_ge(m_y, at)
                a.copy(xgt.rearrange("p k t -> p (k t)"), bank[6][:, :]).then_inc(m_xe, 1)

            def expert_y(b, m):
                e.wait_ge(m_y, since(b, MPB, m + 1))
                if due(at := since(b, 16 * MPB // 2, 16 * (m // 2))):
                    e.wait_ge(m_st[m % 2], at)
                a.activation(yo[:, m % 2, :], bank[7][:, :], ACT.Relu).then_inc(m_ye, 1)

            def pair_out(b, i):
                e.wait_ge(b_o2, since(b, NG // 2, i + 1))
                if due(at := since(b, TPB, 0)):
                    e.wait_ge(b_p, at)
                a.copy(ot[:, i].rearrange("p t f -> p (t f)"), bank[6][:, :]).then_inc(b_o2e, 1)

            def sequence(b):
                turned(b, 0)
                turned(b, 1)
                expert_x(b, 0)
                expert_y(b, 0)
                for h in range(NG):
                    exps(b, h, 0, 3)
                    expert_x(b, h + 1)
                    exps(b, h, 3, NJ)
                    expert_y(b, h + 1)
                    if h % 2 == 0 and h:
                        pair_out(b, h // 2 - 1)
                    if h + 2 < NG:
                        turned(b, h + 2)
                    e.wait_ge(b_pv, since(b, 4 * NG, 4 * h + 4))
                    if due(at := since(b, NG, h)):
                        e.wait_ge(b_ot, at)
                    a.copy(oe, bank[4][:, :]).then_inc(b_o, 1)
                pair_out(b, NG // 2 - 1)
                expert_x(b, MPB - 1)
                expert_y(b, MPB - 1)
                for u in range(TPB):
                    e.wait_ge(b_p, since(b, TPB, u + 1))
                    e.wait_ge(b_q, since(b, NG, NG))
                    a.copy(s_tok[:, b, u, :], bank[u % 2][:, :]).then_inc(b_s, 1)

            sequence(0)
            with e.Fori(1, NB) as b:
                sequence(b)

        def pe_b(e):
            t = nc.tensor
            phase_a_over(e)
            e.wait_ge(b_wo, 16)
            e.wait_ge(b_init, 1)

            def turn(b, h, n):
                if n == 0:
                    e.wait_ge(b_q, since(b, NG, h + 1))
                    if h == 0:
                        if due(at := since(b, 2 * NG, 0)):
                            e.wait_ge(b_me, at)
                    elif h == 1:
                        e.wait_ge(b_te, since(b, 3 * NG, 3))
                    else:
                        e.wait_ge(b_me, since(b, 2 * NG, 2 * (h - 1)))
                else:
                    e.wait_ge(b_te, since(b, 3 * NG, 3 * h + n))
                if n == 2:
                    e.wait_ge(b_k, since(b, NG, h + 1))
                for x in range(2 if n < 2 else 1):
                    for q in range(TPB):
                        src = qstk[:, q, 2 * n + x, :] if n < 2 else kstk[:, q, :]
                        i = t.transpose(tb[:, x, q * P:(q + 1) * P], src, ident_b[:, :])
                i.then_inc(b_tq, 1)

            def turn_maxima(b, h, n):
                if n == 0:
                    e.wait_ge(b_mx, since(b, NG, h + 1))
                    if h + 1 < NG:
                        e.wait_ge(b_te, since(b, 3 * NG, 3 * (h + 2)))
                    else:
                        e.wait_ge(b_me, since(b, 2 * NG, 2 * h))
                else:
                    e.wait_ge(b_me, since(b, 2 * NG, 2 * h + 1))
                for x in range(2):
                    for q in range(TPB):
                        i = t.transpose(tb[96:P, x, q * P:(q + 1) * P], mstk[:, h % 2, q, 2 * n + x, :], ident_b[:, :])
                i.then_inc(b_tm, 1)

            def scores_1(b, h, n):
                q, r, m = JOBS1[n]
                if n == 0:
                    e.wait_ge(b_te, since(b, 3 * NG, 3 * (h + 1)))
                    if h == 0:
                        if due(at := since(b, TPB, 0)):
                            e.wait_ge(b_s, at)
                if due(at := since(b, NJ * NG, NJ * h + n - 1)):
                    e.wait_ge(b_m, at)
                w = P * (q + 1)
                for x in range(m):
                    o = bank[(NJ * h + n) % 2][:, x * w:(x + 1) * w]
                    t.matmul(o, qt[:, h % 2, r + x, q * P:(q + 1) * P], kt[:, h % 2, 0:w], start=True, stop=True)
                    i = t.matmul(o[:, q * P:], ident_b[:, :], mask_b[:, :], start=False, stop=True, skip_group_check=True)
                i.then_inc(b_s1, 1)

            def scores_2(b, h, n):
                j, r, m = JOBS2[n]
                if n == 0:
                    e.wait_ge(b_me, since(b, 2 * NG, 2 * (h + 1)))
                if due(at := since(b, NJ * NG, NJ * h + n - 1)):
                    e.wait_ge(b_e, at)
                for x in range(m):
                    i = t.matmul(bank[2 + (NJ * h + n) % 2][:, x * JW[j]:(x + 1) * JW[j]], kt[:, h % 2, j * P:(j + 1) * P],
                                 qt[:, h % 2, r + x, j * P:], start=True, stop=True)
                i.then_inc(b_s2, 1)

            def values(b, h, j):
                if j == 0:
                    if due(at := since(b, NG, h)):
                        e.wait_ge(b_o, at)
                    if h == 0:
                        e.wait_ge(b_v, b + 1)
                e.wait_ge(b_sel, since(b, 4 * NG, 4 * h + j + 1))
                for r in range(R):
                    i = t.matmul(bank[4][VW * r:VW * (r + 1), j * P:], vb[:, j, h, :],
                                 pt[:, JO[j] + r * JW[j]:JO[j] + (r + 1) * JW[j]], start=(j == 0), stop=(j == TPB - 1),
                                 skip_group_check=True)
                i.then_inc(b_pv, 1)

            def turn_out(b, h):
                e.wait_ge(b_o, since(b, NG, h + 1))
                if h % 2 == 0 and h:
                    e.wait_ge(b_o2e, since(b, NG // 2, h // 2))
                else:
                    e.wait_ge(m_xe, since(b, MPB, h + 2))
                for q in range(TPB):
                    i = t.transpose(xb[:, q, :], oe[:, q * P:(q + 1) * P], ident)
                i.then_inc(b_ot, 1)

            def turn_pair(b, h):
                e.wait_ge(b_on, since(b, NG, h + 1))
                if h + 1 < NG:
                    e.wait_ge(m_xe, since(b, MPB, h + 3))
                for q in range(TPB):
                    i = t.transpose(xb[:, q, :], o2[:, q, :], ident)
                i.then_inc(b_o2, 1)

            def expert(b, m, step):
                if step == 0:
                    e.wait_ge(m_x[m % 2], since(b, 16 * MPB // 2, 16 * (m // 2 + 1)))
                    if m == 0:
                        if due(at := since(b, MPB, 0)):
                            e.wait_ge(m_xe, at)
                    elif m == 1:
                        e.wait_ge(m_xe, since(b, MPB, 1))
                    elif m + 1 < MPB:
                        e.wait_ge(b_on, since(b, NG, m - 1))
                    else:
                        e.wait_ge(b_o2e, since(b, NG // 2, NG // 2))
                    for k in range(KB):
                        i = t.transpose(xb[:, k, :], xg[:, m % 2, k * P:(k + 1) * P], ident)
                    i.then_inc(m_xt, 1)
                    return
                if step == 1:
                    ex[0] = e.value_load(eid_i[0:1, bass.ds(b * MPB + m, 1)], min_val=0, max_val=E - 1)
                    if due(at := since(b, MPB, m)):
                        e.wait_ge(m_ye, at)
                    t.matmul(bank[7][:, :], sel_e[:, ex[0], :], be3[:, :], start=True, stop=False)
                    e.wait_ge(m_xe, since(b, MPB, m + 1))
                k = step - 1
                i = t.matmul(bank[7][:, :], xgt[:, k, :], w_e[:, ex[0], k, :], start=False, stop=(k == KB - 1))
                if k == KB - 1:
                    i.then_inc(m_y, 1)

            ex = [None]
            def sequence(b):
                for h in range(2):
                    for n in range(3):
                        turn(b, h, n)
                for n in range(NJ):
                    scores_1(b, 0, n)
                for step in range(KB + 1):
                    expert(b, 0, step)
                turn_maxima(b, 0, 0)
                turn_maxima(b, 0, 1)
                for h in range(NG):
                    for n in range(NJ):
                        if h + 1 < NG:
                            scores_1(b, h + 1, n)
                        scores_2(b, h, n)
                        if n % 2 == 0 and n >= 2:
                            expert(b, h + 1, n // 2 - 1)
                    if h % 2 == 0 and h:
                        turn_pair(b, h - 1)
                    for j in range(TPB):
                        values(b, h, j)
                        if h + 2 < NG and j < 3:
                            turn(b, h + 2, j)
                    if h + 1 < NG:
                        turn_maxima(b, h + 1, 0)
                        turn_maxima(b, h + 1, 1)
                    turn_out(b, h)
                turn_pair(b, NG - 1)
                for step in range(KB + 1):
                    expert(b, MPB - 1, step)
                for u in range(TPB):
                    if u < 2:
                        e.wait_ge(b_o2e, since(b, NG // 2, NG // 2))
                        e.wait_ge(b_m, since(b, NJ * NG, NJ * NG))
                    else:
                        e.wait_ge(b_s, since(b, TPB, u - 1))
                    for k in range(KB):
                        i = t.matmul(bank[u % 2][:, :], ot[:, k, u, :], wo[:, k, :], start=(k == 0), stop=(k == KB - 1))
                    i.then_inc(b_p, 1)

            sequence(0)
            with e.Fori(1, NB) as b:
                sequence(b)

        def sp_b(e):
            for u in range(TPB):
                e.wait_ge(a_kvg[u % 2], NT // 2)
            e.dma_start(wo, wo_d.rearrange("(k p) n -> p k n", p=P)).then_inc(b_wo, 16)
            def sequence(b):
                for m in range(MPB):
                    e.wait_ge(m_ye, since(b, MPB, m + 1))
                    e.dma_start(y_t[b * MPB + m], yo[:, m % 2, :]).then_inc(m_st[m % 2], 16)

            sequence(0)
            with e.Fori(1, NB) as b:
                sequence(b)

        w_lin = w_e[:, 0]
        c_x = take([P, TPB, D], restart=0)
        c_y = take([P, TPB, TOPK, D])
        c_xn = take([P, 2, D])
        c_xt = take([P, 2, KB, P])
        c_g = take([P, 2, D])
        c_o = take([P, 2, D])
        c_st = take([P, TPB, 8])
        c_mv = take([P, TPB, 2])
        c_rstd = take([P, TPB, 1])
        c_bias = take([P, D])
        c_scale = take([P, KB, KB])
        c_slot = take([P, TOPK, TPB], U32)
        c_w, c_ws = sem("c_w"), sem("c_ws")
        c_ld, c_ga = sems("c_ld", TPB), sems("c_ga", TPB)
        c_idx = sem("c_idx")
        c_z, c_gate, c_x1, c_stat, c_r, c_n = (sems(n, 2) for n in ("c_z", "c_gate", "c_x1", "c_stat", "c_r", "c_n"))
        c_tr, c_te, c_lin, c_conv, c_pre, c_sil, c_done = (
            sems(n, 2) for n in ("c_tr", "c_te", "c_lin", "c_conv", "c_pre", "c_sil", "c_done"))
        c_out = sems("c_out", TPB)

        def phase_b_over(e):
            e.wait_ge(b_s, NB * TPB)
            for par in range(2):
                e.wait_ge(m_st[par], 16 * NB * MPB // 2)

        def sp_c(e):
            phase_b_over(e)
            e.dma_start(w_lin, wft_d.rearrange("(k p) n -> p k n", p=P)).then_inc(c_w, 16)
            e.dma_start(c_bias, bf_d.partition_broadcast(P)).then_inc(c_w, 16)
            e.dma_start(c_scale, sc_d.partition_broadcast(P)).then_inc(c_w, 16)
            for u in range(TPB):
                e.dma_start(c_x[:, u, :], x_t[u]).then_inc(c_ld[u], 16)

            def go(b, more):
                for u in range(TPB):
                    e.wait_ge(c_done[u % 2], nth(b, u))
                    e.dma_start(out_t[b * TPB + u], c_o[:, u % 2, :]).then_inc(c_out[u], 16)
                    if more:
                        e.dma_start(c_x[:, u, :], x_t[(b + 1) * TPB + u]).then_inc(c_ld[u], 16)

            go(0, True)
            with e.Fori(1, NB - 1) as b:
                go(b, True)
            go(NB - 1, False)
            for u in range(TPB):
                e.wait_ge(c_out[u], 16 * NB)

        def pool_c(e, st):
            g = nc.gpsimd
            phase_b_over(e)

            def rows(b):
                for u in range(TPB):
                    if due(at := 32 * b):
                        e.wait_ge(c_ga[u], at)
                alone(e)
                g.tensor_copy(c_slot, slots[:, :, bass.ts(b, TPB)]).then_inc(c_idx, 1)
                e.wait_ge(c_idx, b + 1)
                for u in range(TPB):
                    if due(at := nth(b, u) - 2):
                        e.wait_ge(c_x1[u % 2], at)
                    alone(e)
                    for k in range(TOPK):
                        e.indirect_dma_start(c_y[:, u, k, :], None, y_d, bass.IndirectOffsetOnAxis(ap=c_slot[:, k, u:u + 1], axis=0))\
                         .then_inc(c_ga[u], 16)

            def root(b, u):
                e.wait_ge(c_stat[u % 2], nth(b, u))
                g.tensor_tensor(c_rstd[:, u, :], c_mv[:, u, 1:2], const("eps"), ALU.add).then_inc(pool_steps, st.one())
                e.wait_ge(pool_steps, st.count())
                g.tensor_tensor(c_rstd[:, u, :], c_rstd[:, u, :], const("half"), ALU.pow).then_inc(c_r[u % 2], 1)

            def go(b, more):
                for u in range(TPB):
                    root(b, u)
                    if u == TPB - 1 and more:
                        rows(b + 1)

            rows(0)
            go(0, True)
            st.close()
            with e.Fori(1, NB - 1) as b:
                st.enter(b, TPB)
                go(b, True)
            st.leave(1, NB - 1)
            go(NB - 1, False)
            st.close()

        def dve_c(e, st):
            v = nc.vector
            phase_b_over(e)
            e.wait_ge(c_w, 48)
            w4 = w_lin.rearrange("p k (o c) -> p k o c", o=KB)
            sc4 = c_scale.rearrange("p o k -> p k o").unsqueeze(3)
            for k in range(KB):
                i = v.tensor_tensor(w4[:, k], w4[:, k], sc4[:, k].to_broadcast([P, KB, P]), ALU.mult)
                i.then_inc(c_ws, 1)

            def front(b, u):
                e.wait_ge(c_ga[u], b * 32 + 32)
                v.tensor_tensor(c_y[:, u, 0, :], c_y[:, u, 0, :], c_y[:, u, 1, :], ALU.add).then_inc(c_z[u % 2], 1)
                e.wait_ge(c_gate[u % 2], nth(b, u))
                v.tensor_tensor(s_tok[:, b, u, :], s_tok[:, b, u, :], c_y[:, u, 1, :], ALU.mult).then_inc(dve_steps, st.one())
                e.wait_ge(c_ld[u], b * 16 + 16)
                e.wait_ge(dve_steps, st.count())
                v.tensor_tensor(s_tok[:, b, u, :], s_tok[:, b, u, :], c_x[:, u, :], ALU.add).then_inc(c_x1[u % 2], 1)
                e.wait_ge(c_x1[u % 2], nth(b, u))
                alone(e)
                v.bn_stats(c_st[:, u, 0:6], s_tok[:, b, u, :]).then_inc(dve_steps, st.one())
                e.wait_ge(dve_steps, st.count())
                alone(e)
                v.bn_aggr(c_mv[:, u, :], c_st[:, u, 0:6]).then_inc(c_stat[u % 2], 1)

            def norm(b, u):
                e.wait_ge(c_stat[u % 2], nth(b, u))
                if due(at := nth(b, u) - 1):
                    e.wait_ge(c_tr[u % 2], at)
                e.wait_ge(c_r[u % 2], nth(b, u))
                v.tensor_scalar(c_xn[:, u % 2, :], s_tok[:, b, u, :], c_mv[:, u, 0:1], c_rstd[:, u, :],
                                ALU.subtract, ALU.mult).then_inc(c_n[u % 2], 1)

            def back(b, u):
                e.wait_ge(c_lin[u % 2], nth(b, u))
                if due(at := nth(b, u) - 1):
                    e.wait_ge(c_done[u % 2], at)
                v.tensor_tensor(c_g[:, u % 2, :], bank[2 + u % 2][:, :], c_bias, ALU.add).then_inc(c_pre[u % 2], 1)
                e.wait_ge(c_conv[u % 2], nth(b, u))
                e.wait_ge(c_sil[u % 2], nth(b, u))
                if u >= 2:
                    e.wait_ge(c_out[u - 2], 16 * b + 16)
                else:
                    if due(at := 16 * b):
                        e.wait_ge(c_out[u + 2], at)
                v.tensor_tensor(c_o[:, u % 2, :], bank[4 + u % 2][:, :], c_g[:, u % 2, :], ALU.mult).then_inc(dve_steps, st.one())
                e.wait_ge(dve_steps, st.count())
                v.tensor_tensor(c_o[:, u % 2, :], c_o[:, u % 2, :], s_tok[:, b, u, :], ALU.add).then_inc(c_done[u % 2], 1)

            def go(b, more):
                for u in range(TPB):
                    nxt = (b + (u + 1) // TPB, (u + 1) % TPB)
                    if u + 1 < TPB or more:
                        front(*nxt)
                        norm(*nxt)
                    back(b, u)

            front(0, 0)
            norm(0, 0)
            st.close()
            go(0, True)
            st.close()
            with e.Fori(1, NB - 1) as b:
                st.enter(b, TPB * 3)
                go(b, True)
            st.leave(1, NB - 1)
            go(NB - 1, False)
            st.close()

        def act_c(e):
            a = nc.scalar
            phase_b_over(e)

            def gate(b, u):
                e.wait_ge(c_z[u % 2], nth(b, u))
                a.activation(c_y[:, u, 1, :], c_y[:, u, 0, :], ACT.Silu, scale=1.0 / TOPK).then_inc(c_gate[u % 2], 1)

            def go(b, more):
                for u in range(TPB):
                    if u + 1 < TPB or more:
                        nxt = (b + (u + 1) // TPB, (u + 1) % TPB)
                        gate(*nxt)
                        lift(*nxt)
                    e.wait_ge(c_pre[u % 2], nth(b, u))
                    a.activation(c_g[:, u % 2, :], c_g[:, u % 2, :], ACT.Silu).then_inc(c_sil[u % 2], 1)

            def lift(b, u):
                e.wait_ge(c_tr[u % 2], nth(b, u))
                if due(at := nth(b, u) - 1):
                    e.wait_ge(c_conv[u % 2], at)
                a.copy(c_xt[:, u % 2].rearrange("p k t -> p (k t)"), bank[u % 2][:, :]).then_inc(c_te[u % 2], 1)

            gate(0, 0)
            lift(0, 0)
            go(0, True)
            with e.Fori(1, NB - 1) as b:
                go(b, True)
            go(NB - 1, False)

        def pe_c(e):
            t = nc.tensor
            phase_b_over(e)
            e.wait_ge(c_ws, KB)

            def turn(b, u):
                e.wait_ge(c_n[u % 2], nth(b, u))
                if due(at := nth(b, u) - 1):
                    e.wait_ge(c_te[u % 2], at)
                for k in range(KB):
                    i = t.transpose(bank[u % 2][:, k * P:(k + 1) * P], c_xn[:, u % 2, k * P:(k + 1) * P], ident)
                i.then_inc(c_tr[u % 2], 1)

            def work(b, u):
                e.wait_ge(c_te[u % 2], nth(b, u))
                if due(at := nth(b, u) - 1):
                    e.wait_ge(c_done[u % 2], at)
                for k in range(KB):
                    i = t.matmul(bank[2 + u % 2][:, :], c_xt[:, u % 2, k, :], w_lin[:, k, :], start=(k == 0), stop=(k == KB - 1))
                i.then_inc(c_lin[u % 2], 1)
                for k in range(KB):
                    i = t.matmul(bank[4 + u % 2][:, k * P:], c_xt[:, u % 2, k, :], toep[:, 0:D - k * P],
                                 start=(k == 0), stop=(k == KB - 1), skip_group_check=True)
                i.then_inc(c_conv[u % 2], 1)

            def go(b, more):
                for u in range(TPB):
                    if u + 1 < TPB or more:
                        turn(b + (u + 1) // TPB, (u + 1) % TPB)
                    work(b, u)

            turn(0, 0)
            go(0, True)
            with e.Fori(1, NB - 1) as b:
                go(b, True)
            go(NB - 1, False)

        @block.sync
        def _(e):
            sp_a(e)
            sp_taps(e)
            sp_route(e)
            sp_b(e)
            sp_c(e)

        @block.vector
        def _(e):
            st = Steps()
            dve_s4(e, st)
            dve_a(e, st)
            dve_taps(e, st)
            dve_route(e, st)
            dve_b(e, st)
            dve_c(e, st)

        @block.gpsimd
        def _(e):
            st = Steps()
            pool_a(e, st)
            pool_route(e, st)
            pool_b(e, st)
            pool_c(e, st)

        @block.scalar
        def _(e):
            act_a(e)
            act_b(e)
            act_c(e)

        @block.tensor
        def _(e):
            pe_a(e)
            pe_taps(e)
            pe_route(e)
            pe_b(e)
            pe_c(e)


_INS = ["L0_attn_x", "L0_attn_wq", "L0_attn_wk", "L0_attn_wv", "L0_attn_wo", "L0_ffn_W_gate", "L0_ffn_b_gate",
        "L0_ffn_W_e", "L0_ffn_b_e", "L1_attn_Lambda_ri", "L1_attn_p_ri", "L1_attn_q_ri", "L1_attn_Vc_ri",
        "L1_attn_Ct_ri", "L1_attn_Bp", "L1_attn_D", "L1_attn_log_step", "L1_ffn_weight",
        "L1_ffn_weight_scale_inv", "L1_ffn_bias"]
_TURNED = {"L1_attn_Vc_ri": (1, 0, 2), "L1_ffn_weight": (1, 0)}


def kernel(**inputs):
    import concourse.bacc as bacc
    from concourse.bass_utils import run_bass_kernel_spmd

    nc = bacc.Bacc("TRN2", target_bir_lowering=False, num_devices=1)
    given = [(n, np.ascontiguousarray(np.asarray(inputs[n]).transpose(_TURNED[n]) if n in _TURNED else inputs[n])) for n in _INS]
    given += list(zip(("constants", "dft"), constants()))
    arrays = {f"in_{n}": a for n, a in given}
    args = [nc.dram_tensor(f"in_{n}", a.shape, mybir.dt.from_np(a.dtype), kind="ExternalInput").ap() for n, a in given]
    out = nc.dram_tensor("out", (NB, S, D), F32, kind="ExternalOutput").ap()
    build(nc, *args, out)
    return run_bass_kernel_spmd(nc, [arrays], core_ids=[0]).results[0]["out"]
```

```python
from contextlib import ExitStack

import numpy as np

import concourse.bass as bass
from concourse import mybir
from concourse.alu_op_type import AluOpType as ALU

ACT = mybir.ActivationFunctionType
AX = mybir.AxisListType
F32 = mybir.dt.float32
BF16 = mybir.dt.bfloat16
U32 = mybir.dt.uint32
I32 = mybir.dt.int32

P = 128
NB, S, D = 4, 512, 512
KB = D // P
TPB = S // P
NT = NB * TPB
H, HD, KV = 32, 16, 8
R = H // KV
E, TOPK = 8, 2
NS = 64
MT = NT * TOPK + E
MPB = MT // NB
EPS = 1e-5
NEG = -1.0e30
VW = 32
KVG = 2 * KV * HD + E
JW = [S - P * j for j in range(TPB)]
JO = [R * sum(JW[:j]) for j in range(TPB)]

COLS = {}
_at = 0
for _name, _n in (("ident", P), ("mask", P), ("tri", P), ("cos", TPB * 8), ("sin", TPB * 8), ("s4", 16),
                  ("lower", E * E), ("i128", NT), ("tile", MT), ("token", NT), ("half", 1), ("eps", 1), ("sel", E)):
    COLS[_name] = (_at, _at + _n)
    _at += _n
NCONST = _at


def constants():
    c = np.zeros((P, NCONST), np.float32)

    def put(name, a):
        c[:, COLS[name][0]:COLS[name][1]] = np.asarray(a, np.float32).reshape(-1, COLS[name][1] - COLS[name][0])

    p = np.arange(P)
    put("ident", np.eye(P))
    put("mask", np.where(p[None, :] > p[:, None], NEG, 0.0))
    put("tri", p[:, None] < p[None, :])
    freq = (np.float32(1.0) / np.float32(10000.0) ** (np.arange(0, HD, 2, dtype=np.float32) / np.float32(HD))).astype(np.float32)
    angle = (np.arange(S, dtype=np.float32)[:, None] * freq[None, :]).astype(np.float32).astype(np.float64)
    put("cos", np.cos(angle).reshape(TPB, P, 8).transpose(1, 0, 2).reshape(P, -1))
    put("sin", np.sin(angle).reshape(TPB, P, 8).transpose(1, 0, 2).reshape(P, -1))
    theta = 2 * np.pi * np.arange(D) / D
    s4 = np.stack([1 - np.cos(theta), np.sin(theta), (1 + np.cos(theta)) / 2, -np.sin(theta) / 2])
    put("s4", s4.reshape(4, KB, P).transpose(2, 0, 1).reshape(P, -1))
    put("lower", (np.arange(E)[None, :] < np.arange(E)[:, None]).reshape(1, -1))
    put("i128", P * np.arange(NT)[None, :])
    put("tile", np.arange(MT)[None, :])
    put("token", p[:, None] + P * np.arange(NT)[None, :])
    put("half", -0.5)
    put("eps", EPS)
    put("sel", np.arange(E)[None, :] == p[:, None] % 32)
    ang = 2 * np.pi * ((np.arange(D)[:, None] * np.arange(D)[None, :]) % D) / D
    dft = np.stack([np.cos(ang), -np.sin(ang)]) / D
    return c, dft.astype(np.float32)


def due(n):
    return not isinstance(n, int) or n > 0


def nth(b, u):
    return b * (TPB // 2) + u // 2 + 1


def alone(e):
    e.nop(nofuse=True)


class Steps:

    def __init__(self):
        self.base, self.k, self.loop, self.per, self.start = 0, 0, None, 0, 0

    def one(self):
        self.k += 1
        return 1

    def count(self):
        n = self.base + self.k
        assert n > 0
        return n if self.loop is None else (self.loop - self.start) * self.per + n

    def enter(self, loop, per, start=1):
        self.close()
        self.loop, self.per, self.start = loop, per, start

    def leave(self, start, end):
        assert self.k == self.per, (self.k, self.per)
        self.base += self.per * (end - start)
        self.loop, self.k = None, 0

    def close(self):
        self.base += self.k
        self.k = 0


def build(nc, x_d, wq_d, wk_d, wv_d, wo_d, wg_d, bg_d, we_d, be_d, lam_d, p_d, q_d, vct_d, ct_d, bp_d, dd_d,
          step_d, wft_d, sc_d, bf_d, const_d, dft_d, out_d):
    ctx = ExitStack()
    with ctx:
        def sb(name, shape, dt=F32):
            return ctx.enter_context(nc.sbuf_tensor(name, shape, dt))

        def ps(name, shape, dt=F32):
            return ctx.enter_context(nc.psum_tensor(name, shape, dt))

        def sem(name):
            return ctx.enter_context(nc.semaphore(name))

        def sems(name, n):
            return [sem(f"{name}{i}") for i in range(n)]

        xn_d = nc.dram_tensor("xn_rows", [NT * P, D], F32).ap()
        slot_d = nc.dram_tensor("token_of_slot", [MT * P, 1], U32).ap()
        y_d = nc.dram_tensor("expert_rows", [MT * P, D], F32).ap()
        kpad_d = nc.dram_tensor("s4_taps_rows", [P, P + D], F32).ap()

        x_t = x_d.rearrange("b (t p) d -> (b t) p d", p=P)
        out_t = out_d.rearrange("b (t p) d -> (b t) p d", p=P)
        xn_t = xn_d.rearrange("(n p) d -> n p d", p=P)
        y_t = y_d.rearrange("(n p) d -> n p d", p=P)

        cst = sb("cst", [P, NCONST])

        def const(name):
            return cst[:, COLS[name][0]:COLS[name][1]]

        ident = const("ident")
        ident_b = sb("ident_b", [P, P], BF16)
        mask_b = sb("mask_b", [P, P], BF16)
        tri_b = sb("tri_b", [P, P], BF16)
        ones_b = sb("ones_b", [P, P], BF16)
        w_e = sb("w_e", [P, E, KB, D])
        w_proj = sb("w_proj", [P, KB * (D + KVG)])
        wq = w_proj[:, 0:KB * D].rearrange("p (k n) -> p k n", k=KB)
        wkvg = w_proj[:, KB * D:].rearrange("p (k n) -> p k n", k=KB)
        wo = wq
        q_tok = sb("q_tok", [P, NB, TPB, D])
        s_tok = q_tok
        k_tok = sb("k_tok", [P, NB, TPB, KV * HD])
        v_tok = sb("v_tok", [P, NB, TPB, KV * HD])
        toep = sb("toep", [P, D])
        slots = sb("slots", [P, TOPK, NT], U32)
        slots_i = sb("slots_i", [P, MT], U32)
        eid_i = sb("eid_i", [1, MT], I32)
        be3 = sb("be3", [P, D], BF16)
        sel_e = sb("sel_e", [P, E, P], BF16)
        zero = sb("zero", [P, MT], U32)
        tok_i = sb("tok_i", [P, NT], U32)
        NAR = 18400
        arena = sb("arena", [P, NAR])
        used = [0]

        def take(shape, dt=F32, restart=None):
            if restart is not None:
                used[0] = restart
            n = int(np.prod(shape[1:]))
            words = n if dt in (F32, U32, I32) else (n + 1) // 2
            a = arena[:, used[0]:used[0] + words]
            used[0] += words
            assert used[0] <= NAR, used[0]
            if dt != F32:
                a = a.bitcast(dt)
            names = "abcdef"[:len(shape) - 1]
            if len(shape) > 2:
                a = a.rearrange(f"p ({' '.join(names)}) -> p {' '.join(names)}",
                                **{m: k for m, k in zip(names, shape[1:])})
            return a

        bank = [ps(f"bank{i}", [P, D]) for i in range(8)]

        a_load = sem("a_load")
        a_w = sem("a_w")
        a_x = sems("a_x", TPB)
        a_stat = sems("a_stat", 2)
        a_rstd = sems("a_rstd", 2)
        a_xn = sems("a_xn", 2)
        a_store = sems("a_store", TPB)
        a_tr = sems("a_tr", 2)
        a_xt = sems("a_xt", 2)
        a_q = sems("a_q", 2)
        a_kvg = sems("a_kvg", 2)
        a_rope = sems("a_rope", 2)
        a_add = sems("a_add", 2)
        dve_steps, pool_steps = sem("dve_steps"), sem("pool_steps")

        xin = take([P, TPB, D], restart=0)
        xn = take([P, 2, D])
        xt = take([P, 2, KB, P])
        rt = take([P, 2, 2, D + KV * HD])
        stats = take([P, TPB, 8])
        mv = take([P, TPB, 2])
        rstd = take([P, TPB, 1])
        bgb = take([P, E])
        logit = take([P, NT, E])
        be_f = take([P, D])
        e_load = sem("e_load")
        be_load = sem("be_load")
        ps_t, ps_q, ps_kvg = bank[0:2], bank[2:4], bank[4:6]

        lam_b = take([P, NS, 2])
        left_b = take([P, 2, NS, 2])
        right_b = take([P, 2, NS, 2])
        vct = take([P, NS, 2])
        bp_c = take([P, 1])
        bp_w = take([P, P])
        log_step = take([P, 1])
        inv_step = take([P, 1])
        d_c = take([P, 1])
        dft = take([P, 2, KB, D])
        num = take([P, 2, 2, 2, NS])
        num_t = take([P, 2, 2, NS])
        den_r, den_i, den_a, den_b = (take([P, KB, NS]) for _ in range(4))
        big = [take([P, KB, 4, NS]) for _ in range(3)]
        sums = take([P, 2, KB, 4])
        hx = take([P, 6, KB, 2])
        w_r, w_i, sq = (take([P, KB]) for _ in range(3))
        roots = take([P, 2, KB])
        taps = take([P, P + D])
        s4_load = sem("s4_load")
        s4_b = sem("s4_b")
        s4_bw = sem("s4_bw")
        s4_step = sem("s4_step")
        s4_roots = sem("s4_roots")
        s4_taps = sem("s4_taps")
        s4_row = sem("s4_row")
        s4_out = sem("s4_out")
        s4_toep = sem("s4_toep")
        slot_zero = sem("slot_zero")

        rank = take([P, NT, E], restart=0)
        first, second, tot, scan_a, scan_b, pos = (take([P, NT, E]) for _ in range(6))
        chosen_b = take([P, NT, E], BF16)
        tiles_of, end_a, end_b = (take([P, E]) for _ in range(3))
        slot_f = take([P, NT])
        eid_f = take([P, MT])
        r_chosen = sem("r_chosen")
        r_count = sem("r_count")
        r_slots = sem("r_slots")
        r_eid = sem("r_eid")
        r_scatter = sem("r_scatter")
        r_load = sem("r_load")

        block = ctx.enter_context(nc.Block())

        def sp_a(e):
            e.dma_start(cst[:, :], const_d).then_inc(a_load, 16)
            e.dma_start(bgb, bg_d.partition_broadcast(P)).then_inc(a_load, 16)
            e.dma_start(wq, wq_d.rearrange("(k p) n -> p k n", p=P)).then_inc(a_w, 16)
            e.dma_start(wkvg[:, :, 0:KV * HD], wk_d.rearrange("(k p) n -> p k n", p=P)).then_inc(a_w, 16)
            e.dma_start(wkvg[:, :, KV * HD:2 * KV * HD], wv_d.rearrange("(k p) n -> p k n", p=P)).then_inc(a_w, 16)
            e.dma_start(wkvg[:, :, 2 * KV * HD:], wg_d.rearrange("(k p) n -> p k n", p=P)).then_inc(a_w, 16)
            for u in range(TPB):
                e.dma_start(xin[:, u, :], x_t[u]).then_inc(a_x[u], 16)
            for part in range(3):
                e.dma_start(be_f[32 * part:32 * part + E, :], be_d).then_inc(be_load, 16)

            def store_and_load(b, more):
                for u in range(TPB):
                    e.wait_ge(a_xn[u % 2], nth(b, u))
                    e.dma_start(xn_t[b * TPB + u], xn[:, u % 2, :]).then_inc(a_store[u], 16)
                    if more:
                        e.dma_start(xin[:, u, :], x_t[(b + 1) * TPB + u]).then_inc(a_x[u], 16)

            store_and_load(0, True)
            with e.Fori(1, NB - 1) as b:
                store_and_load(b, True)
            store_and_load(NB - 1, False)

        def dve_a(e, st):
            v = nc.vector
            e.wait_ge(a_load, 32)
            v.tensor_copy(ident_b[:, :], ident).then_inc(dve_steps, st.one())
            v.tensor_copy(mask_b[:, :], const("mask")).then_inc(dve_steps, st.one())
            v.tensor_copy(tri_b[:, :], const("tri")).then_inc(dve_steps, st.one())
            v.memset(ones_b[:, :], 1.0).then_inc(dve_steps, st.one())
            v.tensor_copy(sel_e[:, :, :], const("sel").unsqueeze(2).to_broadcast([P, E, P])).then_inc(dve_steps, st.one())
            v.memset(be3[:, :], 0.0).then_inc(dve_steps, st.one())
            e.wait_ge(be_load, 48)
            e.wait_ge(dve_steps, st.count())
            for part in range(3):
                rows = slice(32 * part, 32 * part + E)
                for cut in range(part + 1):
                    v.tensor_copy(be3[rows, :], be_f[rows, :]).then_inc(dve_steps, st.one())
                    e.wait_ge(dve_steps, st.count())
                    if cut < part:
                        v.tensor_tensor(be_f[rows, :], be_f[rows, :], be3[rows, :], ALU.subtract).then_inc(dve_steps, st.one())
                        e.wait_ge(dve_steps, st.count())
            v.tensor_copy(tok_i[:, :], const("token")).then_inc(dve_steps, st.one())
            st.close()

            def stat(b, u):
                e.wait_ge(a_x[u], b * 16 + 16)
                v.bn_stats(stats[:, u, 0:6], xin[:, u, :]).then_inc(dve_steps, st.one())
                e.wait_ge(dve_steps, st.count())
                alone(e)
                v.bn_aggr(mv[:, u, :], stats[:, u, 0:6]).then_inc(a_stat[u % 2], 1)

            def normalise(b, u):
                e.wait_ge(a_stat[u % 2], nth(b, u))
                e.wait_ge(a_rstd[u % 2], nth(b, u))
                if due(at := nth(b, u) - 1):
                    e.wait_ge(a_tr[u % 2], at)
                if u >= 2:
                    e.wait_ge(a_store[u - 2], b * 16 + 16)
                else:
                    if due(at := b * 16):
                        e.wait_ge(a_store[u + 2], at)
                v.tensor_scalar(xn[:, u % 2, :], xin[:, u, :], mv[:, u, 0:1], rstd[:, u, :],
                                ALU.subtract, ALU.mult).then_inc(a_xn[u % 2], 1)

            def rope(b, u):
                if due(at := 4 * (nth(b, u) - 1)):
                    e.wait_ge(a_add[u % 2], at)
                for name, w, off, heads, src in (("q", D, 0, H, ps_q), ("k", KV * HD, D, KV, ps_kvg)):
                    e.wait_ge((a_q if name == "q" else a_kvg)[u % 2], nth(b, u))
                    x4 = src[u % 2][:, 0:w].rearrange("p (h d c) -> p h c d", h=heads, c=2)
                    for i, table in enumerate(("cos", "sin")):
                        o4 = rt[:, u % 2, i, off:off + w].rearrange("p (h c d) -> p h c d", h=heads, c=2)
                        tab = const(table)[:, u * 8:u * 8 + 8].unsqueeze(1).unsqueeze(1)
                        v.tensor_tensor(o4, x4, tab.to_broadcast([P, heads, 2, 8]), ALU.mult).then_inc(dve_steps, st.one())
                v.tensor_copy(v_tok[:, b, u, :], ps_kvg[u % 2][:, KV * HD:2 * KV * HD]).then_inc(dve_steps, st.one())
                e.wait_ge(dve_steps, st.count())
                v.tensor_tensor(logit[:, b * TPB + u, :], ps_kvg[u % 2][:, 2 * KV * HD:KVG], bgb, ALU.add)\
                    .then_inc(a_rope[u % 2], 1)

            def ahead(b, u, more, *stages):
                if u + 2 < TPB or more:
                    for stage in stages:
                        stage(b + (u + 2) // TPB, (u + 2) % TPB)

            def sequence(b, more):
                for u in range(TPB):
                    ahead(b, u, more, stat, normalise)
                    rope(b, u)

            for u in range(2):
                stat(0, u)
                normalise(0, u)
            st.close()
            sequence(0, True)
            st.close()
            with e.Fori(1, NB - 1) as b:
                st.enter(b, TPB * (1 + 4 + 1))
                sequence(b, True)
            st.leave(1, NB - 1)
            sequence(NB - 1, False)
            st.close()

        def act_s4_loads(e):
            for dst, src in ((lam_b, lam_d), (left_b[:, 0], ct_d.rearrange("o n c -> (o n) c")), (left_b[:, 1], q_d), (right_b[:, 1], p_d)):
                e.dma_start(dst, src.partition_broadcast(P)).then_inc(s4_load, 16)
            e.dma_start(vct[0:NS], vct_d).then_inc(s4_load, 16)
            e.dma_start(bp_c[0:NS], bp_d).then_inc(s4_load, 16)
            e.dma_start(log_step, step_d.partition_broadcast(P)).then_inc(s4_load, 16)
            e.dma_start(d_c, dd_d.partition_broadcast(P)).then_inc(s4_load, 16)
            e.dma_start(dft, dft_d.rearrange("c (k p) n -> p c k n", p=P)).then_inc(s4_load, 16)

        def dve_s4(e, st):
            v = nc.vector

            def tt(out, a, b, op):
                v.tensor_tensor(out, a, b, op).then_inc(dve_steps, st.one())
                e.wait_ge(dve_steps, st.count())

            e.wait_ge(a_load, 32)
            e.wait_ge(s4_load, 144)
            v.tensor_scalar(bp_w[0:NS, :], ident[0:NS, :], 0.0, bp_c[0:NS, :], ALU.mult, ALU.add).then_inc(s4_bw, 1)
            e.wait_ge(s4_b, 1)
            v.tensor_copy(right_b[:, 0], bank[6][:, 0:2 * NS].rearrange("p (n c) -> p n c", c=2)).then_inc(dve_steps, st.one())
            e.wait_ge(dve_steps, st.count())
            shape = [P, 2, 2, NS]
            lr, li = (left_b[:, :, :, c].unsqueeze(2).to_broadcast(shape) for c in (0, 1))
            rr, ri = (right_b[:, :, :, c].unsqueeze(1).to_broadcast(shape) for c in (0, 1))
            tt(num[:, 0], lr, rr, ALU.mult)
            tt(num_t, li, ri, ALU.mult)
            tt(num[:, 0], num[:, 0], num_t, ALU.add)
            tt(num[:, 1], lr, ri, ALU.mult)
            tt(num_t, li, rr, ALU.mult)
            tt(num[:, 1], num[:, 1], num_t, ALU.subtract)
            tab = const("s4").rearrange("p (c k) -> p c k", c=4)
            shape = [P, KB, NS]
            lam_r, lam_i = (lam_b[:, :, c].unsqueeze(1).to_broadcast(shape) for c in (0, 1))
            h_r, h_i = (tab[:, c].unsqueeze(2).to_broadcast(shape) for c in (2, 3))
            e.wait_ge(s4_step, 1)
            v.tensor_scalar(sq, tab[:, 0], inv_step, None, ALU.mult).then_inc(dve_steps, st.one())
            e.wait_ge(dve_steps, st.count())
            v.tensor_scalar(w_r, tab[:, 1], inv_step, None, ALU.mult).then_inc(dve_steps, st.one())
            e.wait_ge(dve_steps, st.count())
            for den, top, x, y, op in ((den_r, sq, h_r, h_i, ALU.add), (den_i, w_r, h_i, h_r, ALU.subtract)):
                tt(den, lam_r, x, ALU.mult)
                tt(den_a, lam_i, y, ALU.mult)
                tt(den, top.unsqueeze(2).to_broadcast(shape), den, ALU.subtract)
                tt(den, den, den_a, op)
            tt(den_a, den_r, den_r, ALU.mult)
            tt(den_b, den_i, den_i, ALU.mult)
            tt(den_a, den_a, den_b, ALU.add)
            v.reciprocal(den_a, den_a).then_inc(dve_steps, st.one())
            e.wait_ge(dve_steps, st.count())
            tt(den_r, den_r, den_a, ALU.mult)
            tt(den_i, den_i, den_a, ALU.mult)
            shape = [P, KB, 4, NS]
            n_r, n_i = (num[:, c].rearrange("p l r n -> p (l r) n").unsqueeze(1).to_broadcast(shape) for c in (0, 1))
            d_r, d_i = (d.unsqueeze(2).to_broadcast(shape) for d in (den_r, den_i))
            for c, x, y, op in ((0, n_r, n_i, ALU.add), (1, n_i, n_r, ALU.subtract)):
                tt(big[0], x, d_r, ALU.mult)
                tt(big[1], y, d_i, ALU.mult)
                tt(big[2], big[0], big[1], op)
                v.tensor_reduce(sums[:, c], big[2], AX.X, ALU.add).then_inc(dve_steps, st.one())
                e.wait_ge(dve_steps, st.count())
            shape = [P, KB, 2]
            h_r, h_i = (tab[:, c].unsqueeze(2).to_broadcast(shape) for c in (2, 3))
            s_r, s_i = sums[:, 0, :, 2:4], sums[:, 1, :, 2:4]
            tt(hx[:, 0], h_r, s_r, ALU.mult)
            tt(hx[:, 1], h_i, s_i, ALU.mult)
            tt(hx[:, 0], hx[:, 0], hx[:, 1], ALU.subtract)
            tt(hx[:, 1], h_r, s_i, ALU.mult)
            tt(hx[:, 2], h_i, s_r, ALU.mult)
            tt(hx[:, 1], hx[:, 1], hx[:, 2], ALU.add)
            y_r, y_i, x_r, x_i = hx[:, 0, :, 0], hx[:, 1, :, 0], hx[:, 0, :, 1], hx[:, 1, :, 1]
            v.tensor_scalar(x_r, x_r, 1.0, None, ALU.add).then_inc(dve_steps, st.one())
            e.wait_ge(dve_steps, st.count())
            tt(sq, x_r, x_r, ALU.mult)
            tt(w_r, x_i, x_i, ALU.mult)
            tt(sq, sq, w_r, ALU.add)
            v.reciprocal(sq, sq).then_inc(dve_steps, st.one())
            e.wait_ge(dve_steps, st.count())
            t0, t1 = hx[:, 3, :, 0], hx[:, 4, :, 0]
            for w, a, b, op in ((w_r, y_r, y_i, ALU.add), (w_i, y_i, y_r, ALU.subtract)):
                tt(t0, a, x_r, ALU.mult)
                tt(t1, b, x_i, ALU.mult)
                tt(w, t0, t1, op)
                tt(w, w, sq, ALU.mult)
            a_r, a_i = sums[:, 0, :, 1], sums[:, 1, :, 1]
            for c, x, y, op in ((0, w_r, w_i, ALU.subtract), (1, w_i, w_r, ALU.add)):
                tt(t0, a_r, x, ALU.mult)
                tt(t1, a_i, y, ALU.mult)
                tt(t0, t0, t1, op)
                tt(roots[:, c], sums[:, c, :, 0], t0, ALU.subtract)
            v.memset(taps[:, 0:P], 0.0).then_inc(s4_roots, 1)
            st.close()

        def dve_taps(e, st):
            v = nc.vector
            e.wait_ge(s4_taps, 1)
            v.tensor_copy(taps[:, P:P + D], bank[6][:, :]).then_inc(dve_steps, st.one())
            e.wait_ge(dve_steps, st.count())
            v.tensor_tensor(taps[:, P:P + 1], taps[:, P:P + 1], d_c, ALU.add).then_inc(s4_row, 1)
            st.close()

        def pe_s4(e):
            t = nc.tensor
            e.wait_ge(s4_bw, 1)
            t.matmul(bank[6][:, 0:2 * NS], bp_w[0:NS, :], vct[0:NS].rearrange("p n c -> p (n c)"), start=True, stop=True).then_inc(s4_b, 1)

        def pe_taps(e):
            t = nc.tensor
            e.wait_ge(s4_roots, 1)
            for c in range(2):
                for k in range(KB):
                    i = t.matmul(bank[6][:, :], roots[:, c, k:k + 1].to_broadcast([P, P]), dft[:, c, k, :], start=(c + k == 0), stop=(c + k == KB))
            i.then_inc(s4_taps, 1)

        def sp_taps(e):
            e.wait_ge(s4_row, 1)
            e.dma_start(kpad_d, taps).then_inc(s4_out, 16)
            e.wait_ge(s4_out, 16)
            e.dma_start(toep[:, :], bass.AP(kpad_d.tensor, P, [[P + D - 1, P], [1, D]])).then_inc(s4_toep, 16)

        def pool_a(e, st):
            g = nc.gpsimd
            g.memset(zero[:, :], 0).then_inc(pool_steps, st.one())
            e.wait_ge(pool_steps, st.count())
            st.close()
            e.dma_start(slot_d.rearrange("(p m) o -> p (m o)", p=P), zero[:, :]).then_inc(slot_zero, 16)
            e.wait_ge(a_load, 32)

            def inverse_root(b, u):
                e.wait_ge(a_stat[u % 2], nth(b, u))
                g.tensor_tensor(rstd[:, u, :], mv[:, u, 1:2], const("eps"), ALU.add).then_inc(pool_steps, st.one())
                e.wait_ge(pool_steps, st.count())
                g.tensor_tensor(rstd[:, u, :], rstd[:, u, :], const("half"), ALU.pow).then_inc(a_rstd[u % 2], 1)

            def add(b, u):
                e.wait_ge(a_rope[u % 2], nth(b, u))
                alone(e)
                for w, off, heads, dst in ((D, 0, H, q_tok), (KV * HD, D, KV, k_tok)):
                    xc, xs = (rt[:, u % 2, i, off:off + w].rearrange("p (h c d) -> p h c d", h=heads, c=2) for i in (0, 1))
                    o = dst[:, b, u, :].rearrange("p (h c d) -> p h c d", h=heads, c=2)
                    for c, op in ((0, ALU.subtract), (1, ALU.add)):
                        i = g.tensor_tensor(o[:, :, c, :], xc[:, :, c, :], xs[:, :, 1 - c, :], op)
                        i.then_inc(a_add[u % 2], 1)

            def sequence(b, more):
                for u in range(TPB):
                    if u + 2 < TPB or more:
                        inverse_root(b + (u + 2) // TPB, (u + 2) % TPB)
                    add(b, u)

            inverse_root(0, 0)
            inverse_root(0, 1)
            st.close()
            sequence(0, True)
            st.close()
            with e.Fori(1, NB - 1) as b:
                st.enter(b, TPB)
                sequence(b, True)
            st.leave(1, NB - 1)
            sequence(NB - 1, False)
            st.close()

        def act_a(e):
            act_s4_loads(e)
            for x in range(E):
                e.dma_start(w_e[:, x], we_d[x].rearrange("(k p) n -> p k n", p=P)).then_inc(e_load, 16)
            e.wait_ge(s4_load, 144)
            nc.scalar.activation(inv_step, log_step, ACT.Exp, scale=-1.0).then_inc(s4_step, 1)
            def sequence(b):
                for u in range(TPB):
                    e.wait_ge(a_tr[u % 2], nth(b, u))
                    if due(at := nth(b, u) - 1):
                        e.wait_ge(a_kvg[u % 2], at)
                    nc.scalar.copy(xt[:, u % 2, :, :].rearrange("p k t -> p (k t)"), ps_t[u % 2][:, :]).then_inc(a_xt[u % 2], 1)

            sequence(0)
            with e.Fori(1, NB) as b:
                sequence(b)

        def pe_a(e):
            t = nc.tensor
            e.wait_ge(a_load, 32)

            def turn(b, u):
                e.wait_ge(a_xn[u % 2], nth(b, u))
                if due(at := nth(b, u) - 1):
                    e.wait_ge(a_xt[u % 2], at)
                for k in range(KB):
                    i = t.transpose(ps_t[u % 2][:, k * P:(k + 1) * P], xn[:, u % 2, k * P:(k + 1) * P], ident)
                i.then_inc(a_tr[u % 2], 1)

            pe_s4(e)
            e.wait_ge(a_w, 64)

            def sequence(b, more):
                for u in range(TPB):
                    if u + 1 < TPB or more:
                        turn(b + (u + 1) // TPB, (u + 1) % TPB)
                    e.wait_ge(a_xt[u % 2], nth(b, u))
                    if due(at := nth(b, u) - 1):
                        e.wait_ge(a_rope[u % 2], at)
                    for w, out, n, signal in ((wq, ps_q, D, a_q), (wkvg, ps_kvg, KVG, a_kvg)):
                        for k in range(KB):
                            i = t.matmul(out[u % 2][:, 0:n], xt[:, u % 2, k, :], w[:, k, :], start=(k == 0), stop=(k == KB - 1))
                        i.then_inc(signal[u % 2], 1)

            turn(0, 0)
            sequence(0, True)
            with e.Fori(1, NB - 1) as b:
                sequence(b, True)
            sequence(NB - 1, False)

        def dve_route(e, st):
            v = nc.vector

            def tt(out, a, b, op):
                v.tensor_tensor(out, a, b, op).then_inc(dve_steps, st.one())
                e.wait_ge(dve_steps, st.count())

            for u in range(TPB):
                e.wait_ge(a_rope[u % 2], NT // 2)
            e.wait_ge(dve_steps, st.count())
            shape = [P, NT, E, E]
            other = logit.unsqueeze(2).to_broadcast(shape)
            own = logit.unsqueeze(3).to_broadcast(shape)
            above, equal = (x.rearrange("p k v n -> p (k v n)").rearrange("p (t e j) -> p t e j", t=NT, e=E) for x in big[0:2])
            tt(above, other, own, ALU.is_gt)
            tt(equal, other, own, ALU.is_equal)
            lower = const("lower").rearrange("p (e j) -> p e j", e=E).unsqueeze(1).to_broadcast(shape)
            tt(equal, equal, lower, ALU.mult)
            tt(above, above, equal, ALU.add)
            v.tensor_reduce(rank, above, AX.X, ALU.add).then_inc(dve_steps, st.one())
            e.wait_ge(dve_steps, st.count())
            v.tensor_scalar(first, rank, 0.0, None, ALU.is_equal).then_inc(dve_steps, st.one())
            e.wait_ge(dve_steps, st.count())
            v.tensor_scalar(second, rank, 1.0, None, ALU.is_equal).then_inc(dve_steps, st.one())
            e.wait_ge(dve_steps, st.count())
            v.tensor_tensor(chosen_b, first, second, ALU.add).then_inc(r_chosen, 1)
            e.wait_ge(r_count, 1)
            flat = lambda x: x.rearrange("p t e -> p (t e)")
            v.tensor_copy(flat(tot), bank[6][:, P:2 * P]).then_inc(dve_steps, st.one())
            e.wait_ge(dve_steps, st.count())
            a, o = tot, scan_a
            for step in (1, 2, 4, 8):
                v.tensor_copy(o[:, 0:step], a[:, 0:step]).then_inc(dve_steps, st.one())
                tt(o[:, step:], a[:, step:], a[:, 0:NT - step], ALU.add)
                a, o = o, (scan_b if o is scan_a else scan_a)
            incl = a
            tt(flat(pos), flat(incl), bank[6][:, 0:P], ALU.add)
            tt(pos, pos, tot, ALU.subtract)
            n_e = incl[:, NT - 1, :]
            cmp = above.rearrange("p t e j -> p (t e j)")[:, 0:E * NT].rearrange("p (e i) -> p e i", e=E)
            tt(cmp, n_e.unsqueeze(2).to_broadcast([P, E, NT]), const("i128").unsqueeze(1).to_broadcast([P, E, NT]), ALU.is_gt)
            v.tensor_reduce(tiles_of, cmp, AX.X, ALU.add).then_inc(dve_steps, st.one())
            e.wait_ge(dve_steps, st.count())
            a, o = tiles_of, end_a
            for step in (1, 2, 4):
                v.tensor_copy(o[:, 0:step], a[:, 0:step]).then_inc(dve_steps, st.one())
                tt(o[:, step:], a[:, step:], a[:, 0:E - step], ALU.add)
                a, o = o, (end_b if o is end_a else end_a)
            end = a
            tt(o, end, tiles_of, ALU.subtract)
            v.tensor_scalar(o, o, float(P), None, ALU.mult).then_inc(dve_steps, st.one())
            e.wait_ge(dve_steps, st.count())
            tt(pos, pos, o.unsqueeze(1).to_broadcast([P, NT, E]), ALU.add)
            for k, pick in enumerate((first, second)):
                tt(pick, pick, pos, ALU.mult)
                v.tensor_reduce(slot_f, pick, AX.X, ALU.add).then_inc(dve_steps, st.one())
                e.wait_ge(dve_steps, st.count())
                v.tensor_copy(slots[:, k, :], slot_f).then_inc(r_slots, 1)
                e.wait_ge(r_slots, k + 1)
            cmp = above.rearrange("p t e j -> p (t e j)")[:, 0:MT * E].rearrange("p (i e) -> p i e", e=E)
            tt(cmp, end.unsqueeze(1).to_broadcast([P, MT, E]), const("tile").unsqueeze(2).to_broadcast([P, MT, E]), ALU.is_le)
            v.tensor_reduce(eid_f, cmp, AX.X, ALU.add).then_inc(dve_steps, st.one())
            e.wait_ge(dve_steps, st.count())
            v.tensor_scalar(eid_f, eid_f, float(E - 1), None, ALU.min).then_inc(dve_steps, st.one())
            e.wait_ge(dve_steps, st.count())
            v.tensor_copy(eid_i[:, :], eid_f[0:1, :]).then_inc(r_eid, 1)
            st.close()

        def pe_route(e):
            t = nc.tensor
            e.wait_ge(r_chosen, 1)
            rhs = chosen_b.rearrange("p t e -> p (t e)")
            e.wait_ge(s4_row, 1)
            t.matmul(bank[6][:, 0:P], tri_b[:, :], rhs, start=True, stop=True)
            t.matmul(bank[6][:, P:2 * P], ones_b[:, :], rhs, start=True, stop=True).then_inc(r_count, 1)

        def pool_route(e, st):
            e.wait_ge(slot_zero, 16)
            for k in range(TOPK):
                e.wait_ge(r_slots, k + 1)
                for n in range(NT):
                    e.indirect_dma_start(slot_d, bass.IndirectOffsetOnAxis(ap=slots[:, k, n:n + 1], axis=0),
                                         tok_i[:, n:n + 1], None).then_inc(r_scatter, 16)

        def sp_route(e):
            e.wait_ge(r_scatter, 16 * TOPK * NT)
            e.dma_start(slots_i[:, :], slot_d.rearrange("(i p) o -> p (i o)", p=P), allow_slow_non_contiguous=True)\
             .then_inc(r_load, 16)

        qstk = take([P, TPB, R, P], BF16, restart=0)
        mstk = take([P, 2, TPB, R, 32], BF16)
        kstk = take([P, TPB, P], BF16)
        qt = take([P, 2, R, S], BF16)
        kt = take([P, 2, S], BF16)
        pt = take([P, JO[-1] + R * JW[-1]])
        vb = take([P, TPB, KV, VW])
        ot = take([P, KB, TPB, P])
        ot_0 = take([P, TPB, P])
        oe = take([P, S])
        o2 = take([P, TPB, 2 * R * HD])
        xg = take([P, 2, D])
        xgt = take([P, KB, P])
        yo = take([P, 2, D])
        rest = take([P, TPB, R, HD])
        krest = take([P, TPB, HD])
        rmax = take([P, TPB, R])
        rmax_t = take([P, TPB, R])
        rsum = take([P, TPB, R])
        tok_b = take([P, 2, 1], U32)

        b_init = sem("b_init")
        b_wo = sem("b_wo")
        b_v = sem("b_v")
        b_q, b_k = sem("b_q"), sem("b_k")
        b_tq, b_te = sem("b_tq"), sem("b_te")
        b_tm, b_me = sem("b_tm"), sem("b_me")
        b_s1, b_m, b_mx = sem("b_s1"), sem("b_m"), sem("b_mx")
        b_s2, b_e, b_sel, b_pv = sem("b_s2"), sem("b_e"), sem("b_sel"), sem("b_pv")
        b_o, b_ot, b_on, b_o2, b_o2e = sem("b_o"), sem("b_ot"), sem("b_on"), sem("b_o2"), sem("b_o2e")
        b_p, b_s, b_o0 = sem("b_p"), sem("b_s"), sem("b_o0")
        m_idx, m_xt, m_xe, m_y, m_ye = sem("m_idx"), sem("m_xt"), sem("m_xe"), sem("m_y"), sem("m_ye")
        m_x, m_st = sems("m_x", 2), sems("m_st", 2)

        NG = KV
        JOBS1 = [(q, h, n) for q, n in ((3, 1), (2, 1), (1, 2), (0, 4)) for h in range(0, R, n)]
        JOBS2 = [(j, h, n) for j, n in ((0, 1), (1, 1), (2, 2), (3, 4)) for h in range(0, R, n)]
        NJ = len(JOBS1)
        LAST2 = [max(i for i, job in enumerate(JOBS2) if job[0] == j) + 1 for j in range(TPB)]
        tb = bank[5][:, :].bitcast(BF16).rearrange("p (h s) -> p h s", h=2)
        xb = bank[6][:, :].rearrange("p (k t) -> p k t", k=KB)

        def nth_of(per, b, h, k):
            return b * (NG * per) + (h * per + k)

        def next_group(b, h, n):
            return b + (h + n) // NG, (h + n) % NG

        MAIN = {0: 0, 1: 1, 2: 2, 3: 3, 4: 4, 5: 5, 6: 7, 7: 8}
        SECOND = {5: 6, 7: 9}
        NTU, NMU = R // 2 + 1, R // 2

        def phase_a_over(e):
            for u in range(TPB):
                e.wait_ge(a_add[u % 2], 4 * NT // 2)
                e.wait_ge(a_store[u], 16 * NB)
            e.wait_ge(r_eid, 1)
            e.wait_ge(s4_toep, 16)
            e.wait_ge(e_load, 16 * E)

        def pool_b(e, st):
            g = nc.gpsimd
            phase_a_over(e)
            g.memset(kstk[:, :, 112:P], 1.0).then_inc(pool_steps, st.one())
            g.memset(mstk, 0.0).then_inc(pool_steps, st.one())
            g.memset(qstk[:, :, :, 112:P], 0.0).then_inc(pool_steps, st.one())
            g.memset(vb[:, :, :, HD:HD + 1], 1.0).then_inc(pool_steps, st.one())
            g.memset(vb[:, :, :, HD + 1:], 0.0).then_inc(b_init, 1)
            e.wait_ge(pool_steps, st.count())
            e.wait_ge(b_init, 1)
            e.wait_ge(r_load, 16)
            st.close()

            def values(b):
                if due(at := nth_of(4, b, 0, 0)):
                    e.wait_ge(b_pv, at)
                alone(e)
                g.tensor_copy(vb[:, :, :, 0:HD], v_tok[:, b].rearrange("p t (h d) -> p t h d", h=KV)).then_inc(b_v, 1)

            def k_parts(b, h):
                if due(at := nth_of(NTU, b, h, 0)):
                    e.wait_ge(b_tq, at)
                e.wait_ge(pool_steps, st.count())
                alone(e)
                k = k_tok[:, b, :, HD * h:HD * h + HD]
                shape = [P, TPB, 2, HD]

                def twice(a, c):
                    return kstk[:, :, a:c].rearrange("p t (n d) -> p t n d", n=2)

                g.tensor_copy(twice(0, 32), k.unsqueeze(2).to_broadcast(shape)).then_inc(pool_steps, st.one())
                g.tensor_copy(kstk[:, :, 96:112], k).then_inc(pool_steps, st.one())
                e.wait_ge(pool_steps, st.count())
                alone(e)
                g.tensor_tensor(krest, k, kstk[:, :, 0:HD], ALU.subtract).then_inc(pool_steps, st.one())
                e.wait_ge(pool_steps, st.count())
                alone(e)
                g.tensor_copy(twice(32, 64), krest.unsqueeze(2).to_broadcast(shape)).then_inc(pool_steps, st.one())
                e.wait_ge(pool_steps, st.count())
                alone(e)
                g.tensor_tensor(twice(64, 96), krest.unsqueeze(2).to_broadcast(shape), twice(32, 64), ALU.subtract).then_inc(b_k, 1)

            def select(b, h):
                for j in range(TPB):
                    e.wait_ge(b_e, nth_of(NJ, b, h, LAST2[j]))
                    alone(e)
                    diag = pt[:, JO[j]:JO[j] + R * JW[j]].rearrange("p (h q) -> p h q", h=R)[:, :, 0:P]
                    g.affine_select(out=diag, in_=diag, compare_op=ALU.is_ge, fill=0.0, base=0,
                                    pattern=[[0, R], [1, P]], channel_multiplier=-1).then_inc(b_sel, 1)

            def gather(b, m):
                if due(at := b * (8 * MPB) + 16 * (m // 2)):
                    e.wait_ge(m_x[m % 2], at)
                alone(e)
                g.tensor_copy(tok_b[:, m % 2], slots_i[:, bass.ds(b * MPB + m, 1)]).then_inc(m_idx, 1)
                if due(at := b * MPB + (m - 1)):
                    e.wait_ge(m_xt, at)
                e.wait_ge(m_idx, b * MPB + (m + 1))
                alone(e)
                e.indirect_dma_start(xg[:, m % 2, :], None, xn_d, bass.IndirectOffsetOnAxis(ap=tok_b[:, m % 2, :], axis=0))\
                 .then_inc(m_x[m % 2], 16)

            def go(b, more):
                for h in range(NG):
                    if h == 0:
                        values(b)
                    if h + 2 < NG or more:
                        k_parts(*next_group(b, h, 2))
                    select(b, h)
                    for m in (MAIN[h], SECOND.get(h)):
                        if m is not None and (m + 2 < MPB or more):
                            gather(b + (m + 2) // MPB, (m + 2) % MPB)

            k_parts(0, 0)
            gather(0, 0)
            gather(0, 1)
            k_parts(0, 1)
            go(0, True)
            st.close()
            with e.Fori(1, NB - 1) as b:
                st.enter(b, 4 * NG)
                go(b, True)
            st.leave(1, NB - 1)
            go(NB - 1, False)
            st.close()

        def dve_b(e, st):
            v = nc.vector
            phase_a_over(e)
            e.wait_ge(b_init, 1)

            def q_parts(b, h, piece):
                q = q_tok[:, b, :, R * HD * h:R * HD * (h + 1)].rearrange("p t (h d) -> p t h d", h=R)
                high, mid, low = (qstk[:, :, :, a:a + HD] for a in (0, 16, 96))
                if piece == 0:
                    if due(at := nth_of(NTU, b, h, 0)):
                        e.wait_ge(b_tq, at)
                    v.tensor_copy(high, q).then_inc(dve_steps, st.one())
                if piece == 1:
                    e.wait_ge(dve_steps, st.count())
                    v.tensor_tensor(rest, q, high, ALU.subtract).then_inc(dve_steps, st.one())
                if piece == 2:
                    e.wait_ge(dve_steps, st.count())
                    v.tensor_copy(mid, rest).then_inc(dve_steps, st.one())
                if piece == 3:
                    e.wait_ge(dve_steps, st.count())
                    v.tensor_copy(qstk[:, :, :, 32:64], qstk[:, :, :, 0:32]).then_inc(dve_steps, st.one())
                    v.tensor_copy(qstk[:, :, :, 64:96], qstk[:, :, :, 0:32]).then_inc(dve_steps, st.one())
                if piece == 4:
                    v.tensor_tensor(low, rest, mid, ALU.subtract).then_inc(dve_steps, st.one())
                if piece == 5:
                    if due(at := nth_of(NMU, b, h, -NMU)):
                        e.wait_ge(b_tm, at)
                    e.wait_ge(dve_steps, st.count())
                    v.tensor_copy(mstk[:, h % 2, :, :, 0:HD], low).then_inc(b_q, 1)

            def maxima(b, h, n):
                q, r, m = JOBS1[n]
                if n == 0 and due(at := nth_of(1, b, h, 0)):
                    e.wait_ge(b_mx, at)
                e.wait_ge(b_s1, nth_of(NJ, b, h, n + 1))
                w = P * (q + 1)
                v.tensor_reduce(rmax[:, q, r:r + m], bank[(NJ * h + n) % 2][:, 0:m * w].rearrange("p (h k) -> p h k", h=m),
                                AX.X, ALU.max).then_inc(b_m, 1)

            def maxima_parts(b, h):
                e.wait_ge(b_m, nth_of(NJ, b, h, NJ))
                part = [mstk[:, h % 2, :, :, HD + i] for i in range(3)]
                v.tensor_scalar(part[0], rmax, -1.0, None, ALU.mult).then_inc(dve_steps, st.one())
                e.wait_ge(dve_steps, st.count())
                v.scalar_tensor_tensor(out=rmax_t, in0=rmax, scalar=-1.0, in1=part[0], op0=ALU.mult, op1=ALU.subtract).then_inc(dve_steps, st.one())
                e.wait_ge(dve_steps, st.count())
                v.tensor_copy(part[1], rmax_t).then_inc(dve_steps, st.one())
                e.wait_ge(dve_steps, st.count())
                v.tensor_tensor(part[2], rmax_t, part[1], ALU.subtract).then_inc(b_mx, 1)

            def maxima_rows(b, h):
                for i in range(NMU):
                    e.wait_ge(b_tm, nth_of(NMU, b, h, i + 1))
                    v.tensor_copy(qt[96:P, h % 2, 2 * i:2 * i + 2, :], tb[96:P]).then_inc(b_me, 1)

            def normalise(b, h):
                e.wait_ge(b_ot, nth_of(1, b, h, 1))
                o4 = bank[6][:, :].rearrange("p (t r c) -> p t r c", t=TPB, r=R)
                v.reciprocal(rsum, o4[:, :, :, HD]).then_inc(dve_steps, st.one())
                if h % 2 == 0 and due(at := b * (NG // 2) + h // 2):
                    e.wait_ge(b_o2, at)
                e.wait_ge(dve_steps, st.count())
                half = o2[:, :, (h % 2) * R * HD:(h % 2 + 1) * R * HD].rearrange("p t (r d) -> p t r d", r=R)
                v.tensor_tensor(half, o4[:, :, :, 0:HD], rsum.unsqueeze(3).to_broadcast([P, TPB, R, HD]), ALU.mult)\
                    .then_inc(b_on, 1)

            def go(b, more):
                for h in range(NG):
                    for n in range(NJ):
                        if h + 1 < NG or more:
                            maxima(*next_group(b, h, 1), n)
                        if n == 1 and h > 0:
                            normalise(b, h - 1)
                        if n == 1 and h == 0 and due(b):
                            normalise(b - 1, NG - 1)
                        if 2 <= n < 8 and (h + 2 < NG or more):
                            q_parts(*next_group(b, h, 2), n - 2)
                    if h + 1 < NG or more:
                        maxima_parts(*next_group(b, h, 1))
                        maxima_rows(*next_group(b, h, 1))

            for h in range(2):
                for piece in range(6):
                    q_parts(0, h, piece)
            for n in range(NJ):
                maxima(0, 0, n)
            maxima_parts(0, 0)
            maxima_rows(0, 0)
            st.close()
            go(0, True)
            st.close()
            with e.Fori(1, NB - 1) as b:
                st.enter(b, NG * (6 + 3 + 1))
                go(b, True)
            st.leave(1, NB - 1)
            go(NB - 1, False)
            normalise(NB - 1, NG - 1)
            st.close()

        def act_b(e):
            a = nc.scalar
            phase_a_over(e)

            def turned(b, h, i):
                e.wait_ge(b_tq, nth_of(NTU, b, h, i + 1))
                if i == 0 and due(at := nth_of(NJ, b, h, -NJ)):
                    e.wait_ge(b_s2, at)
                if i < NTU - 1:
                    a.copy(qt[:, h % 2, 2 * i:2 * i + 2, :], tb).then_inc(b_te, 1)
                else:
                    a.copy(kt[:, h % 2, :], tb[:, 0, :]).then_inc(b_te, 1)

            def exps(b, h, n):
                j, r, m = JOBS2[n]
                e.wait_ge(b_s2, nth_of(NJ, b, h, n + 1))
                if due(at := nth_of(4, b, h, j - 3)):
                    e.wait_ge(b_pv, at)
                o = pt[:, JO[j] + r * JW[j]:JO[j] + (r + m) * JW[j]]
                a.activation(o, bank[2 + (NJ * h + n) % 2][:, 0:m * JW[j]], ACT.Exp, scale=HD ** -0.5).then_inc(b_e, 1)

            def expert_x(b, m):
                e.wait_ge(m_xt, b * MPB + (m + 1))
                if due(at := b * MPB + m):
                    e.wait_ge(m_y, at)
                a.copy(xgt.rearrange("p k t -> p (k t)"), bank[6][:, :]).then_inc(m_xe, 1)

            def expert_y(b, m):
                e.wait_ge(m_y, b * MPB + (m + 1))
                if due(at := b * (8 * MPB) + 16 * (m // 2)):
                    e.wait_ge(m_st[m % 2], at)
                a.activation(yo[:, m % 2, :], bank[7][:, :], ACT.Relu).then_inc(m_ye, 1)

            def pair_out(b, i):
                e.wait_ge(b_o2, b * (NG // 2) + (i + 1))
                a.copy((ot[:, i] if i else ot_0).rearrange("p t f -> p (t f)"), bank[6][:, :]).then_inc(b_o2e, 1)

            def first_pair(b):
                e.wait_ge(b_o2e, b * (NG // 2) + 1)
                if due(at := b * TPB):
                    e.wait_ge(b_p, at)
                a.copy(ot[:, 0].rearrange("p t f -> p (t f)"), ot_0.rearrange("p t f -> p (t f)")).then_inc(b_o0, 1)

            def projected(b, u, from_bank=7):
                e.wait_ge(b_p, b * TPB + (u + 1))
                e.wait_ge(b_q, nth_of(1, b, NG, 0))
                a.copy(s_tok[:, b, u, :], bank[from_bank][:, :]).then_inc(b_s, 1)

            def output(b, h):
                e.wait_ge(b_pv, nth_of(4, b, h, 4))
                if due(at := nth_of(1, b, h, 0)):
                    e.wait_ge(b_ot, at)
                a.copy(oe, bank[4][:, :]).then_inc(b_o, 1)

            def go(b, more):
                for h in range(NG):
                    second = SECOND.get(h)
                    late = h >= TPB and second is None
                    for n in range(NJ):
                        exps(b, h, n)
                        if n == 2:
                            expert_x(b, MAIN[h])
                    if not late:
                        expert_y(b, MAIN[h])
                    if h == 0 and due(b):
                        pair_out(b - 1, NG // 2 - 1)
                    if h % 2 == 0 and h:
                        pair_out(b, h // 2 - 1)
                    if second is not None:
                        expert_x(b, second)
                    if h + 2 < NG or more:
                        for i in range(NTU):
                            turned(*next_group(b, h, 2), i)
                    output(b, h)
                    if late:
                        expert_y(b, MAIN[h])
                    if h < TPB and due(b):
                        projected(b - 1, h)
                    if h == TPB:
                        first_pair(b)
                    if second is not None:
                        expert_y(b, second)

            for h in range(2):
                for i in range(NTU):
                    turned(0, h, i)
            go(0, True)
            with e.Fori(1, NB - 1) as b:
                go(b, True)
            go(NB - 1, False)
            pair_out(NB - 1, NG // 2 - 1)
            for u in range(TPB):
                projected(NB - 1, u, 7 * (u % 2))

        def pe_b(e):
            t = nc.tensor
            phase_a_over(e)
            e.wait_ge(b_wo, 16)
            e.wait_ge(b_init, 1)

            def turn(b, h, i):
                if i == 0:
                    e.wait_ge(b_q, nth_of(1, b, h, 1))
                if i == NTU - 1:
                    e.wait_ge(b_k, nth_of(1, b, h, 1))
                if i > 0:
                    e.wait_ge(b_te, nth_of(NTU, b, h, i))
                elif h == 1 and not due(b):
                    e.wait_ge(b_te, NTU)
                elif due(at := nth_of(NMU, b, h, -NMU)):
                    e.wait_ge(b_me, at)
                for x in range(2 if i < NTU - 1 else 1):
                    for q in range(TPB):
                        src = qstk[:, q, 2 * i + x, :] if i < NTU - 1 else kstk[:, q, :]
                        j = t.transpose(tb[:, x, q * P:(q + 1) * P], src, ident_b[:, :])
                j.then_inc(b_tq, 1)

            def turn_maxima(b, h, i, last):
                if i == 0:
                    e.wait_ge(b_mx, nth_of(1, b, h, 1))
                    e.wait_ge(b_te, nth_of(NTU, b, h, NTU if last else 2 * NTU))
                if due(at := nth_of(NMU, b, h, i)):
                    e.wait_ge(b_me, at)
                for x in range(2):
                    for q in range(TPB):
                        j = t.transpose(tb[96:P, x, q * P:(q + 1) * P], mstk[:, h % 2, q, 2 * i + x, :], ident_b[:, :])
                j.then_inc(b_tm, 1)

            def scores_1(b, h, n):
                q, r, m = JOBS1[n]
                if n == 0:
                    e.wait_ge(b_te, nth_of(NTU, b, h, NTU))
                if due(at := nth_of(NJ, b, h, n - 1)):
                    e.wait_ge(b_m, at)
                w = P * (q + 1)
                for x in range(m):
                    o = bank[(NJ * h + n) % 2][:, x * w:(x + 1) * w]
                    t.matmul(o, qt[:, h % 2, r + x, q * P:(q + 1) * P], kt[:, h % 2, 0:w], start=True, stop=True)
                    i = t.matmul(o[:, q * P:], ident_b[:, :], mask_b[:, :], start=False, stop=True, skip_group_check=True)
                i.then_inc(b_s1, 1)

            def scores_2(b, h, n):
                j, r, m = JOBS2[n]
                if n == 0:
                    e.wait_ge(b_me, nth_of(NMU, b, h, NMU))
                if due(at := nth_of(NJ, b, h, n - 1)):
                    e.wait_ge(b_e, at)
                for x in range(m):
                    i = t.matmul(bank[2 + (NJ * h + n) % 2][:, x * JW[j]:(x + 1) * JW[j]], kt[:, h % 2, j * P:(j + 1) * P],
                                 qt[:, h % 2, r + x, j * P:], start=True, stop=True)
                i.then_inc(b_s2, 1)

            def values(b, h, j):
                if j == 0:
                    if due(at := nth_of(1, b, h, 0)):
                        e.wait_ge(b_o, at)
                    if h == 0:
                        e.wait_ge(b_v, b + 1)
                e.wait_ge(b_sel, nth_of(4, b, h, j + 1))
                for r in range(R):
                    i = t.matmul(bank[4][VW * r:VW * (r + 1), j * P:], vb[:, j, h, :],
                                 pt[:, JO[j] + r * JW[j]:JO[j] + (r + 1) * JW[j]], start=(j == 0), stop=(j == TPB - 1),
                                 skip_group_check=True)
                i.then_inc(b_pv, 1)

            def turn_out(b, h):
                e.wait_ge(b_o, nth_of(1, b, h, 1))
                if h % 2 == 0 and due(at := b * (NG // 2) + h // 2):
                    e.wait_ge(b_o2e, at)
                e.wait_ge(m_xe, b * MPB + (SECOND.get(h, MAIN[h]) + 1))
                for q in range(TPB):
                    i = t.transpose(xb[:, q, :], oe[:, q * P:(q + 1) * P], ident)
                i.then_inc(b_ot, 1)

            def turn_pair(b, i, m):
                e.wait_ge(b_on, nth_of(1, b, 2 * i, 2))
                e.wait_ge(m_xe, m)
                for q in range(TPB):
                    j = t.transpose(xb[:, q, :], o2[:, q, :], ident)
                j.then_inc(b_o2, 1)

            def expert(b, h, m, step):
                if step == 0:
                    e.wait_ge(m_x[m % 2], b * (8 * MPB) + 16 * (m // 2 + 1))
                    if m == MAIN[h]:
                        if due(at := nth_of(1, b, h, 0)):
                            e.wait_ge(b_on, at)
                    else:
                        e.wait_ge(m_xe, b * MPB + m)
                    for k in range(KB):
                        i = t.transpose(xb[:, k, :], xg[:, m % 2, k * P:(k + 1) * P], ident)
                    i.then_inc(m_xt, 1)
                    return
                if step == 1:
                    ex[0] = e.value_load(eid_i[0:1, bass.ds(b * MPB + m, 1)], min_val=0, max_val=E - 1)
                    if due(at := b * MPB + m):
                        e.wait_ge(m_ye, at)
                    if 0 < h <= TPB and due(b):
                        e.wait_ge(b_s, (b - 1) * TPB + h)
                    t.matmul(bank[7][:, :], sel_e[:, ex[0], :], be3[:, :], start=True, stop=False)
                    e.wait_ge(m_xe, b * MPB + (m + 1))
                k = step - 1
                i = t.matmul(bank[7][:, :], xgt[:, k, :], w_e[:, ex[0], k, :], start=False, stop=(k == KB - 1))
                if k == KB - 1:
                    i.then_inc(m_y, 1)

            def project(b, u, k, m, to_bank=7):
                if k == 0:
                    e.wait_ge(b_o2e, b * (NG // 2) + NG // 2)
                    e.wait_ge(b_o0, b + 1)
                    e.wait_ge(m_ye, m)
                    if u > 0:
                        e.wait_ge(b_s, b * TPB + u)
                i = t.matmul(bank[to_bank][:, :], ot[:, k, u, :], wo[:, k, :], start=(k == 0), stop=(k == KB - 1))
                if k == KB - 1:
                    i.then_inc(b_p, 1)

            ex = [None]

            def go(b, more):
                for h in range(NG):
                    second = SECOND.get(h)
                    late = h >= TPB and second is None

                    def filler(k):
                        if h < TPB and due(b):
                            project(b - 1, h, k, b * MPB + (MAIN[h] + 1))
                        if second is not None:
                            expert(b, h, second, k + 1)
                        if late and k in (1, 2):
                            expert(b, h, MAIN[h], k + 2)

                    def transposes(*units):
                        if h + 2 < NG or more:
                            for i in units:
                                turn(*next_group(b, h, 2), i)

                    def maxima(i):
                        if h + 1 < NG or more:
                            turn_maxima(*next_group(b, h, 1), i, not (h + 2 < NG or more))

                    for n in range(NJ):
                        if h + 1 < NG or more:
                            scores_1(*next_group(b, h, 1), n)
                        scores_2(b, h, n)
                        if n == 2:
                            expert(b, h, MAIN[h], 0)
                        elif late and n in (5, 9):
                            expert(b, h, MAIN[h], 1 if n == 5 else 2)
                        elif not late and n in (4, 6, 8, 10):
                            expert(b, h, MAIN[h], n // 2 - 1)
                    if h == 0 and due(b):
                        turn_pair(b - 1, NG // 2 - 1, b * MPB + (MAIN[h] + 1))
                    if h % 2 == 0 and h:
                        turn_pair(b, h // 2 - 1, b * MPB + (MAIN[h] + 1))
                    if second is not None:
                        expert(b, h, second, 0)
                    transposes(0)
                    values(b, h, 0)
                    filler(0)
                    transposes(1)
                    values(b, h, 1)
                    values(b, h, 2)
                    transposes(2)
                    filler(1)
                    values(b, h, 3)
                    maxima(0)
                    filler(2)
                    maxima(1)
                    filler(3)
                    turn_out(b, h)

            for h in range(2):
                for i in range(NTU):
                    turn(0, h, i)
            for n in range(NJ):
                scores_1(0, 0, n)
            for i in range(NMU):
                turn_maxima(0, 0, i, False)
            go(0, True)
            with e.Fori(1, NB - 1) as b:
                go(b, True)
            go(NB - 1, False)
            turn_pair(NB - 1, NG // 2 - 1, NB * MPB)
            for u in range(TPB):
                for k in range(KB):
                    project(NB - 1, u, k, NB * MPB, 7 * (u % 2))

        def sp_b(e):
            for u in range(TPB):
                e.wait_ge(a_kvg[u % 2], NT // 2)
            e.dma_start(wo, wo_d.rearrange("(k p) n -> p k n", p=P)).then_inc(b_wo, 16)

            def go(b):
                for m in range(MPB):
                    e.wait_ge(m_ye, b * MPB + (m + 1))
                    e.dma_start(y_t[b * MPB + m], yo[:, m % 2, :]).then_inc(m_st[m % 2], 16)

            go(0)
            with e.Fori(1, NB) as b:
                go(b)

        w_lin = w_e[:, 0]
        c_x = take([P, TPB, D], restart=0)
        c_y = take([P, TPB, TOPK, D])
        c_xn = take([P, 2, D])
        c_xt = take([P, 2, KB, P])
        c_g = take([P, 2, D])
        c_o = take([P, 2, D])
        c_st = take([P, TPB, 8])
        c_mv = take([P, TPB, 2])
        c_rstd = take([P, TPB, 1])
        c_bias = take([P, D])
        c_scale = take([P, KB, KB])
        c_slot = take([P, TPB, TOPK, 1], U32)
        c_w, c_ws = sem("c_w"), sem("c_ws")
        c_ld, c_ga = sems("c_ld", TPB), sems("c_ga", TPB)
        c_idx = sem("c_idx")
        c_z, c_gate, c_x1, c_stat, c_r, c_n = (sems(n, 2) for n in ("c_z", "c_gate", "c_x1", "c_stat", "c_r", "c_n"))
        c_tr, c_te, c_lin, c_conv, c_pre, c_sil, c_prod, c_done = (
            sems(n, 2) for n in ("c_tr", "c_te", "c_lin", "c_conv", "c_pre", "c_sil", "c_prod", "c_done"))
        c_out = sems("c_out", TPB)

        def phase_b_over(e):
            e.wait_ge(b_s, NB * TPB)
            for par in range(2):
                e.wait_ge(m_st[par], 16 * NB * MPB // 2)

        def sp_c(e):
            phase_b_over(e)
            e.dma_start(w_lin, wft_d.rearrange("(k p) n -> p k n", p=P)).then_inc(c_w, 16)
            e.dma_start(c_bias, bf_d.partition_broadcast(P)).then_inc(c_w, 16)
            e.dma_start(c_scale, sc_d.partition_broadcast(P)).then_inc(c_w, 16)
            for u in range(TPB):
                e.dma_start(c_x[:, u, :], x_t[u]).then_inc(c_ld[u], 16)

            def go(b, more):
                for u in range(TPB):
                    e.wait_ge(c_done[u % 2], nth(b, u))
                    e.dma_start(out_t[b * TPB + u], c_o[:, u % 2, :]).then_inc(c_out[u], 16)
                    if more:
                        e.dma_start(c_x[:, u, :], x_t[(b + 1) * TPB + u]).then_inc(c_ld[u], 16)

            go(0, True)
            with e.Fori(1, NB - 1) as b:
                go(b, True)
            go(NB - 1, False)
            for u in range(TPB):
                e.wait_ge(c_out[u], 16 * NB)

        def pool_c(e, st):
            g = nc.gpsimd
            phase_b_over(e)

            def rows(b, u):
                if due(at := 32 * b):
                    e.wait_ge(c_ga[u], at)
                alone(e)
                g.tensor_copy(c_slot[:, u], slots[:, :, bass.ds(b * TPB + u, 1)]).then_inc(c_idx, 1)
                e.wait_ge(c_idx, b * TPB + u + 1)
                if due(at := nth(b, u) - 2):
                    e.wait_ge(c_x1[u % 2], at)
                alone(e)
                for k in range(TOPK):
                    e.indirect_dma_start(c_y[:, u, k, :], None, y_d, bass.IndirectOffsetOnAxis(ap=c_slot[:, u, k, :], axis=0))\
                     .then_inc(c_ga[u], 16)

            def root(b, u):
                e.wait_ge(c_stat[u % 2], nth(b, u))
                g.tensor_tensor(c_rstd[:, u, :], c_mv[:, u, 1:2], const("eps"), ALU.add).then_inc(pool_steps, st.one())
                e.wait_ge(pool_steps, st.count())
                g.tensor_tensor(c_rstd[:, u, :], c_rstd[:, u, :], const("half"), ALU.pow).then_inc(c_r[u % 2], 1)

            def total(b, u):
                e.wait_ge(c_prod[u % 2], nth(b, u))
                alone(e)
                g.tensor_tensor(c_o[:, u % 2, :], c_o[:, u % 2, :], s_tok[:, b, u, :], ALU.add).then_inc(c_done[u % 2], 1)

            def go(b, more):
                for u in range(TPB):
                    if more:
                        rows(b + 1, u)
                    if u + 2 < TPB or more:
                        root(b + (u + 2) // TPB, (u + 2) % TPB)
                    total(b, u)

            for u in range(TPB):
                rows(0, u)
            root(0, 0)
            root(0, 1)
            st.close()
            go(0, True)
            st.close()
            with e.Fori(1, NB - 1) as b:
                st.enter(b, TPB)
                go(b, True)
            st.leave(1, NB - 1)
            go(NB - 1, False)
            st.close()

        def dve_c(e, st):
            v = nc.vector
            phase_b_over(e)
            e.wait_ge(c_w, 48)
            w4 = w_lin.rearrange("p k (o c) -> p k o c", o=KB)
            sc4 = c_scale.rearrange("p o k -> p k o").unsqueeze(3)
            for k in range(KB):
                i = v.tensor_tensor(w4[:, k], w4[:, k], sc4[:, k].to_broadcast([P, KB, P]), ALU.mult)
                i.then_inc(c_ws, 1)

            def experts(b, u):
                e.wait_ge(c_ga[u], b * 32 + 32)
                v.tensor_tensor(c_y[:, u, 0, :], c_y[:, u, 0, :], c_y[:, u, 1, :], ALU.add).then_inc(c_z[u % 2], 1)

            def front(b, u):
                e.wait_ge(c_gate[u % 2], nth(b, u))
                v.tensor_tensor(s_tok[:, b, u, :], s_tok[:, b, u, :], c_y[:, u, 1, :], ALU.mult).then_inc(dve_steps, st.one())
                e.wait_ge(c_ld[u], b * 16 + 16)
                e.wait_ge(dve_steps, st.count())
                v.tensor_tensor(s_tok[:, b, u, :], s_tok[:, b, u, :], c_x[:, u, :], ALU.add).then_inc(c_x1[u % 2], 1)
                e.wait_ge(c_x1[u % 2], nth(b, u))
                alone(e)
                v.bn_stats(c_st[:, u, 0:6], s_tok[:, b, u, :]).then_inc(dve_steps, st.one())
                e.wait_ge(dve_steps, st.count())
                alone(e)
                v.bn_aggr(c_mv[:, u, :], c_st[:, u, 0:6]).then_inc(c_stat[u % 2], 1)

            def norm(b, u):
                e.wait_ge(c_stat[u % 2], nth(b, u))
                if due(at := nth(b, u) - 1):
                    e.wait_ge(c_tr[u % 2], at)
                e.wait_ge(c_r[u % 2], nth(b, u))
                v.tensor_scalar(c_xn[:, u % 2, :], s_tok[:, b, u, :], c_mv[:, u, 0:1], c_rstd[:, u, :],
                                ALU.subtract, ALU.mult).then_inc(c_n[u % 2], 1)

            def bias(b, u):
                e.wait_ge(c_lin[u % 2], nth(b, u))
                if due(at := nth(b, u) - 1):
                    e.wait_ge(c_prod[u % 2], at)
                v.tensor_tensor(c_g[:, u % 2, :], bank[2 + u % 2][:, :], c_bias, ALU.add).then_inc(c_pre[u % 2], 1)

            def product(b, u):
                e.wait_ge(c_conv[u % 2], nth(b, u))
                e.wait_ge(c_sil[u % 2], nth(b, u))
                if u >= 2:
                    e.wait_ge(c_out[u - 2], 16 * b + 16)
                elif due(at := 16 * b):
                    e.wait_ge(c_out[u + 2], at)
                v.tensor_tensor(c_o[:, u % 2, :], bank[4 + u % 2][:, :], c_g[:, u % 2, :], ALU.mult).then_inc(c_prod[u % 2], 1)

            def go(b, more):
                for u in range(TPB):
                    if u + 3 < TPB or more:
                        experts(b + (u + 3) // TPB, (u + 3) % TPB)
                    if u + 2 < TPB or more:
                        front(b + (u + 2) // TPB, (u + 2) % TPB)
                    bias(b, u)
                    if u + 2 < TPB or more:
                        norm(b + (u + 2) // TPB, (u + 2) % TPB)
                    product(b, u)

            for u in range(3):
                experts(0, u)
            for u in range(2):
                front(0, u)
                norm(0, u)
            st.close()
            go(0, True)
            st.close()
            with e.Fori(1, NB - 1) as b:
                st.enter(b, TPB * 2)
                go(b, True)
            st.leave(1, NB - 1)
            go(NB - 1, False)
            st.close()

        def act_c(e):
            a = nc.scalar
            phase_b_over(e)

            def gate(b, u):
                e.wait_ge(c_z[u % 2], nth(b, u))
                a.activation(c_y[:, u, 1, :], c_y[:, u, 0, :], ACT.Silu, scale=1.0 / TOPK).then_inc(c_gate[u % 2], 1)

            def go(b, more):
                for u in range(TPB):
                    if u + 3 < TPB or more:
                        gate(b + (u + 3) // TPB, (u + 3) % TPB)
                    if u + 1 < TPB or more:
                        lift(b + (u + 1) // TPB, (u + 1) % TPB)
                    e.wait_ge(c_pre[u % 2], nth(b, u))
                    a.activation(c_g[:, u % 2, :], c_g[:, u % 2, :], ACT.Silu).then_inc(c_sil[u % 2], 1)

            def lift(b, u):
                e.wait_ge(c_tr[u % 2], nth(b, u))
                if due(at := nth(b, u) - 1):
                    e.wait_ge(c_conv[u % 2], at)
                a.copy(c_xt[:, u % 2].rearrange("p k t -> p (k t)"), bank[u % 2][:, :]).then_inc(c_te[u % 2], 1)

            for u in range(3):
                gate(0, u)
            lift(0, 0)
            go(0, True)
            with e.Fori(1, NB - 1) as b:
                go(b, True)
            go(NB - 1, False)

        def pe_c(e):
            t = nc.tensor
            phase_b_over(e)
            e.wait_ge(c_ws, KB)

            def turn(b, u):
                e.wait_ge(c_n[u % 2], nth(b, u))
                if due(at := nth(b, u) - 1):
                    e.wait_ge(c_te[u % 2], at)
                for k in range(KB):
                    i = t.transpose(bank[u % 2][:, k * P:(k + 1) * P], c_xn[:, u % 2, k * P:(k + 1) * P], ident)
                i.then_inc(c_tr[u % 2], 1)

            def work(b, u):
                e.wait_ge(c_te[u % 2], nth(b, u))
                if due(at := nth(b, u) - 1):
                    e.wait_ge(c_prod[u % 2], at)
                for k in range(KB):
                    i = t.matmul(bank[2 + u % 2][:, :], c_xt[:, u % 2, k, :], w_lin[:, k, :], start=(k == 0), stop=(k == KB - 1))
                i.then_inc(c_lin[u % 2], 1)
                for k in range(KB):
                    i = t.matmul(bank[4 + u % 2][:, k * P:], c_xt[:, u % 2, k, :], toep[:, 0:D - k * P],
                                 start=(k == 0), stop=(k == KB - 1), skip_group_check=True)
                i.then_inc(c_conv[u % 2], 1)

            def go(b, more):
                for u in range(TPB):
                    if u + 1 < TPB or more:
                        turn(b + (u + 1) // TPB, (u + 1) % TPB)
                    work(b, u)

            turn(0, 0)
            go(0, True)
            with e.Fori(1, NB - 1) as b:
                go(b, True)
            go(NB - 1, False)

        @block.sync
        def _(e):
            sp_a(e)
            sp_taps(e)
            sp_route(e)
            sp_b(e)
            sp_c(e)

        @block.vector
        def _(e):
            st = Steps()
            dve_s4(e, st)
            dve_a(e, st)
            dve_taps(e, st)
            dve_route(e, st)
            dve_b(e, st)
            dve_c(e, st)

        @block.gpsimd
        def _(e):
            st = Steps()
            pool_a(e, st)
            pool_route(e, st)
            pool_b(e, st)
            pool_c(e, st)

        @block.scalar
        def _(e):
            act_a(e)
            act_b(e)
            act_c(e)

        @block.tensor
        def _(e):
            pe_a(e)
            pe_taps(e)
            pe_route(e)
            pe_b(e)
            pe_c(e)


_INS = ["L0_attn_x", "L0_attn_wq", "L0_attn_wk", "L0_attn_wv", "L0_attn_wo", "L0_ffn_W_gate", "L0_ffn_b_gate",
        "L0_ffn_W_e", "L0_ffn_b_e", "L1_attn_Lambda_ri", "L1_attn_p_ri", "L1_attn_q_ri", "L1_attn_Vc_ri",
        "L1_attn_Ct_ri", "L1_attn_Bp", "L1_attn_D", "L1_attn_log_step", "L1_ffn_weight",
        "L1_ffn_weight_scale_inv", "L1_ffn_bias"]
_TURNED = {"L1_attn_Vc_ri": (1, 0, 2), "L1_ffn_weight": (1, 0)}


def kernel(**inputs):
    import concourse.bacc as bacc
    from concourse.bass_utils import run_bass_kernel_spmd

    nc = bacc.Bacc("TRN2", target_bir_lowering=False, num_devices=1)
    given = [(n, np.ascontiguousarray(np.asarray(inputs[n]).transpose(_TURNED[n]) if n in _TURNED else inputs[n])) for n in _INS]
    given += list(zip(("constants", "dft"), constants()))
    arrays = {f"in_{n}": a for n, a in given}
    args = [nc.dram_tensor(f"in_{n}", a.shape, mybir.dt.from_np(a.dtype), kind="ExternalInput").ap() for n, a in given]
    out = nc.dram_tensor("out", (NB, S, D), F32, kind="ExternalOutput").ap()
    build(nc, *args, out)
    return run_bass_kernel_spmd(nc, [arrays], core_ids=[0]).results[0]["out"]
```

```python
from contextlib import ExitStack

import numpy as np

import concourse.bass as bass
from concourse import mybir
from concourse.alu_op_type import AluOpType as ALU

ACT = mybir.ActivationFunctionType
AX = mybir.AxisListType
F32 = mybir.dt.float32
BF16 = mybir.dt.bfloat16
U32 = mybir.dt.uint32
F32R = mybir.dt.float32r
I32 = mybir.dt.int32

P = 128
NB, S, D = 4, 512, 512
KB = D // P
TPB = S // P
NT = NB * TPB
H, HD, KV = 32, 16, 8
R = H // KV
E, TOPK = 8, 2
NS = 64
MT = NT * TOPK + E
MPB = MT // NB
EPS = 1e-5
NEG = -1.0e30
VW = 32
KVG = 2 * KV * HD + E
JW = [S - P * j for j in range(TPB)]
JO = [R * sum(JW[:j]) for j in range(TPB)]

COLS = {}
_at = 0
for _name, _n in (("ident", P), ("mask", P), ("tri", P), ("cos", TPB * 8), ("sin", TPB * 8), ("s4", 16),
                  ("lower", E * E), ("i128", NT), ("i128m", MT + 1), ("tile", MT), ("iota", P), ("tilenum", TOPK * NT), ("part", 1), ("half", 1), ("eps", 1), ("minus", 1), ("sel", E)):
    COLS[_name] = (_at, _at + _n)
    _at += _n
NCONST = _at


def constants():
    c = np.zeros((P, NCONST), np.float32)

    def put(name, a):
        c[:, COLS[name][0]:COLS[name][1]] = np.asarray(a, np.float32).reshape(-1, COLS[name][1] - COLS[name][0])

    p = np.arange(P)
    put("ident", np.eye(P))
    put("mask", np.where(p[None, :] > p[:, None], NEG, 0.0))
    put("tri", p[:, None] < p[None, :])
    freq = (np.float32(1.0) / np.float32(10000.0) ** (np.arange(0, HD, 2, dtype=np.float32) / np.float32(HD))).astype(np.float32)
    angle = (np.arange(S, dtype=np.float32)[:, None] * freq[None, :]).astype(np.float32).astype(np.float64)
    put("cos", np.cos(angle).reshape(TPB, P, 8).transpose(1, 0, 2).reshape(P, -1))
    put("sin", np.sin(angle).reshape(TPB, P, 8).transpose(1, 0, 2).reshape(P, -1))
    theta = 2 * np.pi * np.arange(D) / D
    s4 = np.stack([1 - np.cos(theta), np.sin(theta), (1 + np.cos(theta)) / 2, -np.sin(theta) / 2])
    put("s4", s4.reshape(4, KB, P).transpose(2, 0, 1).reshape(P, -1))
    put("lower", (np.arange(E)[None, :] < np.arange(E)[:, None]).reshape(1, -1))
    put("i128", P * np.arange(NT)[None, :])
    put("tile", np.arange(MT)[None, :])
    put("i128m", P * np.arange(MT + 1)[None, :])
    put("iota", p[None, :])
    put("tilenum", np.arange(TOPK * NT)[None, :] % NT)
    put("part", p)
    put("half", -0.5)
    put("eps", EPS)
    put("minus", -1.0)
    put("sel", np.arange(E)[None, :] == p[:, None] % 32)
    ang = 2 * np.pi * ((np.arange(D)[:, None] * np.arange(D)[None, :]) % D) / D
    dft = np.stack([np.cos(ang), -np.sin(ang)]) / D
    return c, dft.astype(np.float32)


def due(n):
    return not isinstance(n, int) or n > 0


def nth(b, u):
    return b * (TPB // 2) + u // 2 + 1


def alone(e):
    e.nop(nofuse=True)


def aligned(address):
    return (address + 31) // 32 * 32


class Steps:

    def __init__(self):
        self.base, self.k, self.loop, self.per, self.start = 0, 0, None, 0, 0

    def one(self):
        self.k += 1
        return 1

    def count(self):
        n = self.base + self.k
        assert n > 0
        return n if self.loop is None else (self.loop - self.start) * self.per + n

    def enter(self, loop, per, start=1):
        self.close()
        self.loop, self.per, self.start = loop, per, start

    def leave(self, start, end):
        assert self.k == self.per, (self.k, self.per)
        self.base += self.per * (end - start)
        self.loop, self.k = None, 0

    def close(self):
        self.base += self.k
        self.k = 0


def build(nc, x_d, wq_d, wk_d, wv_d, wo_d, wg_d, bg_d, we_d, be_d, lam_d, p_d, q_d, vct_d, ct_d, bp_d, dd_d,
          step_d, wft_d, sc_d, bf_d, const_d, dft_d, out_d):
    ctx = ExitStack()
    with ctx:
        def sb(name, shape, dt=F32):
            return ctx.enter_context(nc.sbuf_tensor(name, shape, dt))

        def ps(name, shape, dt=F32):
            return ctx.enter_context(nc.psum_tensor(name, shape, dt))

        def sem(name):
            return ctx.enter_context(nc.semaphore(name))

        def sems(name, n):
            return [sem(f"{name}{i}") for i in range(n)]

        xn_d = nc.dram_tensor("xn_rows", [NT * P, D], F32).ap()
        y_d = nc.dram_tensor("expert_rows", [MT * P, D], F32).ap()
        kpad_d = nc.dram_tensor("s4_taps_rows", [P, P + D], F32).ap()

        x_t = x_d.rearrange("b (t p) d -> (b t) p d", p=P)
        out_t = out_d.rearrange("b (t p) d -> (b t) p d", p=P)
        xn_t = xn_d.rearrange("(n p) d -> n p d", p=P)
        y_t = y_d.rearrange("(n p) d -> n p d", p=P)

        cst = sb("cst", [P, NCONST])

        def const(name):
            return cst[:, COLS[name][0]:COLS[name][1]]

        ident = const("ident")
        ident_b = sb("ident_b", [P, P], BF16)
        mask_b = sb("mask_b", [P, P], BF16)
        tri_b = sb("tri_b", [P, P], BF16)
        ones_b = sb("ones_b", [P, P], BF16)
        starts = {"w_e": aligned(nc.sbuf_base)}
        w_e = sb("w_e", [P, E, KB, D])
        starts["w_proj"] = aligned(nc.sbuf_base)
        w_proj = sb("w_proj", [P, KB * (D + KVG)])
        wq = w_proj[:, 0:KB * D].rearrange("p (k n) -> p k n", k=KB)
        wkvg = w_proj[:, KB * D:].rearrange("p (k n) -> p k n", k=KB)
        wo = wq
        q_tok = sb("q_tok", [P, NB, TPB, D])
        s_tok = q_tok
        k_tok = sb("k_tok", [P, NB, TPB, KV * HD])
        v_tok = sb("v_tok", [P, NB, TPB, KV * HD])
        starts["toep"] = aligned(nc.sbuf_base)
        toep = sb("toep", [P, D])
        iota_b = sb("iota_b", [P, P], BF16)
        number_b = sb("number_b", [P, TOPK * NT], BF16)
        d_c = sb("d_c", [P, 1])[:, :]
        roots = sb("roots", [P, 2, KB])
        slots = sb("slots", [P, TOPK, NT], U32)
        slots_i = sb("slots_i", [P, MT], U32)
        eid_i = sb("eid_i", [1, MT], I32)
        be3 = sb("be3", [P, D], BF16)
        sel_e = sb("sel_e", [P, E, P], BF16)
        inv_step = sb("inv_step", [P, 1])[:, :]
        NAR = 18728
        starts["arena"] = aligned(nc.sbuf_base)
        arena = sb("arena", [P, NAR])
        used = [0]

        def take(shape, dt=F32, restart=None):
            if restart is not None:
                used[0] = restart
            n = int(np.prod(shape[1:]))
            words = n if dt in (F32, U32, I32) else (n + 1) // 2
            a = arena[:, used[0]:used[0] + words]
            used[0] += words
            assert used[0] <= NAR, used[0]
            if dt != F32:
                a = a.bitcast(dt)
            names = "abcdef"[:len(shape) - 1]
            if len(shape) > 2:
                a = a.rearrange(f"p ({' '.join(names)}) -> p {' '.join(names)}",
                                **{m: k for m, k in zip(names, shape[1:])})
            return a

        bank = [ps(f"bank{i}", [P, D]) for i in range(8)]

        def parts(name, shape, space, word):
            return nc.alloc_sbuf_tensor_at(name, shape, F32R, offset=starts[space] + 4 * word)

        a_load = sem("a_load")
        a_wq, a_w = sem("a_wq"), sem("a_w")
        a_x = sems("a_x", TPB)
        a_stat = sems("a_stat", 2)
        a_rstd = sems("a_rstd", 2)
        a_xn = sems("a_xn", 2)
        a_store = sems("a_store", TPB)
        a_tr = sems("a_tr", 2)
        a_xt = sems("a_xt", 2)
        a_xl = sems("a_xl", 2)
        a_high, a_low = sem("a_high"), sem("a_low")
        a_q = sems("a_q", 2)
        a_kvg = sems("a_kvg", 2)
        a_rope = sems("a_rope", 2)
        a_add = sems("a_add", 2)
        dve_steps, pool_steps = sem("dve_steps"), sem("pool_steps")

        xin = take([P, TPB, D], restart=0)
        xn = take([P, 2, D])
        xh = parts("xh", [P, 2, KB, P], "arena", used[0])
        take([P, 2, KB, P])
        proj_high, proj_low = (parts(name, [P, KB * (D + KVG)], space, word)
                               for name, space, word in (("proj_high", "w_e", (E - E // NB) * KB * D), ("proj_low", "w_proj", 0)))
        assert D + KVG <= E // NB * D
        cut = KB * D
        wq_parts, wkvg_parts = ([w[:, span].rearrange("p (k n) -> p k n", k=KB) for w in (proj_high, proj_low)]
                                for span in (slice(0, cut), slice(cut, None)))
        rt = take([P, 2, 2, D + KV * HD])
        stats = take([P, TPB, 8])
        mv = take([P, TPB, 2])
        rstd = take([P, TPB, 1])
        shift = take([P, TPB, 1])
        bgb = take([P, E])
        logit = take([P, NT, E])
        be_f = take([P, D])
        e_load = sem("e_load")
        be_load = sem("be_load")
        ps_t, ps_q, ps_kvg = bank[0:2], bank[2:4], bank[4:6]

        left_b = take([P, 2, NS, 2])
        right_b = take([P, 2, NS, 2])
        vct = take([P, NS, 2])
        bp_c = take([P, 1])
        bp_w = take([P, P])
        log_step = take([P, 1])
        num_t = take([P, 2, 2, NS])
        above, equal = take([P, TPB, E, E]), take([P, TPB, E, E])
        rank = take([P, TPB, E])
        s4_load = sem("s4_load")
        s4_b = sem("s4_b")
        s4_bw = sem("s4_bw")
        s4_step = sem("s4_step")
        s4_roots = sem("s4_roots")
        s4_taps = sem("s4_taps")
        s4_row = sem("s4_row")
        s4_out = sem("s4_out")
        s4_toep = sem("s4_toep")

        RB_AT = 10496 + S + TPB * 2 * R * HD
        assert used[0] <= RB_AT - 2 * D
        xl = parts("xl", [P, 2, KB, P], "arena", RB_AT - 2 * D)
        first, second, tot, scan_a, scan_b, pos = (take([P, NT, E], restart=None if n else RB_AT) for n in range(6))
        chosen_b = take([P, NT, E], BF16)
        tiles_of, end_a, end_b = (take([P, E]) for _ in range(3))
        slot_f = take([P, TOPK, NT])
        slot_q = take([P, TOPK, NT])
        slot_p = take([P, TOPK, NT], BF16)
        eid_f = take([P, MT])
        compared = arena[:, RB_AT + 2 * NT * E:RB_AT + 2 * NT * E + MT * E]
        reached = take([P, TOPK * NT, MT + 2], BF16)[:, :, 0:MT + 1]
        of_tile = take([P, TOPK * NT, 2, MT], BF16)
        of_place = take([P, TOPK * NT, P], BF16)
        assert used[0] <= 16640, used[0]
        r_chosen = sem("r_chosen")
        r_count = sem("r_count")
        r_slots = sem("r_slots")
        r_eid = sem("r_eid")
        r_tile = sem("r_tile")
        r_place = sem("r_place")
        r_back = sem("r_back")
        r_tokens = sem("r_tokens")

        block = ctx.enter_context(nc.Block())

        def sp_a(e):
            e.dma_start(cst[:, :], const_d).then_inc(a_load, 16)
            e.dma_start(bgb, bg_d.partition_broadcast(P)).then_inc(a_load, 16)
            for u in range(2):
                e.dma_start(xin[:, u, :], x_t[u]).then_inc(a_x[u], 16)
            e.dma_start(wq, wq_d.rearrange("(k p) n -> p k n", p=P)).then_inc(a_wq, 16)
            e.dma_start(wkvg[:, :, 0:KV * HD], wk_d.rearrange("(k p) n -> p k n", p=P)).then_inc(a_w, 16)
            e.dma_start(wkvg[:, :, KV * HD:2 * KV * HD], wv_d.rearrange("(k p) n -> p k n", p=P)).then_inc(a_w, 16)
            e.dma_start(wkvg[:, :, 2 * KV * HD:], wg_d.rearrange("(k p) n -> p k n", p=P)).then_inc(a_w, 16)
            for u in range(2, TPB):
                e.dma_start(xin[:, u, :], x_t[u]).then_inc(a_x[u], 16)
            for part in range(3):
                e.dma_start(be_f[32 * part:32 * part + E, :], be_d).then_inc(be_load, 16)

            def store_and_load(b, more):
                for u in range(TPB):
                    e.wait_ge(a_xn[u % 2], nth(b, u))
                    e.dma_start(xn_t[b * TPB + u], xn[:, u % 2, :]).then_inc(a_store[u], 16)
                    if more:
                        e.dma_start(xin[:, u, :], x_t[(b + 1) * TPB + u]).then_inc(a_x[u], 16)

            store_and_load(0, True)
            with e.Fori(1, NB - 1) as b:
                store_and_load(b, True)
            store_and_load(NB - 1, False)

        def dve_a(e, st):
            v = nc.vector
            e.wait_ge(a_load, 32)

            def prepare(b, u):
                if (b, u) == (0, 2):
                    e.wait_ge(s4_load, 128)
                    v.tensor_scalar(bp_w[0:NS, :], ident[0:NS, :], 0.0, bp_c[0:NS, :], ALU.mult, ALU.add).then_inc(s4_bw, 1)
                if (b, u) == (0, 1):
                    v.tensor_copy(ident_b[:, :], ident).then_inc(dve_steps, st.one())
                    v.tensor_copy(mask_b[:, :], const("mask")).then_inc(dve_steps, st.one())
                    v.tensor_copy(tri_b[:, :], const("tri")).then_inc(dve_steps, st.one())
                    v.memset(ones_b[:, :], 1.0).then_inc(dve_steps, st.one())
                    v.memset(be3[:, :], 0.0).then_inc(dve_steps, st.one())
                if (b, u) == (0, 3):
                    v.tensor_copy(iota_b[:, :], const("iota")).then_inc(dve_steps, st.one())
                    v.tensor_copy(number_b[:, :], const("tilenum")).then_inc(dve_steps, st.one())
                if (b, u) == (0, 2):
                    v.tensor_copy(sel_e[:, :, :], const("sel").unsqueeze(2).to_broadcast([P, E, P])).then_inc(dve_steps, st.one())
                if (b, u) == (NB - 1, 0):
                    e.wait_ge(s4_b, 1)
                    v.tensor_copy(right_b[:, 0], bank[6][:, 0:2 * NS].rearrange("p (n c) -> p n c", c=2)).then_inc(dve_steps, st.one())
                if b == NB - 1 and u < 2:
                    bias_parts((2,) if u else (0, 1))
                if b == NB - 1 and u >= 2:
                    numerators(u - 2)

            def bias_parts(parts):
                e.wait_ge(be_load, 48)
                e.wait_ge(dve_steps, st.count())
                for part in parts:
                    rows = slice(32 * part, 32 * part + E)
                    for cut in range(part + 1):
                        v.tensor_copy(be3[rows, :], be_f[rows, :]).then_inc(dve_steps, st.one())
                        e.wait_ge(dve_steps, st.count())
                        if cut < part:
                            v.tensor_tensor(be_f[rows, :], be_f[rows, :], be3[rows, :], ALU.subtract).then_inc(dve_steps, st.one())
                            e.wait_ge(dve_steps, st.count())

            def numerators(c):
                shape = [P, 2, 2, NS]
                lr, li = (left_b[:, :, :, i].unsqueeze(2).to_broadcast(shape) for i in (0, 1))
                rr, ri = (right_b[:, :, :, i].unsqueeze(1).to_broadcast(shape) for i in (0, 1))
                v.tensor_tensor(num[:, c], lr, rr if c == 0 else ri, ALU.mult).then_inc(dve_steps, st.one())
                e.wait_ge(dve_steps, st.count())
                v.tensor_tensor(num_t, li, ri if c == 0 else rr, ALU.mult).then_inc(dve_steps, st.one())
                e.wait_ge(dve_steps, st.count())
                v.tensor_tensor(num[:, c], num[:, c], num_t, ALU.add if c == 0 else ALU.subtract).then_inc(dve_steps, st.one())
                e.wait_ge(dve_steps, st.count())

            def ranks(b, piece):
                shape = [P, TPB, E, E]
                if piece == 0:
                    for u in (2, 3):
                        e.wait_ge(a_rope[u % 2], nth(b, u))
                    lg = logit[:, bass.ts(b, TPB), :]
                    other = lg.unsqueeze(2).to_broadcast(shape)
                    own = lg.unsqueeze(3).to_broadcast(shape)
                    v.tensor_tensor(above, other, own, ALU.is_gt).then_inc(dve_steps, st.one())
                    v.tensor_tensor(equal, other, own, ALU.is_equal).then_inc(dve_steps, st.one())
                if piece == 1:
                    e.wait_ge(dve_steps, st.count())
                    lower = const("lower").rearrange("p (e j) -> p e j", e=E).unsqueeze(1).to_broadcast(shape)
                    v.tensor_tensor(equal, equal, lower, ALU.mult).then_inc(dve_steps, st.one())
                    e.wait_ge(dve_steps, st.count())
                    v.tensor_tensor(above, above, equal, ALU.add).then_inc(dve_steps, st.one())
                if piece == 2:
                    e.wait_ge(dve_steps, st.count())
                    v.tensor_reduce(rank, above, AX.X, ALU.add).then_inc(dve_steps, st.one())
                if piece == 3:
                    e.wait_ge(dve_steps, st.count())
                    f, s = first[:, bass.ts(b, TPB), :], second[:, bass.ts(b, TPB), :]
                    v.tensor_scalar(f, rank, 0.0, None, ALU.is_equal).then_inc(dve_steps, st.one())
                    v.tensor_scalar(s, rank, 1.0, None, ALU.is_equal).then_inc(dve_steps, st.one())
                    e.wait_ge(dve_steps, st.count())
                    v.tensor_tensor(chosen_b[:, bass.ts(b, TPB), :], f, s, ALU.add).then_inc(r_chosen, 1)

            def statistics(b, u):
                e.wait_ge(a_x[u], b * 16 + 16)
                v.bn_stats(stats[:, u, 0:6], xin[:, u, :]).then_inc(dve_steps, st.one())

            def moments(b, u):
                e.wait_ge(dve_steps, st.count())
                alone(e)
                v.bn_aggr(mv[:, u, :], stats[:, u, 0:6]).then_inc(a_stat[u % 2], 1)

            def split(w, parts_of_w, before):
                for k in range(KB):
                    e.wait_ge(a_high, before + k + 1)
                    v.tensor_tensor(parts_of_w[1][:, k, :], w[:, k, :], parts_of_w[0][:, k, :].bitcast(F32), ALU.subtract)\
                        .then_inc(a_low, 1)

            def low(b, u):
                e.wait_ge(a_xt[u % 2], nth(b, u))
                if due(at := nth(b, u) - 1):
                    e.wait_ge(a_kvg[u % 2], at)
                v.tensor_tensor(xl[:, u % 2].rearrange("p k t -> p (k t)"), ps_t[u % 2][:, :],
                                xh[:, u % 2].rearrange("p k t -> p (k t)").bitcast(F32), ALU.subtract).then_inc(a_xl[u % 2], 1)

            def rope(b, u):
                if due(at := 4 * (nth(b, u) - 1)):
                    e.wait_ge(a_add[u % 2], at)
                for name, w, off, heads, src in (("q", D, 0, H, ps_q), ("k", KV * HD, D, KV, ps_kvg)):
                    e.wait_ge((a_q if name == "q" else a_kvg)[u % 2], nth(b, u))
                    x4 = src[u % 2][:, 0:w].rearrange("p (h d c) -> p h c d", h=heads, c=2)
                    for i, table in enumerate(("cos", "sin")):
                        o4 = rt[:, u % 2, i, off:off + w].rearrange("p (h c d) -> p h c d", h=heads, c=2)
                        tab = const(table)[:, u * 8:u * 8 + 8].unsqueeze(1).unsqueeze(1)
                        v.tensor_tensor(o4, x4, tab.to_broadcast([P, heads, 2, 8]), ALU.mult).then_inc(dve_steps, st.one())
                v.tensor_copy(v_tok[:, b, u, :], ps_kvg[u % 2][:, KV * HD:2 * KV * HD]).then_inc(dve_steps, st.one())
                e.wait_ge(dve_steps, st.count())
                v.tensor_tensor(logit[:, b * TPB + u, :], ps_kvg[u % 2][:, 2 * KV * HD:KVG], bgb, ALU.add)\
                    .then_inc(a_rope[u % 2], 1)

            def ahead(b, u, more, n, stage):
                if u + n < TPB or more:
                    stage(b + (u + n) // TPB, (u + n) % TPB)

            def sequence(b, more):
                for u in range(TPB):
                    ahead(b, u, more, 3, statistics)
                    ahead(b, u, more, 1, low)
                    ahead(b, u, more, 3, moments)
                    if isinstance(b, int) and (b, u) == (NB - 1, TPB - 1):
                        for par in range(2):
                            e.wait_ge(a_add[par], 4 * TPB // 2)
                        e.wait_ge(b_init, 1)
                        for piece in range(6):
                            q_parts(e, st, 0, 0, piece)
                    rope(b, u)
                    if isinstance(b, int):
                        prepare(b, u)
                    if due(b):
                        ranks(b - 1, u)

            for u in range(2):
                statistics(0, u)
                moments(0, u)
            split(wq, wq_parts, 0)
            low(0, 0)
            split(wkvg, wkvg_parts, KB)
            statistics(0, 2)
            moments(0, 2)
            st.close()
            sequence(0, True)
            st.close()
            with e.Fori(1, NB - 1) as b:
                st.enter(b, TPB * (1 + 4 + 1) + 7)
                sequence(b, True)
            st.leave(1, NB - 1)
            sequence(NB - 1, False)
            for piece in range(TPB):
                ranks(NB - 1, piece)
            e.wait_ge(r_chosen, NB)
            st.close()

        def act_s4_loads(e):
            for dst, src in ((lam_b, lam_d), (left_b[:, 0], ct_d.rearrange("o n c -> (o n) c")), (left_b[:, 1], q_d), (right_b[:, 1], p_d)):
                e.dma_start(dst, src.partition_broadcast(P)).then_inc(s4_load, 16)
            e.dma_start(vct[0:NS], vct_d).then_inc(s4_load, 16)
            e.dma_start(bp_c[0:NS], bp_d).then_inc(s4_load, 16)
            e.dma_start(log_step, step_d.partition_broadcast(P)).then_inc(s4_load, 16)
            e.dma_start(d_c, dd_d.partition_broadcast(P)).then_inc(s4_load, 16)

        def dve_s4(e, st, b, h):
            v = nc.vector
            if not (isinstance(b, int) and b == NB - 1):
                h -= 2

            def tt(out, a, b, op):
                v.tensor_tensor(out, a, b, op).then_inc(dve_steps, st.one())
                e.wait_ge(dve_steps, st.count())

            tab = const("s4").rearrange("p (c k) -> p c k", c=4)
            if h == 0:
                if isinstance(b, int) and b == 0:
                    e.wait_ge(s4_step, 1)
                v.tensor_copy(col[:, 0:4], tab[:, :, bass.ds(b, 1)]).then_inc(dve_steps, st.one())
                e.wait_ge(dve_steps, st.count())
                v.tensor_scalar(col[:, 4:6], col[:, 2:4], -1.0, None, ALU.mult).then_inc(dve_steps, st.one())
                v.tensor_scalar(col[:, 0:2], col[:, 0:2], inv_step, None, ALU.mult).then_inc(dve_steps, st.one())
                e.wait_ge(dve_steps, st.count())
                lam_r, lam_i = lam_b[:, :, 0], lam_b[:, :, 1]
                v.tensor_scalar(den_r, lam_r, col[:, 4:5], col[:, 0:1], ALU.mult, ALU.add).then_inc(dve_steps, st.one())
                v.tensor_scalar(den_a, lam_i, col[:, 3:4], None, ALU.mult).then_inc(dve_steps, st.one())
                v.tensor_scalar(den_i, lam_r, col[:, 5:6], col[:, 1:2], ALU.mult, ALU.add).then_inc(dve_steps, st.one())
                v.tensor_scalar(den_b, lam_i, col[:, 4:5], None, ALU.mult).then_inc(dve_steps, st.one())
                e.wait_ge(dve_steps, st.count())
                tt(den_r, den_r, den_a, ALU.add)
                tt(den_i, den_i, den_b, ALU.add)
            if h == 1:
                tt(den_a, den_r, den_r, ALU.mult)
                tt(den_b, den_i, den_i, ALU.mult)
                tt(den_a, den_a, den_b, ALU.add)
                v.reciprocal(den_a, den_a).then_inc(dve_steps, st.one())
                e.wait_ge(dve_steps, st.count())
                tt(den_r, den_r, den_a, ALU.mult)
                tt(den_i, den_i, den_a, ALU.mult)
            shape = [P, 4, NS]
            n_r, n_i = (num[:, c].rearrange("p l r n -> p (l r) n") for c in (0, 1))
            d_r, d_i = (d.unsqueeze(1).to_broadcast(shape) for d in (den_r, den_i))
            for c, x, y, op in ((0, n_r, n_i, ALU.add), (1, n_i, n_r, ALU.subtract)):
                if h == 2 + 2 * c:
                    tt(big[0], x, d_r, ALU.mult)
                    tt(big[1], y, d_i, ALU.mult)
                if h == 3 + 2 * c:
                    tt(big[2], big[0], big[1], op)
                    v.tensor_reduce(part_sum[:, c], big[2], AX.X, ALU.add).then_inc(dve_steps, st.one())
                    e.wait_ge(dve_steps, st.count())
            if h == 5:
                v.tensor_copy(sums[:, :, bass.ds(b, 1), :], part_sum.unsqueeze(2)).then_inc(dve_steps, st.one())
                e.wait_ge(dve_steps, st.count())
            if h < 6 or not (isinstance(b, int) and b == NB - 1):
                return
            if h == 7:
                return
            shape = [P, KB, 2]
            h_r, h_i = (tab[:, c].unsqueeze(2).to_broadcast(shape) for c in (2, 3))
            s_r, s_i = sums[:, 0, :, 2:4], sums[:, 1, :, 2:4]
            tt(hx[:, 0], h_r, s_r, ALU.mult)
            tt(hx[:, 1], h_i, s_i, ALU.mult)
            tt(hx[:, 0], hx[:, 0], hx[:, 1], ALU.subtract)
            tt(hx[:, 1], h_r, s_i, ALU.mult)
            tt(hx[:, 2], h_i, s_r, ALU.mult)
            tt(hx[:, 1], hx[:, 1], hx[:, 2], ALU.add)
            y_r, y_i, x_r, x_i = hx[:, 0, :, 0], hx[:, 1, :, 0], hx[:, 0, :, 1], hx[:, 1, :, 1]
            v.tensor_scalar(x_r, x_r, 1.0, None, ALU.add).then_inc(dve_steps, st.one())
            e.wait_ge(dve_steps, st.count())
            tt(sq, x_r, x_r, ALU.mult)
            tt(w_r, x_i, x_i, ALU.mult)
            tt(sq, sq, w_r, ALU.add)
            v.reciprocal(sq, sq).then_inc(dve_steps, st.one())
            e.wait_ge(dve_steps, st.count())
            t0, t1 = hx[:, 3, :, 0], hx[:, 4, :, 0]
            for w, a, b, op in ((w_r, y_r, y_i, ALU.add), (w_i, y_i, y_r, ALU.subtract)):
                tt(t0, a, x_r, ALU.mult)
                tt(t1, b, x_i, ALU.mult)
                tt(w, t0, t1, op)
                tt(w, w, sq, ALU.mult)
            a_r, a_i = sums[:, 0, :, 1], sums[:, 1, :, 1]
            for c, x, y, op in ((0, w_r, w_i, ALU.subtract), (1, w_i, w_r, ALU.add)):
                tt(t0, a_r, x, ALU.mult)
                tt(t1, a_i, y, ALU.mult)
                tt(t0, t0, t1, op)
                tt(roots[:, c], sums[:, c, :, 0], t0, ALU.subtract)
            e.nop().then_inc(s4_roots, 1)


        def dve_taps(e, st):
            v = nc.vector
            e.wait_ge(s4_taps, 1)
            v.memset(taps[:, 0:P], 0.0).then_inc(dve_steps, st.one())
            v.tensor_copy(taps[:, P:P + D], bank[7][:, :]).then_inc(dve_steps, st.one())
            e.wait_ge(dve_steps, st.count())
            v.tensor_tensor(taps[:, P:P + 1], taps[:, P:P + 1], d_c, ALU.add).then_inc(s4_row, 1)
            st.close()

        def pe_s4(e):
            t = nc.tensor
            e.wait_ge(s4_bw, 1)
            t.matmul(bank[6][:, 0:2 * NS], bp_w[0:NS, :], vct[0:NS].rearrange("p n c -> p (n c)"), start=True, stop=True).then_inc(s4_b, 1)

        def pe_taps(e, part):
            t = nc.tensor
            if part == 0:
                e.wait_ge(s4_roots, 1)
                e.wait_ge(c_dft, 16)
                e.wait_ge(m_ye, NB * MPB)
            for c in range(2):
                for k in range(KB):
                    if (KB * c + k) // 2 != part:
                        continue
                    i = t.matmul(bank[7][:, :], roots[:, c, k:k + 1].to_broadcast([P, P]), dft[:, c, k, :],
                                 start=(c + k == 0), stop=(c + k == KB))
            if part == 3:
                i.then_inc(s4_taps, 1)

        def sp_taps(e):
            e.wait_ge(s4_row, 1)
            e.dma_start(kpad_d, taps).then_inc(s4_out, 16)
            e.wait_ge(s4_out, 16)
            e.dma_start(toep[:, :], bass.AP(kpad_d.tensor, P, [[P + D - 1, P], [1, D]])).then_inc(s4_toep, 16)

        def pool_a(e, st):
            g = nc.gpsimd
            e.wait_ge(a_load, 32)

            def inverse_root(b, u):
                e.wait_ge(a_stat[u % 2], nth(b, u))
                g.tensor_tensor(rstd[:, u, :], mv[:, u, 1:2], const("eps"), ALU.add).then_inc(pool_steps, st.one())
                g.tensor_tensor(shift[:, u, :], mv[:, u, 0:1], const("minus"), ALU.mult).then_inc(pool_steps, st.one())
                e.wait_ge(pool_steps, st.count())
                g.tensor_tensor(rstd[:, u, :], rstd[:, u, :], const("half"), ALU.pow).then_inc(pool_steps, st.one())
                e.wait_ge(pool_steps, st.count())
                g.tensor_tensor(shift[:, u, :], shift[:, u, :], rstd[:, u, :], ALU.mult).then_inc(a_rstd[u % 2], 1)

            def constant_columns():
                for par in range(2):
                    e.wait_ge(a_xn[par], NT // 2)
                g.memset(kstk[:, :, 112:P], 1.0).then_inc(pool_steps, st.one())
                g.memset(mstk, 0.0).then_inc(pool_steps, st.one())
                g.memset(qstk[:, :, :, 112:P], 0.0).then_inc(pool_steps, st.one())
                g.memset(vb[:, :, :, HD:HD + 1], 1.0).then_inc(pool_steps, st.one())
                e.wait_ge(pool_steps, st.count())
                g.memset(vb[:, :, :, HD + 1:], 0.0).then_inc(b_init, 1)

            def add(b, u):
                e.wait_ge(a_rope[u % 2], nth(b, u))
                alone(e)
                for w, off, heads, dst in ((D, 0, H, q_tok), (KV * HD, D, KV, k_tok)):
                    xc, xs = (rt[:, u % 2, i, off:off + w].rearrange("p (h c d) -> p h c d", h=heads, c=2) for i in (0, 1))
                    o = dst[:, b, u, :].rearrange("p (h c d) -> p h c d", h=heads, c=2)
                    for c, op in ((0, ALU.subtract), (1, ALU.add)):
                        i = g.tensor_tensor(o[:, :, c, :], xc[:, :, c, :], xs[:, :, 1 - c, :], op)
                        i.then_inc(a_add[u % 2], 1)

            def sequence(b, more):
                for u in range(TPB):
                    if u + 3 < TPB or more:
                        inverse_root(b + (u + 3) // TPB, (u + 3) % TPB)
                    if isinstance(b, int) and b == NB - 1 and u == 2:
                        constant_columns()
                    add(b, u)

            for u in range(3):
                inverse_root(0, u)
            st.close()
            sequence(0, True)
            st.close()
            with e.Fori(1, NB - 1) as b:
                st.enter(b, 3 * TPB)
                sequence(b, True)
            st.leave(1, NB - 1)
            sequence(NB - 1, False)
            st.close()

        def act_a(e):
            def normalise(b, u):
                e.wait_ge(a_rstd[u % 2], nth(b, u))
                if due(at := nth(b, u) - 1):
                    e.wait_ge(a_tr[u % 2], at)
                if u >= 2:
                    e.wait_ge(a_store[u - 2], b * 16 + 16)
                elif due(at := b * 16):
                    e.wait_ge(a_store[u + 2], at)
                nc.scalar.activation(xn[:, u % 2, :], xin[:, u, :], ACT.Identity, bias=shift[:, u, :], scale=rstd[:, u, :])\
                    .then_inc(a_xn[u % 2], 1)

            def high_parts(w, parts_of_w):
                for k in range(KB):
                    nc.scalar.copy(parts_of_w[0][:, k, :], w[:, k, :]).then_inc(a_high, 1)

            def lift(b, u):
                e.wait_ge(a_tr[u % 2], nth(b, u))
                if due(at := nth(b, u) - 1):
                    e.wait_ge(a_kvg[u % 2], at)
                nc.scalar.copy(xh[:, u % 2].rearrange("p k t -> p (k t)"), ps_t[u % 2][:, :]).then_inc(a_xt[u % 2], 1)

            def sequence(b, more):
                for u in range(TPB):
                    if u + 1 < TPB or more:
                        lift(b + (u + 1) // TPB, (u + 1) % TPB)
                    if u + 2 < TPB or more:
                        normalise(b + (u + 2) // TPB, (u + 2) % TPB)
                    if not due(b) and u == 1:
                        e.wait_ge(a_w, 48)
                        act_s4_loads(e)
                    if u % 2 and more:
                        x = bass.ds(b * (E // NB) + u // 2, 1)
                        e.dma_start(w_e[:, x], we_d[x].rearrange("x (k p) n -> p x k n", p=P)).then_inc(e_load, 16)
                    if not due(b) and u == 3:
                        e.wait_ge(s4_load, 128)
                        nc.scalar.activation(inv_step, log_step, ACT.Exp, scale=-1.0).then_inc(s4_step, 1)

            normalise(0, 0)
            e.wait_ge(a_wq, 16)
            high_parts(wq, wq_parts)
            lift(0, 0)
            normalise(0, 1)
            e.wait_ge(a_w, 48)
            high_parts(wkvg, wkvg_parts)
            sequence(0, True)
            with e.Fori(1, NB - 1) as b:
                sequence(b, True)
            sequence(NB - 1, False)
            for par in range(2):
                e.wait_ge(a_kvg[par], NT // 2)
            for x in range(E - E // NB, E):
                e.dma_start(w_e[:, x], we_d[x].rearrange("(k p) n -> p k n", p=P)).then_inc(e_load, 16)

        def pe_a(e):
            t = nc.tensor
            e.wait_ge(a_load, 32)

            def turn(b, u):
                e.wait_ge(a_xn[u % 2], nth(b, u))
                if due(at := nth(b, u) - 1):
                    e.wait_ge(a_xl[u % 2], at)
                for k in range(KB):
                    i = t.transpose(ps_t[u % 2][:, k * P:(k + 1) * P], xn[:, u % 2, k * P:(k + 1) * P], ident)
                i.then_inc(a_tr[u % 2], 1)

            def sequence(b, more):
                for u in range(TPB):
                    if u + 1 < TPB or more:
                        turn(b + (u + 1) // TPB, (u + 1) % TPB)
                    e.wait_ge(a_xl[u % 2], nth(b, u))
                    if due(at := nth(b, u) - 1):
                        e.wait_ge(a_rope[u % 2], at)
                    for w, out, n, signal, first_block in ((wq_parts, ps_q, D, a_q, 0), (wkvg_parts, ps_kvg, KVG, a_kvg, KB)):
                        for k in range(KB):
                            if not due(b) and u == 0:
                                e.wait_ge(a_low, first_block + k + 1)
                            for x, part in ((xh, 0), (xl, 0), (xh, 1)):
                                i = t.matmul(out[u % 2][:, 0:n], x[:, u % 2, k, :], w[part][:, k, :],
                                             start=(k == 0 and x is xh and part == 0), stop=(k == KB - 1 and part == 1))
                        i.then_inc(signal[u % 2], 1)
                    if not due(b) and u == 3:
                        pe_s4(e)

            turn(0, 0)
            sequence(0, True)
            with e.Fori(1, NB - 1) as b:
                sequence(b, True)
            sequence(NB - 1, False)

        def dve_route(e, st, h):
            v = nc.vector

            def tt(out, a, b, op):
                v.tensor_tensor(out, a, b, op).then_inc(dve_steps, st.one())
                e.wait_ge(dve_steps, st.count())

            def running(a, spare, last, n):
                step = 1
                while step < n:
                    o = last if 2 * step >= n else spare
                    v.tensor_copy(o[:, 0:step], a[:, 0:step]).then_inc(dve_steps, st.one())
                    tt(o[:, step:], a[:, step:], a[:, 0:n - step], ALU.add)
                    a, spare, step = o, a, 2 * step
                return a

            if h < 0:
                e.wait_ge(r_count, 1)
                v.tensor_copy(tot.rearrange("p t e -> p (t e)"), bank[7][:, P:2 * P]).then_inc(dve_steps, st.one())
                v.tensor_copy(pos.rearrange("p t e -> p (t e)"), bank[7][:, 0:P]).then_inc(dve_steps, st.one())
                e.wait_ge(dve_steps, st.count())
                tt(pos, pos, tot, ALU.subtract)
                incl = running(tot, scan_a, scan_b, NT)
                tt(pos, pos, incl, ALU.add)
                n_e = incl[:, NT - 1, :]
                cmp = compared[:, 0:E * NT].rearrange("p (e i) -> p e i", e=E)
                tt(cmp, n_e.unsqueeze(2).to_broadcast([P, E, NT]), const("i128").unsqueeze(1).to_broadcast([P, E, NT]), ALU.is_gt)
                v.tensor_reduce(end_b, cmp, AX.X, ALU.add).then_inc(dve_steps, st.one())
                e.wait_ge(dve_steps, st.count())
                v.tensor_copy(tiles_of, end_b).then_inc(dve_steps, st.one())
                e.wait_ge(dve_steps, st.count())
                running(end_b, scan_a[:, 0, :], end_a, E)
                tt(end_b, end_a, tiles_of, ALU.subtract)
                v.tensor_scalar(end_b, end_b, float(P), None, ALU.mult).then_inc(dve_steps, st.one())
                e.wait_ge(dve_steps, st.count())
                tt(pos, pos, end_b.unsqueeze(1).to_broadcast([P, NT, E]), ALU.add)
            if h == 0:
                for k, pick in enumerate((first, second)):
                    tt(pick, pick, pos, ALU.mult)
                    v.tensor_reduce(slot_f[:, k, :], pick, AX.X, ALU.add).then_inc(dve_steps, st.one())
                    e.wait_ge(dve_steps, st.count())
                v.tensor_copy(slots[:, :, :], slot_f).then_inc(dve_steps, st.one())
                shape = [P, TOPK * NT, MT + 1]
                flat = slot_f.rearrange("p k n -> p (k n)")
                tt(reached, flat.unsqueeze(2).to_broadcast(shape), const("i128m").unsqueeze(1).to_broadcast(shape), ALU.is_ge)
                place = slot_q.rearrange("p k n -> p (k n)")
                v.tensor_reduce(place, reached, AX.X, ALU.add).then_inc(dve_steps, st.one())
                e.wait_ge(dve_steps, st.count())
                v.tensor_scalar(place, place, -1.0, float(-P), ALU.add, ALU.mult).then_inc(dve_steps, st.one())
                e.wait_ge(dve_steps, st.count())
                v.tensor_tensor(slot_p.rearrange("p k n -> p (k n)"), place, flat, ALU.add).then_inc(r_slots, 1)
                e.wait_ge(r_slots, 1)
            if h == 1:
                place = slot_p.rearrange("p k n -> p (k n)").unsqueeze(2).to_broadcast([P, TOPK * NT, P])
                v.tensor_tensor(of_place, place, iota_b[:, :].unsqueeze(1).to_broadcast([P, TOPK * NT, P]), ALU.is_equal)\
                    .then_inc(r_place, 1)
                shape = [P, TOPK * NT, MT]
                tt(of_tile[:, :, 0, :], reached[:, :, 0:MT], reached[:, :, 1:], ALU.subtract)
                numbers = number_b[:, :].unsqueeze(2).to_broadcast(shape)
                tt(of_tile[:, :, 1, :], of_tile[:, :, 0, :], numbers, ALU.mult)
                v.tensor_scalar(of_tile[:, :, 0, :], of_tile[:, :, 0, :], const("part"), None, ALU.mult).then_inc(r_tile, 1)
                cmp = compared.rearrange("p (i e) -> p i e", e=E)
                tt(cmp, end_a.unsqueeze(1).to_broadcast([P, MT, E]), const("tile").unsqueeze(2).to_broadcast([P, MT, E]), ALU.is_le)
                v.tensor_reduce(eid_f, cmp, AX.X, ALU.add).then_inc(dve_steps, st.one())
                e.wait_ge(dve_steps, st.count())
                v.tensor_scalar(eid_f, eid_f, float(E - 1), None, ALU.min).then_inc(dve_steps, st.one())
                e.wait_ge(dve_steps, st.count())
                v.tensor_copy(eid_i[:, :], eid_f[0:1, :]).then_inc(r_eid, 1)

        def dve_tokens(e, st):
            v = nc.vector
            e.wait_ge(r_back, 1)
            v.tensor_scalar(eid_f, bank[7][:, MT:2 * MT], float(P), None, ALU.mult).then_inc(dve_steps, st.one())
            e.wait_ge(dve_steps, st.count())
            v.tensor_tensor(eid_f, eid_f, bank[7][:, 0:MT], ALU.add).then_inc(dve_steps, st.one())
            e.wait_ge(dve_steps, st.count())
            v.tensor_copy(slots_i[:, :], eid_f).then_inc(r_tokens, 1)

        def pe_route(e):
            t = nc.tensor
            e.wait_ge(r_chosen, NB)
            rhs = chosen_b.rearrange("p t e -> p (t e)")
            t.matmul(bank[7][:, 0:P], tri_b[:, :], rhs, start=True, stop=True)
            t.matmul(bank[7][:, P:2 * P], ones_b[:, :], rhs, start=True, stop=True).then_inc(r_count, 1)

        def pe_back(e):
            t = nc.tensor
            e.wait_ge(r_tile, 1)
            e.wait_ge(r_place, 1)
            for n in range(TOPK * NT):
                i = t.matmul(bank[7][:, 0:2 * MT], of_place[:, n, :], of_tile[:, n].rearrange("p c i -> p (c i)"),
                             start=(n == 0), stop=(n == TOPK * NT - 1))
            i.then_inc(r_back, 1)

        qstk = take([P, TPB, R, P], BF16, restart=0)
        mstk = take([P, 2, TPB, R, 32], BF16)
        kstk = take([P, TPB, P], BF16)
        qt = take([P, 2, R, S], BF16)
        kt = take([P, 2, S], BF16)
        pt = take([P, JO[-1] + R * JW[-1]])
        vb = take([P, TPB, KV, VW])
        oe = take([P, S])
        o2 = take([P, TPB, 2 * R * HD])
        ot = take([P, KB, TPB, P])
        ot_0 = take([P, TPB, P])
        OT_END = used[0]
        xg = take([P, 2, D])
        xgt = take([P, KB, P])
        yo = take([P, 2, D])
        rest = take([P, TPB, R, HD])
        krest = take([P, TPB, HD])
        rmax = take([P, TPB, R])
        rmax_t = take([P, TPB, R])
        rsum = take([P, TPB, R])
        tok_b = take([P, 2, 1], U32)
        lam_b = take([P, NS, 2])
        num = toep[:, :].rearrange("p (c l r n) -> p c l r n", c=2, l=2, r=2)
        den_r, den_i, den_a, den_b = (take([P, NS]) for _ in range(4))
        big = [w_proj[:, KB * D + i * 4 * NS:KB * D + (i + 1) * 4 * NS].rearrange("p (a n) -> p a n", n=NS) for i in range(3)]
        col = take([P, 8])
        part_sum = take([P, 2, 4])
        sums = take([P, 2, KB, 4])
        hx = take([P, 6, KB, 2])
        w_r, w_i, sq = (take([P, KB]) for _ in range(3))

        b_init = sem("b_init")
        b_wo = sem("b_wo")
        b_v = sem("b_v")
        b_q, b_k = sem("b_q"), sem("b_k")
        b_tq, b_te = sem("b_tq"), sem("b_te")
        b_tm, b_me = sem("b_tm"), sem("b_me")
        b_s1, b_m, b_mx = sem("b_s1"), sem("b_m"), sem("b_mx")
        b_s2, b_e, b_sel, b_pv = sem("b_s2"), sem("b_e"), sem("b_sel"), sem("b_pv")
        b_o, b_ot, b_on, b_o2, b_o2e = sem("b_o"), sem("b_ot"), sem("b_on"), sem("b_o2"), sem("b_o2e")
        b_p, b_s, b_o0 = sem("b_p"), sem("b_s"), sem("b_o0")
        m_idx, m_xt, m_xe, m_y, m_ye = sem("m_idx"), sem("m_xt"), sem("m_xe"), sem("m_y"), sem("m_ye")
        m_x, m_st = sems("m_x", 2), sems("m_st", 2)

        NG = KV
        JOBS1 = [(q, h, n) for q, n in ((3, 1), (2, 1), (1, 2), (0, 4)) for h in range(0, R, n)]
        JOBS2 = [(j, h, n) for j, n in ((0, 1), (1, 1), (2, 2), (3, 4)) for h in range(0, R, n)]
        NJ = len(JOBS1)
        LAST2 = [max(i for i, job in enumerate(JOBS2) if job[0] == j) + 1 for j in range(TPB)]
        tb = bank[5][:, :].bitcast(BF16).rearrange("p (h s) -> p h s", h=2)
        xb = bank[6][:, :].rearrange("p (k t) -> p k t", k=KB)

        def nth_of(per, b, h, k):
            return b * (NG * per) + (h * per + k)

        def next_group(b, h, n):
            return b + (h + n) // NG, (h + n) % NG

        MIDDLE = [(0, None), (1, None), (2, None), (3, None), (4, None), (5, 6), (7, None), (8, 9)]
        FIRST = [(None, None), (None, None), (0, None), (1, 2), (3, 4), (5, 6), (7, None), (8, 9)]
        LAST = [(0, None), (1, None), (2, None), (3, None), (4, 5), (6, 7), (8, 9), (None, None)]

        def tiles_at(b, h):
            return {0: FIRST, NB - 1: LAST}[b][h] if isinstance(b, int) and b in (0, NB - 1) else MIDDLE[h]

        def tiles_by(b, h):
            return b * MPB + max([m + 1 for g in range(h + 1) for m in tiles_at(b, g) if m is not None], default=0)

        def first_tiles_by(b, h):
            return tiles_by(b, h) - (tiles_at(b, h)[1] is not None)

        TURN_AT, QUARTERS_AT, LATE_AT = 2, (4, 6, 8, 10), (5, 9)
        NTU, NMU = R // 2 + 1, R // 2

        def phase_a_over(e):
            for u in range(TPB):
                e.wait_ge(a_add[u % 2], 4 * NT // 2)
                e.wait_ge(a_store[u], 16 * NB)

        def pool_b(e, st):
            g = nc.gpsimd
            phase_a_over(e)
            e.wait_ge(b_init, 1)

            def values(b):
                if due(at := nth_of(4, b, 0, 0)):
                    e.wait_ge(b_pv, at)
                alone(e)
                g.tensor_copy(vb[:, :, :, 0:HD], v_tok[:, b].rearrange("p t (h d) -> p t h d", h=KV)).then_inc(b_v, 1)

            def k_parts(b, h):
                if due(at := nth_of(NTU, b, h, 0)):
                    e.wait_ge(b_tq, at)
                e.wait_ge(pool_steps, st.count())
                alone(e)
                k = k_tok[:, b, :, HD * h:HD * h + HD]
                shape = [P, TPB, 2, HD]

                def twice(a, c):
                    return kstk[:, :, a:c].rearrange("p t (n d) -> p t n d", n=2)

                g.tensor_copy(twice(0, 32), k.unsqueeze(2).to_broadcast(shape)).then_inc(pool_steps, st.one())
                g.tensor_copy(kstk[:, :, 96:112], k).then_inc(pool_steps, st.one())
                e.wait_ge(pool_steps, st.count())
                alone(e)
                g.tensor_tensor(krest, k, kstk[:, :, 0:HD], ALU.subtract).then_inc(pool_steps, st.one())
                e.wait_ge(pool_steps, st.count())
                alone(e)
                g.tensor_copy(twice(32, 64), krest.unsqueeze(2).to_broadcast(shape)).then_inc(pool_steps, st.one())
                e.wait_ge(pool_steps, st.count())
                alone(e)
                g.tensor_tensor(twice(64, 96), krest.unsqueeze(2).to_broadcast(shape), twice(32, 64), ALU.subtract).then_inc(b_k, 1)

            def select(b, h):
                for j in range(TPB):
                    e.wait_ge(b_e, nth_of(NJ, b, h, LAST2[j]))
                    alone(e)
                    diag = pt[:, JO[j]:JO[j] + R * JW[j]].rearrange("p (h q) -> p h q", h=R)[:, :, 0:P]
                    g.affine_select(out=diag, in_=diag, compare_op=ALU.is_ge, fill=0.0, base=0,
                                    pattern=[[0, R], [1, P]], channel_multiplier=-1).then_inc(b_sel, 1)

            def gather(b, m):
                if due(at := b * (8 * MPB) + 16 * (m // 2)):
                    e.wait_ge(m_x[m % 2], at)
                alone(e)
                g.tensor_copy(tok_b[:, m % 2], slots_i[:, bass.ds(b * MPB + m, 1)]).then_inc(m_idx, 1)
                if due(at := b * MPB + (m - 1)):
                    e.wait_ge(m_xt, at)
                e.wait_ge(m_idx, b * MPB + (m + 1))
                alone(e)
                e.indirect_dma_start(xg[:, m % 2, :], None, xn_d, bass.IndirectOffsetOnAxis(ap=tok_b[:, m % 2, :], axis=0))\
                 .then_inc(m_x[m % 2], 16)

            def go(b, more):
                for h in range(NG):
                    if h == 0:
                        values(b)
                    if h + 2 < NG or more:
                        k_parts(*next_group(b, h, 2))
                    select(b, h)
                    if not due(b) and h == 1:
                        e.wait_ge(r_tokens, 1)
                        gather(0, 0)
                        gather(0, 1)
                    for m in tiles_at(b, h):
                        if m is not None and (m + 2 < MPB or more):
                            gather(b + (m + 2) // MPB, (m + 2) % MPB)

            k_parts(0, 0)
            k_parts(0, 1)
            go(0, True)
            st.close()
            with e.Fori(1, NB - 1) as b:
                st.enter(b, 4 * NG)
                go(b, True)
            st.leave(1, NB - 1)
            go(NB - 1, False)
            st.close()

        def q_parts(e, st, b, h, piece):
            v = nc.vector
            q = q_tok[:, b, :, R * HD * h:R * HD * (h + 1)].rearrange("p t (h d) -> p t h d", h=R)
            high, mid, low = (qstk[:, :, :, a:a + HD] for a in (0, 16, 96))
            if piece == 0:
                if due(at := nth_of(NTU, b, h, 0)):
                    e.wait_ge(b_tq, at)
                v.tensor_copy(high, q).then_inc(dve_steps, st.one())
            if piece == 1:
                e.wait_ge(dve_steps, st.count())
                v.tensor_tensor(rest, q, high, ALU.subtract).then_inc(dve_steps, st.one())
            if piece == 2:
                e.wait_ge(dve_steps, st.count())
                v.tensor_copy(mid, rest).then_inc(dve_steps, st.one())
            if piece == 3:
                e.wait_ge(dve_steps, st.count())
                v.tensor_copy(qstk[:, :, :, 32:64], qstk[:, :, :, 0:32]).then_inc(dve_steps, st.one())
                v.tensor_copy(qstk[:, :, :, 64:96], qstk[:, :, :, 0:32]).then_inc(dve_steps, st.one())
            if piece == 4:
                v.tensor_tensor(low, rest, mid, ALU.subtract).then_inc(dve_steps, st.one())
            if piece == 5:
                if due(at := nth_of(NMU, b, h, -NMU)):
                    e.wait_ge(b_tm, at)
                e.wait_ge(dve_steps, st.count())
                v.tensor_copy(mstk[:, h % 2, :, :, 0:HD], low).then_inc(b_q, 1)

        def dve_b(e, st):
            v = nc.vector

            def maxima(b, h, n):
                q, r, m = JOBS1[n]
                if n == 0 and due(at := nth_of(1, b, h, 0)):
                    e.wait_ge(b_mx, at)
                e.wait_ge(b_s1, nth_of(NJ, b, h, n + 1))
                w = P * (q + 1)
                v.tensor_reduce(rmax[:, q, r:r + m], bank[(NJ * h + n) % 2][:, 0:m * w].rearrange("p (h k) -> p h k", h=m),
                                AX.X, ALU.max).then_inc(b_m, 1)

            def maxima_parts(b, h):
                e.wait_ge(b_m, nth_of(NJ, b, h, NJ))
                part = [mstk[:, h % 2, :, :, HD + i] for i in range(3)]
                v.tensor_scalar(part[0], rmax, -1.0, None, ALU.mult).then_inc(dve_steps, st.one())
                e.wait_ge(dve_steps, st.count())
                v.scalar_tensor_tensor(out=rmax_t, in0=rmax, scalar=-1.0, in1=part[0], op0=ALU.mult, op1=ALU.subtract).then_inc(dve_steps, st.one())
                e.wait_ge(dve_steps, st.count())
                v.tensor_copy(part[1], rmax_t).then_inc(dve_steps, st.one())
                e.wait_ge(dve_steps, st.count())
                v.tensor_tensor(part[2], rmax_t, part[1], ALU.subtract).then_inc(b_mx, 1)

            def maxima_rows(b, h):
                for i in range(NMU):
                    e.wait_ge(b_tm, nth_of(NMU, b, h, i + 1))
                    v.tensor_copy(qt[96:P, h % 2, 2 * i:2 * i + 2, :], tb[96:P]).then_inc(b_me, 1)

            def normalise(b, h):
                e.wait_ge(b_ot, nth_of(1, b, h, 1))
                o4 = bank[6][:, :].rearrange("p (t r c) -> p t r c", t=TPB, r=R)
                v.reciprocal(rsum, o4[:, :, :, HD]).then_inc(dve_steps, st.one())
                if h % 2 == 0 and due(at := b * (NG // 2) + h // 2):
                    e.wait_ge(b_o2, at)
                e.wait_ge(dve_steps, st.count())
                half = o2[:, :, (h % 2) * R * HD:(h % 2 + 1) * R * HD].rearrange("p t (r d) -> p t r d", r=R)
                v.tensor_tensor(half, o4[:, :, :, 0:HD], rsum.unsqueeze(3).to_broadcast([P, TPB, R, HD]), ALU.mult)\
                    .then_inc(b_on, 1)

            def go(b, more):
                for h in range(NG):
                    for n in range(NJ):
                        if h + 1 < NG or more:
                            maxima(*next_group(b, h, 1), n)
                        if n == 0 and h > 0:
                            normalise(b, h - 1)
                        if n == 0 and h == 0 and due(b):
                            normalise(b - 1, NG - 1)
                        if 2 <= n < 8 and (h + 2 < NG or more):
                            q_parts(e, st, *next_group(b, h, 2), n - 2)
                    if h + 1 < NG or more:
                        maxima_parts(*next_group(b, h, 1))
                    dve_s4(e, st, b, h)
                    if not due(b) and h < 2:
                        dve_route(e, st, h)
                    if h + 1 < NG or more:
                        maxima_rows(*next_group(b, h, 1))
                    if not due(b) and h == 1:
                        dve_tokens(e, st)

            phase_a_over(e)
            for piece in range(6):
                q_parts(e, st, 0, 1, piece)
            dve_route(e, st, -1)
            for n in range(NJ):
                maxima(0, 0, n)
            maxima_parts(0, 0)
            maxima_rows(0, 0)
            st.close()
            go(0, True)
            st.close()
            with e.Fori(1, NB - 1) as b:
                st.enter(b, NG * (6 + 3 + 1) + 9 + 6 + 2 * 4 + 1)
                go(b, True)
            st.leave(1, NB - 1)
            go(NB - 1, False)
            dve_scale(e)
            dve_taps(e, st)
            normalise(NB - 1, NG - 1)
            st.close()

        def projected(e, b, u, from_bank=7):
            e.wait_ge(b_p, b * TPB + (u + 1))
            e.wait_ge(b_q, nth_of(1, b, NG, 0))
            nc.scalar.copy(s_tok[:, b, u, :], bank[from_bank][:, :]).then_inc(b_s, 1)

        def act_b(e):
            a = nc.scalar
            phase_a_over(e)

            def turned(b, h, i):
                e.wait_ge(b_tq, nth_of(NTU, b, h, i + 1))
                if i == 0 and due(at := nth_of(NJ, b, h, -NJ)):
                    e.wait_ge(b_s2, at)
                if i < NTU - 1:
                    a.copy(qt[:, h % 2, 2 * i:2 * i + 2, :], tb).then_inc(b_te, 1)
                else:
                    a.copy(kt[:, h % 2, :], tb[:, 0, :]).then_inc(b_te, 1)

            def exps(b, h, n):
                j, r, m = JOBS2[n]
                e.wait_ge(b_s2, nth_of(NJ, b, h, n + 1))
                if due(at := nth_of(4, b, h, j - 3)):
                    e.wait_ge(b_pv, at)
                o = pt[:, JO[j] + r * JW[j]:JO[j] + (r + m) * JW[j]]
                a.activation(o, bank[2 + (NJ * h + n) % 2][:, 0:m * JW[j]], ACT.Exp, scale=HD ** -0.5).then_inc(b_e, 1)

            def expert_x(b, m):
                e.wait_ge(m_xt, b * MPB + (m + 1))
                if due(at := b * MPB + m):
                    e.wait_ge(m_y, at)
                a.copy(xgt.rearrange("p k t -> p (k t)"), bank[6][:, :]).then_inc(m_xe, 1)

            def expert_y(b, m):
                e.wait_ge(m_y, b * MPB + (m + 1))
                if due(at := b * (8 * MPB) + 16 * (m // 2)):
                    e.wait_ge(m_st[m % 2], at)
                a.activation(yo[:, m % 2, :], bank[7][:, :], ACT.Relu).then_inc(m_ye, 1)

            def pair_out(b, i):
                e.wait_ge(b_o2, b * (NG // 2) + (i + 1))
                a.copy((ot[:, i] if i else ot_0).rearrange("p t f -> p (t f)"), bank[6][:, :]).then_inc(b_o2e, 1)

            def first_pair(b):
                e.wait_ge(b_o2e, b * (NG // 2) + 1)
                if due(at := b * TPB):
                    e.wait_ge(b_p, at)
                a.copy(ot[:, 0].rearrange("p t f -> p (t f)"), ot_0.rearrange("p t f -> p (t f)")).then_inc(b_o0, 1)

            def output(b, h):
                e.wait_ge(b_pv, nth_of(4, b, h, 4))
                if due(at := nth_of(1, b, h, 0)):
                    e.wait_ge(b_ot, at)
                a.copy(oe, bank[4][:, :]).then_inc(b_o, 1)

            def go(b, more):
                for h in range(NG):
                    first, second = tiles_at(b, h)
                    late = h >= TPB and second is None
                    for n in range(NJ):
                        exps(b, h, n)
                        if n == TURN_AT and first is not None:
                            expert_x(b, first)
                    if not late and first is not None:
                        expert_y(b, first)
                    if h == 0 and due(b):
                        pair_out(b - 1, NG // 2 - 1)
                    if h % 2 == 0 and h:
                        pair_out(b, h // 2 - 1)
                    if second is not None:
                        expert_x(b, second)
                    if h + 2 < NG or more:
                        for i in range(NTU):
                            turned(*next_group(b, h, 2), i)
                    output(b, h)
                    if late and first is not None:
                        expert_y(b, first)
                    if h < TPB and due(b):
                        projected(e, b - 1, h)
                    if h == TPB:
                        first_pair(b)
                    if second is not None:
                        expert_y(b, second)

            for h in range(2):
                for i in range(NTU):
                    turned(0, h, i)
            go(0, True)
            with e.Fori(1, NB - 1) as b:
                go(b, True)
            go(NB - 1, False)
            pair_out(NB - 1, NG // 2 - 1)
            for u in range(TPB):
                projected(e, NB - 1, u, 7 - u % 2)
                gate(e, 0, u)

        def pe_b(e):
            t = nc.tensor
            for par in range(2):
                e.wait_ge(a_rope[par], NT // 2)
            e.wait_ge(b_init, 1)

            def turn(b, h, i):
                if i == 0:
                    e.wait_ge(b_q, nth_of(1, b, h, 1))
                if i == NTU - 1:
                    e.wait_ge(b_k, nth_of(1, b, h, 1))
                if i > 0:
                    e.wait_ge(b_te, nth_of(NTU, b, h, i))
                elif h == 1 and not due(b):
                    e.wait_ge(b_te, NTU)
                elif due(at := nth_of(NMU, b, h, -NMU)):
                    e.wait_ge(b_me, at)
                for x in range(2 if i < NTU - 1 else 1):
                    for q in range(TPB):
                        src = qstk[:, q, 2 * i + x, :] if i < NTU - 1 else kstk[:, q, :]
                        j = t.transpose(tb[:, x, q * P:(q + 1) * P], src, ident_b[:, :])
                j.then_inc(b_tq, 1)

            def turn_maxima(b, h, i, last):
                if i == 0:
                    e.wait_ge(b_mx, nth_of(1, b, h, 1))
                    e.wait_ge(b_te, nth_of(NTU, b, h, NTU if last else 2 * NTU))
                if due(at := nth_of(NMU, b, h, i)):
                    e.wait_ge(b_me, at)
                for x in range(2):
                    for q in range(TPB):
                        j = t.transpose(tb[96:P, x, q * P:(q + 1) * P], mstk[:, h % 2, q, 2 * i + x, :], ident_b[:, :])
                j.then_inc(b_tm, 1)

            def scores_1(b, h, n):
                q, r, m = JOBS1[n]
                if n == 0:
                    e.wait_ge(b_te, nth_of(NTU, b, h, NTU))
                if due(at := nth_of(NJ, b, h, n - 1)):
                    e.wait_ge(b_m, at)
                w = P * (q + 1)
                for x in range(m):
                    o = bank[(NJ * h + n) % 2][:, x * w:(x + 1) * w]
                    t.matmul(o, qt[:, h % 2, r + x, q * P:(q + 1) * P], kt[:, h % 2, 0:w], start=True, stop=True)
                    i = t.matmul(o[:, q * P:], ident_b[:, :], mask_b[:, :], start=False, stop=True, skip_group_check=True)
                i.then_inc(b_s1, 1)

            def scores_2(b, h, n):
                j, r, m = JOBS2[n]
                if n == 0:
                    e.wait_ge(b_me, nth_of(NMU, b, h, NMU))
                if due(at := nth_of(NJ, b, h, n - 1)):
                    e.wait_ge(b_e, at)
                for x in range(m):
                    i = t.matmul(bank[2 + (NJ * h + n) % 2][:, x * JW[j]:(x + 1) * JW[j]], kt[:, h % 2, j * P:(j + 1) * P],
                                 qt[:, h % 2, r + x, j * P:], start=True, stop=True)
                i.then_inc(b_s2, 1)

            def values(b, h, j):
                if j == 0:
                    if due(at := nth_of(1, b, h, 0)):
                        e.wait_ge(b_o, at)
                    if h == 0:
                        e.wait_ge(b_v, b + 1)
                e.wait_ge(b_sel, nth_of(4, b, h, j + 1))
                for r in range(R):
                    i = t.matmul(bank[4][VW * r:VW * (r + 1), j * P:], vb[:, j, h, :],
                                 pt[:, JO[j] + r * JW[j]:JO[j] + (r + 1) * JW[j]], start=(j == 0), stop=(j == TPB - 1),
                                 skip_group_check=True)
                i.then_inc(b_pv, 1)

            def turn_out(b, h):
                e.wait_ge(b_o, nth_of(1, b, h, 1))
                if h % 2 == 0 and due(at := b * (NG // 2) + h // 2):
                    e.wait_ge(b_o2e, at)
                if due(at := tiles_by(b, h)):
                    e.wait_ge(m_xe, at)
                if h % 2 and tiles_at(b, h)[0] is None:
                    e.wait_ge(b_on, nth_of(1, b, h, 0))
                for q in range(TPB):
                    i = t.transpose(xb[:, q, :], oe[:, q * P:(q + 1) * P], ident)
                i.then_inc(b_ot, 1)

            def turn_pair(b, i, m):
                e.wait_ge(b_on, nth_of(1, b, 2 * i, 2))
                e.wait_ge(m_xe, m)
                for q in range(TPB):
                    j = t.transpose(xb[:, q, :], o2[:, q, :], ident)
                j.then_inc(b_o2, 1)

            def expert(b, h, m, step):
                if step == 0:
                    e.wait_ge(m_x[m % 2], b * (8 * MPB) + 16 * (m // 2 + 1))
                    if m == tiles_at(b, h)[0]:
                        if due(at := nth_of(1, b, h, 0)):
                            e.wait_ge(b_on, at)
                    else:
                        e.wait_ge(m_xe, b * MPB + m)
                        if h % 2 == 0:
                            e.wait_ge(b_o2e, b * (NG // 2) + h // 2)
                    for k in range(KB):
                        i = t.transpose(xb[:, k, :], xg[:, m % 2, k * P:(k + 1) * P], ident)
                    i.then_inc(m_xt, 1)
                    return
                if step == 1:
                    if not due(b) and m == 0:
                        e.wait_ge(r_tokens, 1)
                        e.wait_ge(r_eid, 1)
                    ex[0] = e.value_load(eid_i[0:1, bass.ds(b * MPB + m, 1)], min_val=0, max_val=E - 1)
                    if due(at := b * MPB + m):
                        e.wait_ge(m_ye, at)
                    if 0 < h <= TPB and due(b):
                        e.wait_ge(b_s, (b - 1) * TPB + h)
                    t.matmul(bank[7][:, :], sel_e[:, ex[0], :], be3[:, :], start=True, stop=False)
                    e.wait_ge(m_xe, b * MPB + (m + 1))
                k = step - 1
                i = t.matmul(bank[7][:, :], xgt[:, k, :], w_e[:, ex[0], k, :], start=False, stop=(k == KB - 1))
                if k == KB - 1:
                    i.then_inc(m_y, 1)

            def project(b, u, k, m, to_bank=None):
                if k == 0:
                    e.wait_ge(b_o2e, b * (NG // 2) + NG // 2)
                    e.wait_ge(b_o0, b + 1)
                    e.wait_ge(m_ye, m)
                    if u > int(to_bank is not None):
                        e.wait_ge(b_s, b * TPB + u - int(to_bank is not None))
                i = t.matmul(bank[to_bank or 7][:, :], ot[:, k, u, :], wo[:, k, :], start=(k == 0), stop=(k == KB - 1))
                if k == KB - 1:
                    i.then_inc(b_p, 1)

            ex = [None]

            def go(b, more):
                for h in range(NG):
                    first, second = tiles_at(b, h)
                    late = h >= TPB and second is None

                    def filler(k):
                        if h < TPB and due(b):
                            project(b - 1, h, k, first_tiles_by(b, h))
                        if second is not None:
                            expert(b, h, second, k + 1)
                        if late and first is not None and k in (1, 2):
                            expert(b, h, first, k + 2)
                        if first is None and due(b):
                            pe_taps(e, k)
                        if not due(b) and h == 1 and k == 3:
                            pe_back(e)
                            e.wait_ge(e_load, 16 * E)
                            e.wait_ge(b_wo, 16)

                    def transposes(*units):
                        if h + 2 < NG or more:
                            for i in units:
                                turn(*next_group(b, h, 2), i)

                    def maxima(i):
                        if h + 1 < NG or more:
                            turn_maxima(*next_group(b, h, 1), i, not (h + 2 < NG or more))

                    for n in range(NJ):
                        if h + 1 < NG or more:
                            scores_1(*next_group(b, h, 1), n)
                        scores_2(b, h, n)
                        if first is None:
                            continue
                        if n == TURN_AT:
                            expert(b, h, first, 0)
                        elif n in (LATE_AT if late else QUARTERS_AT):
                            expert(b, h, first, (LATE_AT if late else QUARTERS_AT).index(n) + 1)
                    if h == 0 and due(b):
                        turn_pair(b - 1, NG // 2 - 1, first_tiles_by(b, h))
                    if h % 2 == 0 and h:
                        turn_pair(b, h // 2 - 1, first_tiles_by(b, h))
                    if second is not None:
                        expert(b, h, second, 0)
                    transposes(0)
                    values(b, h, 0)
                    filler(0)
                    transposes(1)
                    values(b, h, 1)
                    values(b, h, 2)
                    transposes(2)
                    filler(1)
                    values(b, h, 3)
                    maxima(0)
                    filler(2)
                    maxima(1)
                    filler(3)
                    turn_out(b, h)

            for h in range(2):
                for i in range(NTU):
                    turn(0, h, i)
                if h == 0:
                    pe_route(e)
            for n in range(NJ):
                scores_1(0, 0, n)
            for i in range(NMU):
                turn_maxima(0, 0, i, False)
            go(0, True)
            with e.Fori(1, NB - 1) as b:
                go(b, True)
            go(NB - 1, False)
            turn_pair(NB - 1, NG // 2 - 1, NB * MPB)
            for u in range(TPB):
                for k in range(KB):
                    if u == 0 and k == 0:
                        e.wait_ge(s4_row, 1)
                    project(NB - 1, u, k, NB * MPB, 7 - u % 2)

        def sp_b(e):
            for u in range(TPB):
                e.wait_ge(a_kvg[u % 2], NT // 2)
            e.dma_start(wo, wo_d.rearrange("(k p) n -> p k n", p=P)).then_inc(b_wo, 16)

            def go(b):
                for m in range(MPB):
                    e.wait_ge(m_ye, b * MPB + (m + 1))
                    e.dma_start(y_t[b * MPB + m], yo[:, m % 2, :]).then_inc(m_st[m % 2], 16)

            go(0)
            with e.Fori(1, NB) as b:
                go(b)

        w_lin, c_x = w_e[:, 0], w_e[:, 1]
        c_y = w_e[:, 2:4].rearrange("p e (t k) d -> p (e t) k d", k=TOPK)
        dft = w_e[:, 4:6]
        c_xn = w_e[:, 6, 0:2]
        c_g, c_o = w_e[:, 7, 0:2], w_e[:, 7, 2:4]
        c_xh = parts("c_xh", [P, 2, KB, P], "arena", 0)
        c_xl = parts("c_xl", [P, 2, KB, P], "arena", 2 * D)
        w_high = parts("w_high", [P, KB, D], "arena", OT_END)
        w_low = parts("w_low", [P, KB, D], "w_e", 0)
        toep_high = parts("toep_high", [P, D], "arena", OT_END + KB * D)
        toep_low = parts("toep_low", [P, D], "toep", 0)
        c_st = take([P, TPB, 8])
        c_mv = take([P, TPB, 2])
        c_rstd = take([P, TPB, 1])
        c_shift = take([P, TPB, 1])
        c_bias = take([P, D])
        c_scale = take([P, KB, KB])
        c_slot = take([P, TPB, TOPK, 1], U32)
        taps = take([P, P + D])
        c_dft = sem("c_dft")
        c_w, c_ws, c_ts = sem("c_w"), sem("c_ws"), sem("c_ts")
        c_lo = sems("c_lo", 2)
        c_ld, c_ga = sems("c_ld", TPB), sems("c_ga", TPB)
        c_idx = sem("c_idx")
        c_z, c_gate, c_x1, c_stat, c_r, c_n = (sems(n, 2) for n in ("c_z", "c_gate", "c_x1", "c_stat", "c_r", "c_n"))
        c_tr, c_te, c_lin, c_conv, c_pre, c_sil, c_prod, c_done = (
            sems(n, 2) for n in ("c_tr", "c_te", "c_lin", "c_conv", "c_pre", "c_sil", "c_prod", "c_done"))
        c_out = sems("c_out", TPB)

        def gate(e, b, u):
            e.wait_ge(c_z[u % 2], nth(b, u))
            nc.scalar.activation(c_y[:, u, 1, :], c_y[:, u, 0, :], ACT.Silu, scale=1.0 / TOPK).then_inc(c_gate[u % 2], 1)

        def sp_c(e):
            e.wait_ge(m_y, NB * MPB)
            e.dma_start(dft, dft_d.rearrange("c (k p) n -> p c k n", p=P)).then_inc(c_dft, 16)
            e.dma_start(w_lin, wft_d.rearrange("(k p) n -> p k n", p=P)).then_inc(c_w, 16)
            e.dma_start(c_bias, bf_d.partition_broadcast(P)).then_inc(c_w, 16)
            e.dma_start(c_scale, sc_d.partition_broadcast(P)).then_inc(c_w, 16)
            for u in range(TPB):
                e.dma_start(c_x[:, u, :], x_t[u]).then_inc(c_ld[u], 16)

            sp_taps(e)

            def store(b, u):
                e.wait_ge(c_done[u % 2], nth(b, u))
                e.dma_start(out_t[b * TPB + u], c_o[:, u % 2, :]).then_inc(c_out[u], 16)

            def go(b, more):
                for u in range(TPB):
                    if more:
                        e.wait_ge(c_x1[u % 2], nth(b, u))
                        e.dma_start(c_x[:, u, :], x_t[(b + 1) * TPB + u]).then_inc(c_ld[u], 16)
                    if u >= 2:
                        store(b, u - 2)
                    elif due(b):
                        store(b - 1, u + 2)

            go(0, True)
            with e.Fori(1, NB - 1) as b:
                go(b, True)
            go(NB - 1, False)
            for u in (2, 3):
                store(NB - 1, u)
            for u in range(TPB):
                e.wait_ge(c_out[u], 16 * NB)

        def pool_c(e, st):
            g = nc.gpsimd
            e.wait_ge(m_y, NB * MPB)
            for par in range(2):
                e.wait_ge(m_st[par], 16 * NB * MPB // 2)

            def rows(b, u):
                if due(at := 32 * b):
                    e.wait_ge(c_ga[u], at)
                alone(e)
                g.tensor_copy(c_slot[:, u], slots[:, :, bass.ds(b * TPB + u, 1)]).then_inc(c_idx, 1)
                e.wait_ge(c_idx, b * TPB + u + 1)
                if due(at := nth(b, u) - 2):
                    e.wait_ge(c_x1[u % 2], at)
                alone(e)
                for k in range(TOPK):
                    e.indirect_dma_start(c_y[:, u, k, :], None, y_d, bass.IndirectOffsetOnAxis(ap=c_slot[:, u, k, :], axis=0))\
                     .then_inc(c_ga[u], 16)

            def root(b, u):
                e.wait_ge(c_stat[u % 2], nth(b, u))
                g.tensor_tensor(c_rstd[:, u, :], c_mv[:, u, 1:2], const("eps"), ALU.add).then_inc(pool_steps, st.one())
                g.tensor_tensor(c_shift[:, u, :], c_mv[:, u, 0:1], const("minus"), ALU.mult).then_inc(pool_steps, st.one())
                e.wait_ge(pool_steps, st.count())
                g.tensor_tensor(c_rstd[:, u, :], c_rstd[:, u, :], const("half"), ALU.pow).then_inc(pool_steps, st.one())
                e.wait_ge(pool_steps, st.count())
                g.tensor_tensor(c_shift[:, u, :], c_shift[:, u, :], c_rstd[:, u, :], ALU.mult).then_inc(c_r[u % 2], 1)

            def total(b, u):
                e.wait_ge(c_prod[u % 2], nth(b, u))
                alone(e)
                g.tensor_tensor(c_o[:, u % 2, :], c_o[:, u % 2, :], s_tok[:, b, u, :], ALU.add).then_inc(c_done[u % 2], 1)

            def go(b, more):
                for u in range(TPB):
                    if u + 1 < TPB or more:
                        root(b + (u + 1) // TPB, (u + 1) % TPB)
                    if more:
                        rows(b + 1, u)
                    if u >= 2:
                        total(b, u - 2)
                    elif due(b):
                        total(b - 1, u + 2)

            for u in range(TPB):
                rows(0, u)
            root(0, 0)
            st.close()
            go(0, True)
            st.close()
            with e.Fori(1, NB - 1) as b:
                st.enter(b, TPB * 3)
                go(b, True)
            st.leave(1, NB - 1)
            go(NB - 1, False)
            for u in (2, 3):
                total(NB - 1, u)
            st.close()

        def dve_scale(e):
            v = nc.vector
            e.wait_ge(c_w, 48)
            w4 = w_lin.rearrange("p k (o c) -> p k o c", o=KB)
            sc4 = c_scale.rearrange("p o k -> p k o").unsqueeze(3)
            for k in range(KB):
                i = v.tensor_tensor(w4[:, k], w4[:, k], sc4[:, k].to_broadcast([P, KB, P]), ALU.mult)
                i.then_inc(c_ws, 1)
            for par in range(2):
                e.wait_ge(m_st[par], 16 * NB * MPB // 2)
            for k in range(KB):
                e.wait_ge(c_ws, k + 1)
                v.tensor_copy(w_high[:, k], w_lin[:, k]).then_inc(c_ws, 1)
            for k in range(KB):
                e.wait_ge(c_ws, KB + k + 1)
                v.tensor_tensor(w_low[:, k], w_lin[:, k], w_high[:, k].bitcast(F32), ALU.subtract).then_inc(c_ws, 1)

        def dve_c(e, st):
            v = nc.vector

            def experts(b, u):
                e.wait_ge(c_ga[u], b * 32 + 32)
                v.tensor_tensor(c_y[:, u, 0, :], c_y[:, u, 0, :], c_y[:, u, 1, :], ALU.add).then_inc(c_z[u % 2], 1)

            def gated(b, u):
                e.wait_ge(c_gate[u % 2], nth(b, u))
                v.tensor_tensor(s_tok[:, b, u, :], s_tok[:, b, u, :], c_y[:, u, 1, :], ALU.mult).then_inc(dve_steps, st.one())

            def layer_in(b, u):
                e.wait_ge(c_ld[u], b * 16 + 16)
                e.wait_ge(dve_steps, st.count())
                v.tensor_tensor(s_tok[:, b, u, :], s_tok[:, b, u, :], c_x[:, u, :], ALU.add).then_inc(c_x1[u % 2], 1)

            def statistics(b, u):
                e.wait_ge(c_x1[u % 2], nth(b, u))
                alone(e)
                v.bn_stats(c_st[:, u, 0:6], s_tok[:, b, u, :]).then_inc(dve_steps, st.one())

            def moments(b, u):
                e.wait_ge(dve_steps, st.count())
                alone(e)
                v.bn_aggr(c_mv[:, u, :], c_st[:, u, 0:6]).then_inc(c_stat[u % 2], 1)

            def low(b, u):
                e.wait_ge(c_te[u % 2], nth(b, u))
                if due(at := nth(b, u) - 1):
                    e.wait_ge(c_conv[u % 2], at)
                v.tensor_tensor(c_xl[:, u % 2].rearrange("p k t -> p (k t)"), bank[u % 2][:, :],
                                c_xh[:, u % 2].rearrange("p k t -> p (k t)").bitcast(F32), ALU.subtract).then_inc(c_lo[u % 2], 1)

            def bias(b, u):
                e.wait_ge(c_lin[u % 2], nth(b, u))
                if due(at := nth(b, u) - 1):
                    e.wait_ge(c_prod[u % 2], at)
                v.tensor_tensor(c_g[:, u % 2, :], bank[2 + u % 2][:, :], c_bias, ALU.add).then_inc(c_pre[u % 2], 1)

            def product(b, u):
                e.wait_ge(c_conv[u % 2], nth(b, u))
                e.wait_ge(c_sil[u % 2], nth(b, u))
                if u >= 2:
                    e.wait_ge(c_out[u - 2], 16 * b + 16)
                elif due(at := 16 * b):
                    e.wait_ge(c_out[u + 2], at)
                v.tensor_tensor(c_o[:, u % 2, :], bank[4 + u % 2][:, :], c_g[:, u % 2, :], ALU.mult).then_inc(c_prod[u % 2], 1)

            def go(b, more):
                for u in range(TPB):
                    ahead = (b + (u + 3) // TPB, (u + 3) % TPB) if u + 3 < TPB or more else None
                    if ahead:
                        gated(*ahead)
                    if u + 1 < TPB or more:
                        low(b + (u + 1) // TPB, (u + 1) % TPB)
                    if ahead:
                        layer_in(*ahead)
                    bias(b, u)
                    if ahead:
                        statistics(*ahead)
                    if more:
                        experts(b + 1, u)
                    if ahead:
                        moments(*ahead)
                    product(b, u)

            for u in range(TPB):
                experts(0, u)
            e.wait_ge(b_s, TPB)
            for u in range(3):
                gated(0, u)
                layer_in(0, u)
                statistics(0, u)
                moments(0, u)
            e.wait_ge(s4_toep, 16)
            v.tensor_copy(toep_high[:, :], toep[:, :]).then_inc(dve_steps, st.one())
            e.wait_ge(dve_steps, st.count())
            v.tensor_tensor(toep_low[:, :], toep[:, :], toep_high[:, :].bitcast(F32), ALU.subtract).then_inc(c_ts, 1)
            e.wait_ge(b_s, NB * TPB)
            low(0, 0)
            st.close()
            go(0, True)
            st.close()
            with e.Fori(1, NB - 1) as b:
                st.enter(b, TPB * 2)
                go(b, True)
            st.leave(1, NB - 1)
            go(NB - 1, False)
            st.close()

        def act_c(e):
            a = nc.scalar

            def go(b, more):
                for u in range(TPB):
                    if u + 1 < TPB or more:
                        lift(b + (u + 1) // TPB, (u + 1) % TPB)
                    if u + 2 < TPB or more:
                        norm(b + (u + 2) // TPB, (u + 2) % TPB)
                    e.wait_ge(c_pre[u % 2], nth(b, u))
                    a.activation(c_g[:, u % 2, :], c_g[:, u % 2, :], ACT.Silu).then_inc(c_sil[u % 2], 1)
                    if more:
                        gate(e, b + 1, u)

            def norm(b, u):
                e.wait_ge(c_r[u % 2], nth(b, u))
                if due(at := nth(b, u) - 1):
                    e.wait_ge(c_tr[u % 2], at)
                a.activation(c_xn[:, u % 2, :], s_tok[:, b, u, :], ACT.Identity, bias=c_shift[:, u, :], scale=c_rstd[:, u, :])\
                    .then_inc(c_n[u % 2], 1)

            def lift(b, u):
                e.wait_ge(c_tr[u % 2], nth(b, u))
                if due(at := nth(b, u) - 1):
                    e.wait_ge(c_conv[u % 2], at)
                a.copy(c_xh[:, u % 2].rearrange("p k t -> p (k t)"), bank[u % 2][:, :]).then_inc(c_te[u % 2], 1)

            norm(0, 0)
            norm(0, 1)
            lift(0, 0)
            go(0, True)
            with e.Fori(1, NB - 1) as b:
                go(b, True)
            go(NB - 1, False)

        def pe_c(e):
            t = nc.tensor
            e.wait_ge(c_ws, 3 * KB)
            e.wait_ge(c_ts, 1)
            e.wait_ge(b_m, NB * NG * NJ)
            e.wait_ge(b_e, NB * NG * NJ)

            def turn(b, u):
                e.wait_ge(c_n[u % 2], nth(b, u))
                if due(at := nth(b, u) - 1):
                    e.wait_ge(c_lo[u % 2], at)
                for k in range(KB):
                    i = t.transpose(bank[u % 2][:, k * P:(k + 1) * P], c_xn[:, u % 2, k * P:(k + 1) * P], ident)
                i.then_inc(c_tr[u % 2], 1)

            def work(b, u):
                e.wait_ge(c_lo[u % 2], nth(b, u))
                if due(at := nth(b, u) - 1):
                    e.wait_ge(c_prod[u % 2], at)
                passes = [(c_xh, 0), (c_xh, 1), (c_xl, 0)]
                for k in range(KB):
                    for n, (x, part) in enumerate(passes):
                        i = t.matmul(bank[2 + u % 2][:, :], x[:, u % 2, k, :], (w_high, w_low)[part][:, k, :],
                                     start=(k + n == 0), stop=(k + n == KB + 1))
                i.then_inc(c_lin[u % 2], 1)
                for k in range(KB):
                    for n, (x, part) in enumerate(passes):
                        i = t.matmul(bank[4 + u % 2][:, k * P:], x[:, u % 2, k, :],
                                     (toep_high, toep_low)[part][:, 0:D - k * P],
                                     start=(k + n == 0), stop=(k + n == KB + 1), skip_group_check=True)
                i.then_inc(c_conv[u % 2], 1)

            def go(b, more):
                for u in range(TPB):
                    if u + 1 < TPB or more:
                        turn(b + (u + 1) // TPB, (u + 1) % TPB)
                    work(b, u)

            turn(0, 0)
            go(0, True)
            with e.Fori(1, NB - 1) as b:
                go(b, True)
            go(NB - 1, False)

        @block.sync
        def _(e):
            sp_a(e)
            sp_b(e)
            sp_c(e)

        @block.vector
        def _(e):
            st = Steps()
            dve_a(e, st)
            dve_b(e, st)
            dve_c(e, st)

        @block.gpsimd
        def _(e):
            st = Steps()
            pool_a(e, st)
            pool_b(e, st)
            pool_c(e, st)

        @block.scalar
        def _(e):
            act_a(e)
            act_b(e)
            act_c(e)

        @block.tensor
        def _(e):
            pe_a(e)
            pe_b(e)
            pe_c(e)


_INS = ["L0_attn_x", "L0_attn_wq", "L0_attn_wk", "L0_attn_wv", "L0_attn_wo", "L0_ffn_W_gate", "L0_ffn_b_gate",
        "L0_ffn_W_e", "L0_ffn_b_e", "L1_attn_Lambda_ri", "L1_attn_p_ri", "L1_attn_q_ri", "L1_attn_Vc_ri",
        "L1_attn_Ct_ri", "L1_attn_Bp", "L1_attn_D", "L1_attn_log_step", "L1_ffn_weight",
        "L1_ffn_weight_scale_inv", "L1_ffn_bias"]
_TURNED = {"L1_attn_Vc_ri": (1, 0, 2), "L1_ffn_weight": (1, 0)}


def kernel(**inputs):
    import concourse.bacc as bacc
    from concourse.bass_utils import run_bass_kernel_spmd

    nc = bacc.Bacc("TRN2", target_bir_lowering=False, num_devices=1)
    given = [(n, np.ascontiguousarray(np.asarray(inputs[n]).transpose(_TURNED[n]) if n in _TURNED else inputs[n])) for n in _INS]
    given += list(zip(("constants", "dft"), constants()))
    arrays = {f"in_{n}": a for n, a in given}
    args = [nc.dram_tensor(f"in_{n}", a.shape, mybir.dt.from_np(a.dtype), kind="ExternalInput").ap() for n, a in given]
    out = nc.dram_tensor("out", (NB, S, D), F32, kind="ExternalOutput").ap()
    build(nc, *args, out)
    return run_bass_kernel_spmd(nc, [arrays], core_ids=[0]).results[0]["out"]
```
